# Optimizing a Trainium2 kernel written in Bass

```python
import numpy as np
import jax
import jax.numpy as jnp

def _softmax(x, axis=-1):
    return jax.nn.softmax(x, axis=axis)

def _gelu(x):
    return jax.nn.gelu(x, approximate=True)

def _silu(x):
    return jax.nn.silu(x)

def _sigmoid(x):
    return jax.nn.sigmoid(x)

def _layernorm(x, axis=-1, eps=1e-05):
    m = jnp.mean(x, axis=axis, keepdims=True)
    v = jnp.var(x, axis=axis, keepdims=True)
    return (x - m) / jnp.sqrt(v + eps)

def _scatter_add(tgt, idx, src, axis=0):
    return tgt.at[idx].add(src)

def _segment_sum(src, seg, n):
    return jax.ops.segment_sum(src, seg, n)
kernel_name = 'mk_gps_d2_gnn_r32_4f9cf1'

def setup_inputs(seed: int=0):
    np.random.seed(seed)
    _w = jnp.asarray

    def _rec_inputs():
        import jax
        import jax.numpy as jnp
        _gk = jax.random.key(seed)
        x = -8.776e-05 + 1 * jax.random.normal(jax.random.fold_in(_gk, 1), (3125, 256), jnp.float32)
        src = jax.random.randint(jax.random.fold_in(_gk, 2), (50000,), 0, 3125, jnp.int32)
        dst = jnp.minimum((3125 * jax.random.uniform(jax.random.fold_in(_gk, 3), (50000,)) ** 2.0).astype(jnp.int32), 99999)
        _o = jnp.argsort(dst, stable=True)
        src = src[_o]
        dst = dst[_o]
        edge_type_2 = jax.random.randint(jax.random.fold_in(_gk, 13), (50000,), 0, 2, jnp.int32)
        return (x, src, dst, edge_type_2)
    x, src, dst, edge_type_2 = _rec_inputs()

    def _L0_gnn_setup():
        import jax, jax.numpy as jnp
        import numpy as np
        N_NODES = 625
        N_EDGES = 10000
        D = 256
        N_LAYERS = 3
        N_RELS = 2
        LN_EPS = 1e-05

        def _layer_norm(h, gamma, beta):
            mu = jnp.mean(h, axis=-1, keepdims=True)
            var = jnp.mean(jnp.square(h - mu), axis=-1, keepdims=True)
            return (h - mu) * jax.lax.rsqrt(var + LN_EPS) * gamma + beta
        key = jax.random.key(seed)
        ks = jax.random.split(key, 10)
        x = jax.random.normal(ks[0], (N_NODES, D), dtype=jnp.float32)
        src = jax.random.randint(ks[1], (N_EDGES,), 0, N_NODES)
        dst = jax.random.randint(ks[2], (N_EDGES,), 0, N_NODES)
        etype = jnp.sort(jax.random.randint(ks[3], (N_EDGES,), 0, N_RELS))
        scale = 1.0 / np.sqrt(D)
        W = jax.random.normal(ks[4], (N_LAYERS, N_RELS, D, D), dtype=jnp.float32) * scale
        bias = jnp.zeros((N_LAYERS, D), dtype=jnp.float32)
        loop_w = jax.random.normal(ks[5], (N_LAYERS, D, D), dtype=jnp.float32) * scale
        ln_gamma = jnp.ones((N_LAYERS, D), dtype=jnp.float32)
        ln_beta = jnp.zeros((N_LAYERS, D), dtype=jnp.float32)
        return {'x': x, 'W': W, 'bias': bias, 'loop_w': loop_w, 'ln_gamma': ln_gamma, 'ln_beta': ln_beta, 'src': src, 'dst': dst, 'etype': etype}
    _L0_gnn_all = _L0_gnn_setup()
    _L0_gnn_in = {k: v for k, v in _L0_gnn_all.items() if k in ('W', 'bias', 'loop_w', 'ln_gamma', 'ln_beta')}
    del _L0_gnn_all

    def _L0_mix_setup():
        import jax, jax.numpy as jnp
        import numpy as np
        EPS = 1e-05

        def _layernorm(x, weight, bias):
            mean = jnp.mean(x, axis=-1, keepdims=True)
            std = jnp.std(x, axis=-1, keepdims=True, ddof=1)
            out = (x - mean) / (std + EPS)
            return weight * out + bias
        key = jax.random.key(seed)
        B, N, C = (4, 1024, 256)
        H, hc = (8, C // 8)
        kx, = jax.random.split(key, 1)
        x = jax.random.normal(kx, (B, N, C), dtype=jnp.float32)
        return {'x': x, 'kln_weight': jnp.ones((H, 1, hc), dtype=jnp.float32), 'kln_bias': jnp.zeros((H, 1, hc), dtype=jnp.float32), 'vln_weight': jnp.ones((H, 1, hc), dtype=jnp.float32), 'vln_bias': jnp.zeros((H, 1, hc), dtype=jnp.float32)}
    _L0_mix_all = _L0_mix_setup()
    _L0_mix_in = {k: v for k, v in _L0_mix_all.items() if k in ('kln_weight', 'kln_bias', 'vln_weight', 'vln_bias')}
    del _L0_mix_all

    def _L0_ffn_setup():
        import jax, jax.numpy as jnp
        import numpy as np
        DIM = 256
        H = 8
        D = 64
        G = 64
        INNER = H * D
        SCALE = D ** (-0.5)
        key = jax.random.key(seed)
        ks = jax.random.split(key, 12)
        B, N = (4, 512)
        x = jax.random.normal(ks[0], (B, N, DIM), dtype=jnp.float32)
        s = lambda fan_in: 1.0 / np.sqrt(fan_in)
        W_fx = jax.random.normal(ks[1], (DIM, INNER), dtype=jnp.float32) * s(DIM)
        b_fx = jnp.zeros((INNER,), dtype=jnp.float32)
        W_x = jax.random.normal(ks[2], (DIM, INNER), dtype=jnp.float32) * s(DIM)
        b_x = jnp.zeros((INNER,), dtype=jnp.float32)
        A = jax.random.normal(ks[3], (G, D), dtype=jnp.float32)
        Q, _ = jnp.linalg.qr(A.T)
        W_slice = Q[:, :G].astype(jnp.float32)
        b_slice = jnp.zeros((G,), dtype=jnp.float32)
        W_q = jax.random.normal(ks[4], (D, D), dtype=jnp.float32) * s(D)
        W_k = jax.random.normal(ks[5], (D, D), dtype=jnp.float32) * s(D)
        W_v = jax.random.normal(ks[6], (D, D), dtype=jnp.float32) * s(D)
        W_out = jax.random.normal(ks[7], (INNER, DIM), dtype=jnp.float32) * s(INNER)
        b_out = jnp.zeros((DIM,), dtype=jnp.float32)
        temperature = jnp.ones((1, H, 1, 1), dtype=jnp.float32) * 0.5
        return {'x': x, 'W_fx': W_fx, 'b_fx': b_fx, 'W_x': W_x, 'b_x': b_x, 'W_slice': W_slice, 'b_slice': b_slice, 'W_q': W_q, 'W_k': W_k, 'W_v': W_v, 'W_out': W_out, 'b_out': b_out, 'temperature': temperature}
    _L0_ffn_all = _L0_ffn_setup()
    _L0_ffn_in = {k: v for k, v in _L0_ffn_all.items() if k in ('W_fx', 'b_fx', 'W_x', 'b_x', 'W_slice', 'b_slice', 'W_q', 'W_k', 'W_v', 'W_out', 'b_out', 'temperature')}
    del _L0_ffn_all

    def _L1_gnn_setup():
        import jax, jax.numpy as jnp
        import numpy as np
        N, IN_CH, HEADS, OUT_CH, E = (50000, 256, 4, 64, 25000)
        key = jax.random.key(seed)
        k1, k2, k3, k4, k5 = jax.random.split(key, 5)
        x = jax.random.normal(k1, (N, IN_CH), dtype=jnp.float32)
        edge_index = jax.random.randint(k2, (2, E), 0, N, dtype=jnp.int64)
        bw = float(np.sqrt(6.0 / (IN_CH + HEADS * OUT_CH)))
        ba = float(np.sqrt(6.0 / (HEADS + OUT_CH)))
        weight = jax.random.uniform(k3, (IN_CH, HEADS * OUT_CH), jnp.float32, -bw, bw)
        attn_l = jax.random.uniform(k4, (HEADS, OUT_CH), jnp.float32, -ba, ba)
        attn_r = jax.random.uniform(k5, (HEADS, OUT_CH), jnp.float32, -ba, ba)
        return {'x': x, 'edge_index': edge_index, 'weight': weight, 'attn_l': attn_l, 'attn_r': attn_r}
    _L1_gnn_all = _L1_gnn_setup()
    _L1_gnn_in = {k: v for k, v in _L1_gnn_all.items() if k in ('weight', 'attn_l', 'attn_r')}
    del _L1_gnn_all

    def _L1_mix_setup():
        import jax, jax.numpy as jnp
        import numpy as np
        EPS_NORM = 1e-06
        EPS_ATTN = 1e-06
        HEADS = 8

        def rmsnorm(x, w):
            ms = jnp.mean(x * x, axis=-1, keepdims=True)
            return w * (x * jax.lax.rsqrt(ms + EPS_NORM))

        def linear_attention(x, w_qkv, w_out, b_out):
            B, N, D = x.shape
            hd = D // HEADS
            qkv = (x @ w_qkv).reshape(B, N, 3, HEADS, hd)
            q, k, v = (qkv[:, :, 0], qkv[:, :, 1], qkv[:, :, 2])
            q = jax.nn.elu(q) + 1.0
            k = jax.nn.elu(k) + 1.0
            kv = jnp.einsum('bnhd,bnhm->bhdm', k, v)
            z = 1.0 / (jnp.einsum('bnhd,bhd->bnh', q, k.sum(axis=1)) + EPS_ATTN)
            out = jnp.einsum('bnhd,bhdm,bnh->bnhm', q, kv, z)
            out = out.reshape(B, N, D)
            return out @ w_out + b_out
        key = jax.random.key(seed)
        ks = jax.random.split(key, 4)
        B, N, D = (16, 256, 256)
        x = jax.random.normal(ks[0], (B, N, D), dtype=jnp.float32)
        w_norm1 = jnp.ones((D,), dtype=jnp.float32)
        w_qkv = jax.random.normal(ks[1], (D, 3 * D), dtype=jnp.float32) * 0.02
        w_out = jax.random.normal(ks[2], (D, D), dtype=jnp.float32) * 0.02
        b_out = jnp.zeros((D,), dtype=jnp.float32)
        w_norm2 = jnp.ones((D,), dtype=jnp.float32)
        return {'x': x, 'w_norm1': w_norm1, 'w_qkv': w_qkv, 'w_out': w_out, 'b_out': b_out, 'w_norm2': w_norm2}
    _L1_mix_all = _L1_mix_setup()
    _L1_mix_in = {k: v for k, v in _L1_mix_all.items() if k in ('w_norm1', 'w_qkv', 'w_out', 'b_out', 'w_norm2')}
    del _L1_mix_all

    def _L1_ffn_setup():
        import jax, jax.numpy as jnp
        import numpy as np
        E = 8
        K = 2
        D = 256
        H = 512
        DOUT = 256
        EPS = 1e-05
        key = jax.random.key(seed)
        ks = jax.random.split(key, 9)
        s = 0.02
        return {'x': jax.random.normal(ks[0], (4, 256, D), jnp.float32), 'gamma': 1.0 + 0.05 * jax.random.normal(ks[1], (D,), jnp.float32), 'beta': 0.05 * jax.random.normal(ks[2], (D,), jnp.float32), 'Wr': 0.01 * jax.random.normal(ks[3], (D, E), jnp.float32), 'br': jnp.zeros((E,), jnp.float32), 'W1': s * jax.random.normal(ks[4], (E, D, H), jnp.float32), 'b1': s * jax.random.normal(ks[5], (E, H), jnp.float32), 'W2': s * jax.random.normal(ks[6], (E, H, DOUT), jnp.float32), 'b2': s * jax.random.normal(ks[7], (E, DOUT), jnp.float32)}
    _L1_ffn_all = _L1_ffn_setup()
    _L1_ffn_in = {k: v for k, v in _L1_ffn_all.items() if k in ('gamma', 'beta', 'Wr', 'br', 'W1', 'b1', 'W2', 'b2')}
    del _L1_ffn_all
    return {'x': x, 'src': src, 'dst': dst, 'edge_type_2': edge_type_2, 'L0_gnn_W': _L0_gnn_in['W'], 'L0_gnn_bias': _L0_gnn_in['bias'], 'L0_gnn_loop_w': _L0_gnn_in['loop_w'], 'L0_gnn_ln_gamma': _L0_gnn_in['ln_gamma'], 'L0_gnn_ln_beta': _L0_gnn_in['ln_beta'], 'L0_mix_kln_weight': _L0_mix_in['kln_weight'], 'L0_mix_kln_bias': _L0_mix_in['kln_bias'], 'L0_mix_vln_weight': _L0_mix_in['vln_weight'], 'L0_mix_vln_bias': _L0_mix_in['vln_bias'], 'L0_ffn_W_fx': _L0_ffn_in['W_fx'], 'L0_ffn_b_fx': _L0_ffn_in['b_fx'], 'L0_ffn_W_x': _L0_ffn_in['W_x'], 'L0_ffn_b_x': _L0_ffn_in['b_x'], 'L0_ffn_W_slice': _L0_ffn_in['W_slice'], 'L0_ffn_b_slice': _L0_ffn_in['b_slice'], 'L0_ffn_W_q': _L0_ffn_in['W_q'], 'L0_ffn_W_k': _L0_ffn_in['W_k'], 'L0_ffn_W_v': _L0_ffn_in['W_v'], 'L0_ffn_W_out': _L0_ffn_in['W_out'], 'L0_ffn_b_out': _L0_ffn_in['b_out'], 'L0_ffn_temperature': _L0_ffn_in['temperature'], 'L1_gnn_weight': _L1_gnn_in['weight'], 'L1_gnn_attn_l': _L1_gnn_in['attn_l'], 'L1_gnn_attn_r': _L1_gnn_in['attn_r'], 'L1_mix_w_norm1': _L1_mix_in['w_norm1'], 'L1_mix_w_qkv': _L1_mix_in['w_qkv'], 'L1_mix_w_out': _L1_mix_in['w_out'], 'L1_mix_b_out': _L1_mix_in['b_out'], 'L1_mix_w_norm2': _L1_mix_in['w_norm2'], 'L1_ffn_gamma': _L1_ffn_in['gamma'], 'L1_ffn_beta': _L1_ffn_in['beta'], 'L1_ffn_Wr': _L1_ffn_in['Wr'], 'L1_ffn_br': _L1_ffn_in['br'], 'L1_ffn_W1': _L1_ffn_in['W1'], 'L1_ffn_b1': _L1_ffn_in['b1'], 'L1_ffn_W2': _L1_ffn_in['W2'], 'L1_ffn_b2': _L1_ffn_in['b2']}

def reference(x, src, dst, edge_type_2, L0_gnn_W, L0_gnn_bias, L0_gnn_loop_w, L0_gnn_ln_gamma, L0_gnn_ln_beta, L0_mix_kln_weight, L0_mix_kln_bias, L0_mix_vln_weight, L0_mix_vln_bias, L0_ffn_W_fx, L0_ffn_b_fx, L0_ffn_W_x, L0_ffn_b_x, L0_ffn_W_slice, L0_ffn_b_slice, L0_ffn_W_q, L0_ffn_W_k, L0_ffn_W_v, L0_ffn_W_out, L0_ffn_b_out, L0_ffn_temperature, L1_gnn_weight, L1_gnn_attn_l, L1_gnn_attn_r, L1_mix_w_norm1, L1_mix_w_qkv, L1_mix_w_out, L1_mix_b_out, L1_mix_w_norm2, L1_ffn_gamma, L1_ffn_beta, L1_ffn_Wr, L1_ffn_br, L1_ffn_W1, L1_ffn_b1, L1_ffn_W2, L1_ffn_b2):
    import jax
    import jax.numpy as jnp

    def _L0_gnn_ref(x, W, bias, loop_w, ln_gamma, ln_beta, src, dst, etype):
        import jax, jax.numpy as jnp
        import numpy as np
        N_NODES = 625
        N_EDGES = 10000
        D = 256
        N_LAYERS = 3
        N_RELS = 2
        LN_EPS = 1e-05

        def _layer_norm(h, gamma, beta):
            mu = jnp.mean(h, axis=-1, keepdims=True)
            var = jnp.mean(jnp.square(h - mu), axis=-1, keepdims=True)
            return (h - mu) * jax.lax.rsqrt(var + LN_EPS) * gamma + beta
        n = x.shape[0]
        is_r0 = (etype == 0)[:, None]
        h = x
        for l in range(N_LAYERS):
            xs = h[src]
            m = jnp.where(is_r0, xs @ W[l, 0], xs @ W[l, 1])
            agg = jax.ops.segment_sum(m, dst, num_segments=n)
            hn = _layer_norm(agg, ln_gamma[l], ln_beta[l])
            hn = hn + bias[l]
            hn = hn + h @ loop_w[l]
            if l < N_LAYERS - 1:
                hn = jax.nn.relu(hn)
            h = hn
        return h

    def _L0_mix_ref(x, kln_weight, kln_bias, vln_weight, vln_bias):
        import jax, jax.numpy as jnp
        import numpy as np
        EPS = 1e-05

        def _layernorm(x, weight, bias):
            mean = jnp.mean(x, axis=-1, keepdims=True)
            std = jnp.std(x, axis=-1, keepdims=True, ddof=1)
            out = (x - mean) / (std + EPS)
            return weight * out + bias
        B, N, C = x.shape
        H = kln_weight.shape[0]
        hc = C // H
        qkv = x.reshape(B, N, H, hc).transpose(0, 2, 1, 3)
        q = qkv
        k = _layernorm(qkv, kln_weight, kln_bias)
        v = _layernorm(qkv, vln_weight, vln_bias)
        kv = jnp.einsum('bhnd,bhne->bhde', k, v) / N
        out = jnp.einsum('bhnd,bhde->bhne', q, kv)
        out = out.transpose(0, 2, 1, 3).reshape(B, N, C)
        return out + x

    def _L0_ffn_ref(x, W_fx, b_fx, W_x, b_x, W_slice, b_slice, W_q, W_k, W_v, W_out, b_out, temperature):
        import jax, jax.numpy as jnp
        import numpy as np
        DIM = 256
        H = 8
        D = 64
        G = 64
        INNER = H * D
        SCALE = D ** (-0.5)
        B, N, _ = x.shape
        fx_mid = (x @ W_fx + b_fx).reshape(B, N, H, D).transpose(0, 2, 1, 3)
        x_mid = (x @ W_x + b_x).reshape(B, N, H, D).transpose(0, 2, 1, 3)
        temp = jnp.clip(temperature, 0.1, 5.0)
        slice_weights = jax.nn.softmax((x_mid @ W_slice + b_slice) / temp, axis=-1)
        slice_norm = slice_weights.sum(axis=2)
        slice_token = jnp.einsum('bhnc,bhng->bhgc', fx_mid, slice_weights)
        slice_token = slice_token / (slice_norm[..., None] + 1e-05)
        q = slice_token @ W_q
        k = slice_token @ W_k
        v = slice_token @ W_v
        attn = jax.nn.softmax(jnp.einsum('bhgc,bhkc->bhgk', q, k) * SCALE, axis=-1)
        out_slice = jnp.einsum('bhgk,bhkc->bhgc', attn, v)
        out_x = jnp.einsum('bhgc,bhng->bhnc', out_slice, slice_weights)
        out_x = out_x.transpose(0, 2, 1, 3).reshape(B, N, INNER)
        return out_x @ W_out + b_out

    def _L1_gnn_ref(x, edge_index, weight, attn_l, attn_r):
        import jax, jax.numpy as jnp
        import numpy as np
        N, IN_CH, HEADS, OUT_CH, E = (50000, 256, 4, 64, 25000)
        heads, out_ch = attn_l.shape
        n = x.shape[0]
        xt = jnp.matmul(x, weight).reshape(-1, heads, out_ch)
        row, col = (edge_index[0], edge_index[1])
        alpha_l = jnp.einsum('ehd,hd->eh', xt[row], attn_l)
        alpha_r = jnp.einsum('ehd,hd->eh', xt[col], attn_r)
        alpha = jax.nn.softmax(jax.nn.leaky_relu(alpha_l + alpha_r, 0.01), axis=1)
        tmp = jnp.einsum('nh,nhd->nd', alpha[:n], xt[col[:n]])
        out = jnp.broadcast_to(tmp[:, None, :], (n, heads, out_ch))
        return out.reshape(n, heads * out_ch)

    def _L1_mix_ref(x, w_norm1, w_qkv, w_out, b_out, w_norm2):
        import jax, jax.numpy as jnp
        import numpy as np
        EPS_NORM = 1e-06
        EPS_ATTN = 1e-06
        HEADS = 8

        def rmsnorm(x, w):
            ms = jnp.mean(x * x, axis=-1, keepdims=True)
            return w * (x * jax.lax.rsqrt(ms + EPS_NORM))

        def linear_attention(x, w_qkv, w_out, b_out):
            B, N, D = x.shape
            hd = D // HEADS
            qkv = (x @ w_qkv).reshape(B, N, 3, HEADS, hd)
            q, k, v = (qkv[:, :, 0], qkv[:, :, 1], qkv[:, :, 2])
            q = jax.nn.elu(q) + 1.0
            k = jax.nn.elu(k) + 1.0
            kv = jnp.einsum('bnhd,bnhm->bhdm', k, v)
            z = 1.0 / (jnp.einsum('bnhd,bhd->bnh', q, k.sum(axis=1)) + EPS_ATTN)
            out = jnp.einsum('bnhd,bhdm,bnh->bnhm', q, kv, z)
            out = out.reshape(B, N, D)
            return out @ w_out + b_out
        h = x + linear_attention(rmsnorm(x, w_norm1), w_qkv, w_out, b_out)
        return h + rmsnorm(h, w_norm2)

    def _L1_ffn_ref(x, gamma, beta, Wr, br, W1, b1, W2, b2):
        import jax, jax.numpy as jnp
        import numpy as np
        E = 8
        K = 2
        D = 256
        H = 512
        DOUT = 256
        EPS = 1e-05
        mu = jnp.mean(x, axis=-1, keepdims=True)
        var = jnp.mean(jnp.square(x - mu), axis=-1, keepdims=True)
        xn = (x - mu) * jax.lax.rsqrt(var + EPS) * gamma + beta
        logits = jnp.einsum('bsd,de->bse', xn, Wr) + br
        top_vals, top_idx = jax.lax.top_k(logits, K)
        w = jax.nn.softmax(top_vals, axis=-1)
        w_full = jnp.einsum('bsk,bske->bse', w, jax.nn.one_hot(top_idx, E, dtype=w.dtype))
        y = jnp.zeros(x.shape[:-1] + (DOUT,), x.dtype)
        for e in range(E):
            h = jax.nn.gelu(jnp.einsum('bsd,dh->bsh', xn, W1[e]) + b1[e], approximate=False)
            y_e = jnp.einsum('bsh,hd->bsd', h, W2[e]) + b2[e]
            y = y + y_e * w_full[..., e, None]
        return y
    edge_index = jnp.stack([src, dst])
    xn = _layernorm(x, axis=-1)
    x = x + _L0_gnn_ref(xn, L0_gnn_W, L0_gnn_bias, L0_gnn_loop_w, L0_gnn_ln_gamma, L0_gnn_ln_beta, src, dst, edge_type_2) + _L0_mix_ref(xn[None], L0_mix_kln_weight, L0_mix_kln_bias, L0_mix_vln_weight, L0_mix_vln_bias)[0]
    x = x + _L0_ffn_ref(_layernorm(x, axis=-1)[None], L0_ffn_W_fx, L0_ffn_b_fx, L0_ffn_W_x, L0_ffn_b_x, L0_ffn_W_slice, L0_ffn_b_slice, L0_ffn_W_q, L0_ffn_W_k, L0_ffn_W_v, L0_ffn_W_out, L0_ffn_b_out, L0_ffn_temperature)[0]
    xn = _layernorm(x, axis=-1)
    x = x + _L1_gnn_ref(xn, edge_index, L1_gnn_weight, L1_gnn_attn_l, L1_gnn_attn_r) + _L1_mix_ref(xn[None], L1_mix_w_norm1, L1_mix_w_qkv, L1_mix_w_out, L1_mix_b_out, L1_mix_w_norm2)[0]
    x = x + _L1_ffn_ref(_layernorm(x, axis=-1)[None], L1_ffn_gamma, L1_ffn_beta, L1_ffn_Wr, L1_ffn_br, L1_ffn_W1, L1_ffn_b1, L1_ffn_W2, L1_ffn_b2)[0]
    return x

_drawn_inputs = setup_inputs


def setup_inputs(seed=0):
    import zlib

    import numpy as np

    out = dict(_drawn_inputs(seed))
    spreads = {'L0_gnn_bias': (0.0, 0.1),
     'L0_gnn_ln_gamma': (1.0, 0.2),
     'L0_gnn_ln_beta': (0.0, 0.1),
     'L0_mix_kln_weight': (1.0, 0.2),
     'L0_mix_kln_bias': (0.0, 0.529),
     'L0_mix_vln_weight': (1.0, 0.2),
     'L0_mix_vln_bias': (0.0, 0.524),
     'L0_ffn_b_fx': (0.0, 0.1),
     'L0_ffn_b_x': (0.0, 0.8),
     'L0_ffn_b_slice': (0.0, 0.8),
     'L0_ffn_b_out': (0.0, 0.1),
     'L0_ffn_temperature': (0.5, 0.6),
     'L1_mix_w_norm1': (1.0, 0.6),
     'L1_mix_b_out': (0.0, 0.1),
     'L1_mix_w_norm2': (1.0, 0.2),
     'L1_ffn_br': (0.0, 0.8)}
    factors = {'L0_ffn_W_x': 8.0,
     'L0_ffn_W_slice': 8.0,
     'L0_ffn_W_q': 8.0,
     'L0_ffn_W_k': 8.0,
     'L1_mix_w_qkv': 3.522,
     'L1_mix_w_out': 4.128,
     'L1_ffn_gamma': 8.0,
     'L1_ffn_beta': 8.0,
     'L1_ffn_Wr': 6.423,
     'L1_ffn_W1': 5.647,
     'L1_ffn_b1': 41.406,
     'L1_ffn_W2': 5.477,
     'L1_ffn_b2': 64.0}
    for name, (base, spread) in spreads.items():
        noise = np.random.default_rng([zlib.crc32(name.encode()), seed]).standard_normal(out[name].shape)
        drawn = base * np.exp(spread * noise) if base else spread * noise
        out[name] = jnp.asarray(drawn.astype(out[name].dtype))
    for name, factor in factors.items():
        out[name] = (out[name] * factor).astype(out[name].dtype)
    return out
```

```python
from contextlib import ExitStack

import concourse.bass as bass
from concourse import mybir

ALU = mybir.AluOpType
ACT = mybir.ActivationFunctionType
AX = mybir.AxisListType
F32 = mybir.dt.float32
F16 = mybir.dt.float16
I32 = mybir.dt.int32
U32 = mybir.dt.uint32

N = 3125
D = 256
E = 50000
WIN = 25
P = N // WIN
RELS = 2
LAYERS = 3
EC = E // P
SLOT = 128
TILES = (E + WIN * (SLOT - 1)) // SLOT
RING = 16
HALF = RING // 2
TILES += -TILES % RING
HEADS = 8
HC = D // HEADS
SD = 64
INNER = HEADS * SD
GH, GD = 4, 64
EXPERTS, HID = 8, 512
GROUP = 4
LN_EPS = 1e-5
RMS_EPS = 1e-6
ROUND = 1.5 * 2 ** 23


class Order:

    def __init__(self, engine, semaphore, tile=0, per=0):
        self.engine, self.semaphore, self.start, self.per, self.k = engine, semaphore, tile * per, per, 0

    def then(self, instruction):
        instruction.then_inc(self.semaphore, 1)
        self.k += 1
        self.engine.wait_ge(self.semaphore, self.start + self.k)

    def close(self):
        assert self.k == self.per, (self.k, self.per)


def wait_from(engine, semaphore, value):
    if isinstance(value, int) and value <= 0:
        return
    engine.wait_ge(semaphore, value)


def over_tiles(engine, step, ahead=None, count=WIN):
    def both(t, b):
        if ahead and not (isinstance(t, int) and t == count - 1):
            ahead(t + 1, 1 - b)
        step(t, b)

    if ahead:
        ahead(0, 0)
    both(0, 0)
    both(1, 1)
    with engine.Fori(2, count - 1 - count % 2, 2) as i:
        both(i, 0)
        both(i + 1, 1)
    if count % 2:
        both(count - 1, 0)


def col(ap, t):
    return ap[:, bass.ds(t, 1)]


class Chip:

    def __init__(self, nc, A, out, keep):
        self.nc, self.A, self.out, self.keep = nc, A, out, keep
        self.X = self.sb(keep, "X", [P, WIN, D])
        self.ident = self.sb(keep, "ident", [128, 128])
        self.tri = self.sb(keep, "tri", [128, 128])
        self.ones = self.sb(keep, "ones", [128, 128])
        self.iota = self.sb(keep, "iota", [128, TILES], F16)
        self.iota_f = self.sb(keep, "iota_f", [128, 128])
        self.blocks = self.sb(keep, "blocks", [128, 128])
        self.heads = self.sb(keep, "heads", [128, 4])
        self.rstd = self.sb(keep, "rstd", [P, WIN])
        self.nmr = self.sb(keep, "nmr", [P, WIN])
        self.stats = self.sb(keep, "stats", [P, WIN, 6])
        self.fin = self.sb(keep, "fin", [P, 4, WIN])
        self.banks = [keep.enter_context(nc.psum_tensor(f"bank{i}", [128, 512], F32)) for i in range(8)]
        self.sems = []

    def sb(self, scope, name, shape, dt=F32):
        return scope.enter_context(self.nc.sbuf_tensor(name, shape, dt))

    def sem(self, *names):
        got = [self.nc.alloc_semaphore(name=n) for n in names]
        self.sems += got
        return got[0] if len(got) == 1 else got

    def recycle(self):
        self.nc.clear_and_free_semaphores(self.sems)
        self.nc.all_engine_barrier()
        self.sems = []

    def normalised(self, out, t):
        return self.nc.vector.tensor_scalar(out, self.X[:, t, :], col(self.rstd, t), col(self.nmr, t), ALU.mult, ALU.add)

    def finish_stats(self, order, var_ready, std_ready, base=0):
        v, fin = self.nc.vector, self.fin
        m0, s0, m1, s1 = (self.stats[:, :, i] for i in (1, 2, 4, 5))
        mean2, d, s, var = (fin[:, i, :] for i in range(4))
        order.then(v.tensor_tensor(mean2, m0, m1, ALU.add))
        order.then(v.tensor_tensor(d, m0, m1, ALU.subtract))
        order.then(v.tensor_tensor(s, s0, s1, ALU.add))
        order.then(v.tensor_tensor(d, d, d, ALU.mult))
        order.then(v.tensor_scalar(d, d, 0.25, LN_EPS, ALU.mult, ALU.add))
        order.then(v.scalar_tensor_tensor(out=var, in0=s, scalar=1.0 / D, in1=d, op0=ALU.mult, op1=ALU.add))
        v.tensor_scalar(mean2, mean2, -0.5, None, ALU.mult).then_inc(var_ready, 1)
        order.engine.wait_ge(std_ready, 1)
        order.then(v.reciprocal(self.rstd[:, :], self.rstd[:, :]))
        order.engine.wait_ge(var_ready, 1)
        order.then(v.tensor_tensor(self.nmr[:, :], mean2, self.rstd[:, :], ALU.mult))

    def root(self, act, var_ready, std_ready):
        act.wait_ge(var_ready, 1)
        self.nc.scalar.activation(self.rstd[:, :], self.fin[:, 3, :], ACT.Sqrt).then_inc(std_ready, 1)


def row_bcast(vector, rows):
    return vector.unsqueeze(0).to_broadcast([rows, vector.shape[0]])


def load_stage(c):
    nc, A = c.nc, c.A
    x_landed, landed, order_s, var_ready, std_ready = c.sem("x_landed", "consts_landed", "load_order", "load_var", "load_std")
    with nc.Block() as block:
        @block.gpsimd
        def _(pool):
            pool.dma_start(c.X[:, :, :], A["x"].rearrange("(p t) d -> p t d", t=WIN)).then_inc(x_landed, 16)

        @block.sync
        def _(sp):
            pairs = [(c.ident, "c_ident"), (c.tri, "c_tri"), (c.iota, "c_iota"), (c.iota_f, "c_iota_f"),
                     (c.blocks, "c_blocks"), (c.heads, "c_heads")]
            for buffer, name in pairs:
                sp.dma_start(buffer[:, :], A[name]).then_inc(landed, 16)
            sp.wait_ge(landed, 16 * len(pairs))

        @block.vector
        def _(dve):
            nc.vector.memset(c.ones[:, :], 1.0)
            dve.wait_ge(x_landed, 16)
            with dve.Fori(0, WIN) as t:
                nc.vector.bn_stats(c.stats[:, t, :], c.X[:, t, :]).then_inc(order_s, 1)
            dve.wait_ge(order_s, WIN)
            order = Order(dve, order_s)
            order.k = WIN
            c.finish_stats(order, var_ready, std_ready)

        @block.scalar
        def _(act):
            c.root(act, var_ready, std_ready)


def mix0_stage(c, mixer):
    nc, A = c.nc, c.A
    with ExitStack() as scope:
        def sb(*a):
            return c.sb(scope, *a)

        xn, xc, sq = sb("mx_xn", [P, WIN, D]), sb("mx_xc", [P, WIN, D]), sb("mx_sq", [P, WIN, D])
        neg_mean, rz = sb("mx_neg_mean", [P, WIN * HEADS]), sb("mx_rz", [P, WIN * HEADS])
        z = sb("mx_z", [P, 2, 2, 129])
        kcol = sb("mx_kcol", [128, 2, 2])
        vrow = sb("mx_vrow", [128, 2, D])
        u = sb("mx_u", [128, 2])
        srow = sb("mx_srow", [128, D])
        landed, order_s, xc_ready, sq_ready, ss_ready, std_ready, z_ready, z_used, zeroed, g_ready = c.sem(
            *("mx_" + n for n in ("landed", "order", "xc_ready", "sq_ready", "ss_ready", "std_ready", "z_ready", "z_used", "zeroed", "g_ready")))
        heads = "p t (h e) -> p (t h) e"
        xn_h, xc_h, sq_h = (b[:, :, :].rearrange(heads, h=HEADS) for b in (xn, xc, sq))
        with nc.Block() as block:
            @block.sync
            def _(sp):
                with nc.allow_non_contiguous_dma(reason="512 floats, once"):
                    for i, n in enumerate(("L0_mix_kln_weight", "L0_mix_kln_bias")):
                        sp.dma_start(kcol[:, :, i], A[n].rearrange("(a h) o e -> (h o e) a", a=2)).then_inc(landed, 16)
                for i, n in enumerate(("L0_mix_vln_weight", "L0_mix_vln_bias")):
                    sp.dma_start(vrow[:, i, :], row_bcast(A[n].rearrange("h o e -> (h o e)"), 128)).then_inc(landed, 16)

            @block.vector
            def _(dve):
                v = nc.vector
                v.memset(c.banks[0][:, :], 0.0).then_inc(zeroed, 1)
                v.memset(c.banks[1][:, :], 0.0).then_inc(zeroed, 1)
                v.memset(z[:, :, :, :], 1.0).then_inc(zeroed, 1)
                with dve.Fori(0, WIN) as t:
                    c.normalised(xn[:, t, :], t).then_inc(order_s, 1)
                dve.wait_ge(order_s, WIN)
                order = Order(dve, order_s)
                order.k = WIN
                order.then(v.tensor_reduce(neg_mean[:, :], xn_h, AX.X, ALU.add))
                order.then(v.tensor_scalar(neg_mean[:, :], neg_mean[:, :], -1.0 / HC, None, ALU.mult))
                v.tensor_tensor(xc_h, xn_h, neg_mean[:, :].unsqueeze(2).to_broadcast([P, WIN * HEADS, HC]), ALU.add).then_inc(xc_ready, 1)
                dve.wait_ge(sq_ready, 1)
                order.then(v.tensor_reduce(rz[:, :], sq_h, AX.X, ALU.add))
                v.tensor_scalar(rz[:, :], rz[:, :], 1.0 / (HC - 1), None, ALU.mult).then_inc(ss_ready, 1)
                dve.wait_ge(std_ready, 1)
                order.then(v.tensor_scalar(rz[:, :], rz[:, :], LN_EPS, None, ALU.add))
                order.then(v.reciprocal(rz[:, :], rz[:, :]))
                dve.wait_ge(zeroed, 3)

                def step(t, b):
                    wait_from(dve, z_used, t - 1)
                    for k in range(2):
                        last = v.tensor_tensor(z[:, b, k, 0:128].rearrange("p (h e) -> p h e", e=HC),
                                               xc[:, t, k * 128:(k + 1) * 128].rearrange("p (h e) -> p h e", e=HC),
                                               rz[:, bass.ds(t * HEADS + 4 * k, 4)].unsqueeze(2).to_broadcast([P, 4, HC]), ALU.mult)
                        last.then_inc(z_ready, 1)
                over_tiles(dve, step)
                dve.wait_ge(g_ready, 1)
                dve.wait_ge(landed, 64)
                order.then(v.tensor_copy(srow[:, :], c.banks[1][:, 0:D]))
                for k in range(2):
                    gram, s_col = c.banks[0][:, 129 * k:129 * k + 128], c.banks[0][:, 129 * k + 128:129 * k + 129]
                    m, cols = mixer[:, k, :], slice(128 * k, 128 * k + 128)
                    kw, kb = kcol[:, k, 0:1], kcol[:, k, 1:2]
                    order.then(v.tensor_scalar(m, srow[:, cols], kb, None, ALU.mult))
                    order.then(v.scalar_tensor_tensor(out=m, in0=gram, scalar=kw, in1=m, op0=ALU.mult, op1=ALU.add))
                    order.then(v.tensor_tensor(m, m, vrow[:, 0, cols], ALU.mult))
                    order.then(v.tensor_scalar(u[:, 0:1], s_col, kw, None, ALU.mult))
                    order.then(v.scalar_tensor_tensor(out=u[:, 1:2], in0=kb, scalar=float(N), in1=u[:, 0:1], op0=ALU.mult, op1=ALU.add))
                    order.then(v.scalar_tensor_tensor(out=m, in0=vrow[:, 1, cols], scalar=u[:, 1:2], in1=m, op0=ALU.mult, op1=ALU.add))
                    order.then(v.scalar_tensor_tensor(out=m, in0=m, scalar=1.0 / N, in1=c.blocks[:, :], op0=ALU.mult, op1=ALU.mult))

            @block.scalar
            def _(act):
                act.wait_ge(xc_ready, 1)
                nc.scalar.activation(sq[:, :, :], xc[:, :, :], ACT.Square).then_inc(sq_ready, 1)
                act.wait_ge(ss_ready, 1)
                nc.scalar.activation(rz[:, :], rz[:, :], ACT.Sqrt).then_inc(std_ready, 1)

            @block.tensor
            def _(pe):
                pe.wait_ge(zeroed, 3)

                def step(t, b):
                    pe.wait_ge(z_ready, 2 * t + 2)
                    for k in range(2):
                        zk = z[:, b, k, :]
                        nc.tensor.matmul(c.banks[0][:, 129 * k:129 * k + 129], zk[:, 0:128], zk, start=False, stop=False, skip_group_check=True)
                        last = nc.tensor.matmul(c.banks[1][:, 128 * k:128 * k + 128], c.ones[0:P, :], zk[:, 0:128], start=False, stop=False, skip_group_check=True)
                    last.then_inc(z_used, 1)
                over_tiles(pe, step)
                pe.wait_ge(z_used, WIN)
                pe.sem_inc(g_ready, 1)


def sort_stage(c, slot_row, slot_dst, slot_win):
    nc, A = c.nc, c.A
    with ExitStack() as scope:
        def sb(name, shape, dt=F32):
            return c.sb(scope, "so_" + name, shape, dt)

        masks = sb("masks", [P, WIN, EC], F16)
        raw = sb("raw", [P, 3, EC], I32)
        win, row, rank, code_hi, code_lo, tmp, tile_of, row_of, zero = (
            sb(n, [P, EC])[:, :] for n in ("win", "row", "rank", "code_hi", "code_lo", "tmp", "tile_of", "row_of", "zero"))
        scans = sb("scans", [P, 2, EC])
        counts, ntile, base = sb("counts", [P, WIN]), sb("ntile", [P, WIN]), sb("base", [P, WIN])
        cum, own = sb("cum", [P, WIN + 1]), sb("own", [1, TILES])
        landed, order_s, counted, summed = c.sem("so_landed", "so_order", "so_counted", "so_summed")
        with nc.Block() as block:
            @block.sync
            def _(sp):
                for i, n in enumerate(("dst", "src", "edge_type_2")):
                    sp.dma_start(raw[:, i, :], A[n].rearrange("(p j) -> p j", j=EC)).then_inc(landed, 16)

            @block.vector
            def _(dve):
                v, order = nc.vector, Order(dve, order_s)
                order.then(v.memset(zero, 0.0))
                dve.wait_ge(landed, 48)
                order.then(v.tensor_copy(rank, raw[:, 0, :]))
                order.then(v.tensor_scalar(tmp, rank, 1.0 / WIN, -(WIN - 1) / 2 / WIN, ALU.mult, ALU.add))
                order.then(v.tensor_scalar(row, tmp, ROUND, ROUND, ALU.add, ALU.subtract))
                order.then(v.scalar_tensor_tensor(out=win, in0=row, scalar=-float(WIN), in1=rank, op0=ALU.mult, op1=ALU.add))
                order.then(v.tensor_copy(code_lo, raw[:, 1, :]))
                order.then(v.tensor_copy(tmp, raw[:, 2, :]))
                order.then(v.tensor_scalar(tmp, tmp, 0.0, float(N), ALU.not_equal, ALU.mult))
                order.then(v.tensor_tensor(code_lo, code_lo, tmp, ALU.add))
                order.then(v.tensor_scalar(tmp, code_lo, 1.0 / 8, -3.5 / 8, ALU.mult, ALU.add))
                order.then(v.tensor_scalar(code_hi, tmp, ROUND, ROUND, ALU.add, ALU.subtract))
                order.then(v.scalar_tensor_tensor(out=code_lo, in0=code_hi, scalar=-8.0, in1=code_lo, op0=ALU.mult, op1=ALU.add))
                order.then(v.tensor_scalar(code_lo, code_lo, 128.0, 1.0, ALU.mult, ALU.add))
                order.then(v.tensor_tensor(code_lo, code_lo, row, ALU.add))
                for w in range(WIN):
                    v.tensor_scalar(masks[:, w, :], win, float(w), 0.0, ALU.is_equal, ALU.add,
                                    accum_out=counts[:, w:w + 1]).then_inc(counted, 1)
                dve.wait_ge(counted, WIN)
                dve.wait_ge(summed, 1)
                totals, before = c.banks[0][0:P, 0:WIN], c.banks[1][0:P, 0:WIN]
                order.then(v.tensor_scalar(ntile[:, :], totals, 1.0 / SLOT, (SLOT / 2 - 0.5) / SLOT, ALU.mult, ALU.add))
                order.then(v.tensor_scalar(ntile[:, :], ntile[:, :], ROUND, ROUND, ALU.add, ALU.subtract))
                order.then(v.memset(cum[:, 0:1], 0.0))
                order.then(v.tensor_tensor_scan(cum[:, 1:WIN + 1], ntile[:, :], zero[:, 0:WIN], 0.0, ALU.add, ALU.add))
                order.then(v.scalar_tensor_tensor(out=base[:, :], in0=cum[:, 0:WIN], scalar=float(SLOT), in1=before, op0=ALU.mult, op1=ALU.add))
                order.then(v.tensor_scalar(base[:, :], base[:, :], -1.0, None, ALU.add))
                order.then(v.memset(rank, 0.0))
                for w in range(WIN):
                    scan = scans[:, w % 2, :]
                    order.then(v.tensor_tensor_scan(scan, masks[:, w, :], zero, base[:, w:w + 1], ALU.add, ALU.add))
                    order.then(v.tensor_tensor(tmp, masks[:, w, :], scan, ALU.mult))
                    order.then(v.tensor_tensor(rank, rank, tmp, ALU.add))
                order.then(v.tensor_scalar(tmp, rank, 1.0 / SLOT, -(SLOT - 1) / 2 / SLOT, ALU.mult, ALU.add))
                order.then(v.tensor_scalar(tile_of, tmp, ROUND, ROUND, ALU.add, ALU.subtract))
                order.then(v.scalar_tensor_tensor(out=row_of, in0=tile_of, scalar=-float(SLOT), in1=rank, op0=ALU.mult, op1=ALU.add))
                order.then(v.memset(own[:, :], 0.0))
                for w in range(WIN - 1):
                    order.then(v.scalar_tensor_tensor(out=own[:, :], in0=c.iota[0:1, :], scalar=cum[0:1, w + 1:w + 2], in1=own[:, :], op0=ALU.is_ge, op1=ALU.add))
                order.then(v.tensor_copy(slot_win[:, :], own[:, :]))

            @block.tensor
            def _(pe):
                pe.wait_ge(counted, WIN)
                nc.tensor.matmul(c.banks[0][0:P, 0:WIN], c.ones[0:P, 0:P], counts[:, :], start=True, stop=True)
                nc.tensor.matmul(c.banks[1][0:P, 0:WIN], c.tri[0:P, 0:P], counts[:, :], start=True, stop=True).then_inc(summed, 1)

        G = 4
        hot_hi, hot_lo = sb("hot_hi", [P, G, SLOT], F16), sb("hot_lo", [P, G, SLOT], F16)
        hot_tile = sb("hot_tile", [P, G, TILES], F16)
        hi, lo, mid = (sb(n, [128, TILES])[:, :] for n in ("hi", "lo", "mid"))
        hots_ready, hots_used, zeroed, moved, move_order = c.sem("hots_ready", "hots_used", "mv_zeroed", "mv_moved", "mv_order")
        with nc.Block() as block:
            @block.vector
            def _(dve):
                v = nc.vector
                v.memset(c.banks[0][:, :], 0.0).then_inc(zeroed, 1)
                v.memset(c.banks[1][:, :], 0.0).then_inc(zeroed, 1)

                def hots(j, g):
                    wait_from(dve, hots_used, j - (G - 1))
                    v.tensor_scalar(hot_tile[:, g, :], c.iota[0:P, :], col(tile_of, j), None, ALU.is_equal)
                    v.tensor_scalar(hot_hi[:, g, :], c.iota[0:P, 0:SLOT], col(row_of, j), col(code_hi, j), ALU.is_equal, ALU.mult)
                    v.tensor_scalar(hot_lo[:, g, :], c.iota[0:P, 0:SLOT], col(row_of, j), col(code_lo, j), ALU.is_equal, ALU.mult).then_inc(hots_ready, 1)

                for g in range(G):
                    hots(g, g)
                with dve.Fori(G, EC - G + 1, G) as j:
                    for g in range(G):
                        hots(j + g, g)
                dve.wait_ge(moved, 1)
                order = Order(dve, move_order)
                order.then(v.tensor_copy(hi, c.banks[0][:, 0:TILES]))
                order.then(v.tensor_copy(lo, c.banks[1][:, 0:TILES]))
                order.then(v.tensor_scalar(mid, lo, 1.0 / 128, -63.5 / 128, ALU.mult, ALU.add))
                order.then(v.tensor_scalar(mid, mid, ROUND, ROUND, ALU.add, ALU.subtract))
                order.then(v.scalar_tensor_tensor(out=lo, in0=mid, scalar=-128.0, in1=lo, op0=ALU.mult, op1=ALU.add))
                order.then(v.tensor_scalar(slot_dst[:, :], lo, -1.0, None, ALU.add))
                order.then(v.scalar_tensor_tensor(out=hi, in0=hi, scalar=8.0, in1=mid, op0=ALU.mult, op1=ALU.add))
                order.then(v.tensor_copy(slot_row[:, :], hi))

            @block.tensor
            def _(pe):
                pe.wait_ge(zeroed, 2)

                def add(j, g):
                    pe.wait_ge(hots_ready, j + 1)
                    nc.tensor.matmul(c.banks[0][:, 0:TILES], hot_hi[:, g, :], hot_tile[:, g, :], start=False, stop=False, skip_group_check=True)
                    nc.tensor.matmul(c.banks[1][:, 0:TILES], hot_lo[:, g, :], hot_tile[:, g, :], start=False, stop=False, skip_group_check=True).then_inc(hots_used, 1)

                with pe.Fori(0, EC - G + 1, G) as j:
                    for g in range(G):
                        add(j + g, g)
                pe.wait_ge(hots_used, EC)
                pe.sem_inc(moved, 1)


def message_stage(c, layer, aggr, selfp, mixer, table_y):
    nc, A, first = c.nc, c.A, layer == 0
    n_ = lambda name: f"me{layer}_{name}"
    with ExitStack() as scope:
        def sb(name, shape, dt=F32):
            return c.sb(scope, n_(name), shape, dt)

        w_rel, w_self = sb("w_rel", [128, 2, RELS * D]), sb("w_self", [128, 2, D])
        bias = sb("bias", [1, 2, D])
        gamma = sb("gamma", [P, D])
        h, normed = sb("h", [P, 2, D]), sb("normed", [P, 2, D])
        hT, y = sb("hT", [128, 2, 2, P]), sb("y", [P, 2, RELS * D])
        ty = table_y.rearrange("(r p t) d -> p r t d", r=RELS, t=WIN)
        landed, order_s, var_ready, std_ready, n_ready, h_ready, turned, t_ready, products, y_ready, kept = c.sem(
            *(n_(n) for n in ("landed", "order", "var", "std", "n_ready", "h_ready", "turned", "t_ready", "products", "y_ready", "kept")))
        y_stored = [c.sem(n_(f"y_stored{i}")) for i in range(2)]
        with nc.Block() as block:
            @block.sync
            def _(sp):
                for r in range(RELS):
                    sp.dma_start(w_rel[:, :, r * D:(r + 1) * D], A["L0_gnn_W"][layer, r].rearrange("(k p) n -> p k n", k=2)).then_inc(landed, 16)
                sp.dma_start(w_self[:, :, :], A["L0_gnn_loop_w"][layer].rearrange("(k p) n -> p k n", k=2)).then_inc(landed, 16)
                for i, n in enumerate(("L0_gnn_bias", "L0_gnn_ln_beta")):
                    sp.dma_start(bias[:, i, :], A[n][layer].unsqueeze(0)).then_inc(landed, 16)
                if not first:
                    sp.dma_start(gamma[:, :], row_bcast(A["L0_gnn_ln_gamma"][layer - 1], P)).then_inc(landed, 16)

                def step(t, b):
                    sp.wait_ge(y_ready, t + 1)
                    sp.dma_start(ty[:, :, t, :], y[:, b, :].rearrange("p (r d) -> p r d", r=RELS)).then_inc(y_stored[b], 16)
                over_tiles(sp, step)
                sp.wait_ge(y_stored[0], 16 * (WIN // 2 + 1))
                sp.wait_ge(y_stored[1], 16 * (WIN // 2))

            @block.vector
            def _(dve):
                v = nc.vector
                if not first:
                    dve.wait_ge(landed, 96)
                    with dve.Fori(0, WIN) as t:
                        v.bn_stats(c.stats[:, t, :], aggr[:, t, :]).then_inc(order_s, 1)
                    dve.wait_ge(order_s, WIN)
                    order = Order(dve, order_s)
                    order.k = WIN
                    c.finish_stats(order, var_ready, std_ready)
                    start = order.k

                def make_h(t, b):
                    wait_from(dve, turned, t - 1)
                    if first:
                        c.normalised(h[:, b, :], t).then_inc(h_ready, 1)
                        return
                    order = Order(dve, order_s, t, 2)
                    order.start = order.start + start
                    order.then(v.tensor_scalar(normed[:, b, :], aggr[:, t, :], col(c.rstd, t), col(c.nmr, t), ALU.mult, ALU.add))
                    order.then(v.tensor_tensor(normed[:, b, :], normed[:, b, :], gamma[:, :], ALU.mult))
                    v.tensor_tensor(h[:, b, :], normed[:, b, :], selfp[:, t, :], ALU.add).then_inc(n_ready, 1)

                def keep(t, b):
                    dve.wait_ge(products, t + 1)
                    if first:
                        v.tensor_scalar(selfp[:, t, :], c.banks[4 + b][0:P, 0:D], 1.0, None, ALU.mult)
                        v.tensor_tensor(c.X[:, t, :], c.X[:, t, :], h[:, b, :], ALU.add).then_inc(order_s, 1)
                        dve.wait_ge(order_s, t + 1)
                        v.tensor_tensor(c.X[:, t, :], c.X[:, t, :], c.banks[4 + b][0:P, D:2 * D], ALU.add).then_inc(kept, 1)
                    else:
                        v.tensor_scalar(selfp[:, t, :], c.banks[4 + b][0:P, 0:D], 1.0, None, ALU.mult).then_inc(kept, 1)
                over_tiles(dve, keep, make_h)

            @block.scalar
            def _(act):
                if not first:
                    c.root(act, var_ready, std_ready)

                def copy_t(t, b):
                    if not first:
                        act.wait_ge(n_ready, t + 1)
                        nc.scalar.activation(h[:, b, :], h[:, b, :], ACT.Relu).then_inc(h_ready, 1)
                    act.wait_ge(turned, t + 1)
                    wait_from(act, products, t - 1)
                    nc.scalar.activation(hT[:, b, :, :], c.banks[b][:, 0:256].rearrange("p (k n) -> p k n", k=2)[:, :, 0:P], ACT.Copy).then_inc(t_ready, 1)

                def copy_y(t, b):
                    act.wait_ge(products, t + 1)
                    if not isinstance(t, int) or t >= 2:
                        act.wait_ge(y_stored[b], t * 8 - 8 * b)
                    nc.scalar.activation(y[:, b, :], c.banks[2 + b][0:P, :], ACT.Copy).then_inc(y_ready, 1)
                over_tiles(act, copy_y, copy_t)

            @block.tensor
            def _(pe):
                def turn(t, b):
                    pe.wait_ge(h_ready, t + 1)
                    wait_from(pe, t_ready, t - 1)
                    for k in range(2):
                        last = nc.tensor.transpose(c.banks[b][:, k * 128:k * 128 + P], h[:, b, k * 128:(k + 1) * 128], c.ident[0:P, 0:P])
                    last.then_inc(turned, 1)

                def multiply(t, b):
                    pe.wait_ge(t_ready, t + 1)
                    wait_from(pe, y_ready, t - 1)
                    wait_from(pe, kept, t - 1)
                    for k in range(2):
                        nc.tensor.matmul(c.banks[2 + b][0:P, :], hT[:, b, k, :], w_rel[:, k, :], start=(k == 0), stop=(k == 1))
                    own = c.banks[4 + b][0:P, 0:D]
                    for k in range(2):
                        nc.tensor.matmul(own, hT[:, b, k, :], w_self[:, k, :], start=(k == 0), stop=False, skip_group_check=True)
                    for i in range(2):
                        last = nc.tensor.matmul(own, c.ones[0:1, 0:P], bias[0:1, i, :], start=False, stop=(i == 1), skip_group_check=True)
                    if first:
                        for k in range(2):
                            last = nc.tensor.matmul(c.banks[4 + b][0:P, D + 128 * k:D + 128 * k + 128], hT[:, b, k, :], mixer[:, k, :],
                                                    start=False, stop=True, skip_group_check=True)
                    last.then_inc(products, 1)
                pe.wait_ge(landed, 80 if first else 96)
                over_tiles(pe, multiply, turn)


def gather_stage(c, layer, aggr, table_y, slot_row, slot_dst, slot_win):
    nc = c.nc
    n_ = lambda name: f"ga{layer}_{name}"
    with ExitStack() as scope:
        def sb(name, shape, dt=F32):
            return c.sb(scope, n_(name), shape, dt)

        index = sb("index", [128, 2, HALF], I32)
        got, hot = sb("got", [128, RING, D]), sb("hot", [128, 4, P])
        index_ready, released, summed, hot_ready, added, zeroed = c.sem(
            *(n_(n) for n in ("index_ready", "released", "summed", "hot_ready", "added", "zeroed")))
        gathered = [c.sem(n_(f"gathered{g}")) for g in range(RING)]
        with nc.Block() as block:
            @block.gpsimd
            def _(pool):
                def half(s, k):
                    wait_from(pool, summed, s - HALF)
                    nc.gpsimd.tensor_copy(index[:, k, :], slot_row[:, bass.ds(s, HALF)]).then_inc(index_ready, 1)
                    pool.wait_ge(index_ready, s // HALF + 1)
                    pool.sem_inc(released, 1)
                    for g in range(HALF):
                        nc.gpsimd.indirect_dma_start(got[:, k * HALF + g, :], None, table_y,
                                                     bass.IndirectOffsetOnAxis(ap=index[:, k, g:g + 1], axis=0)).then_inc(gathered[k * HALF + g], 16)
                half(0, 0)
                half(HALF, 1)
                with pool.Fori(RING, TILES - RING + 1, RING) as s:
                    half(s, 0)
                    half(s + HALF, 1)

            @block.tensor
            def _(pe):
                def total(s, g):
                    pe.wait_ge(hot_ready, s + g + 1)
                    wait_from(pe, added, s + g - 3)
                    pe.wait_ge(gathered[g], s + 16)
                    nc.tensor.matmul(c.banks[g % 4][0:P, 0:D], hot[:, g % 4, :], got[:, g, :], start=True, stop=True).then_inc(summed, 1)
                for g in range(RING):
                    total(0, g)
                with pe.Fori(RING, TILES - RING + 1, RING) as s:
                    for g in range(RING):
                        total(s, g)

            @block.vector
            def _(dve):
                v = nc.vector

                def make_hot(s, g):
                    wait_from(dve, summed, s + g - 3)
                    v.tensor_scalar(hot[:, g % 4, :], c.iota_f[:, 0:P], col(slot_dst, s + g), None, ALU.is_equal).then_inc(hot_ready, 1)

                def add(s, g):
                    w = dve.value_load(slot_win[0:1, bass.ds(s + g, 1)], min_val=0, max_val=WIN - 1)
                    dve.wait_ge(summed, s + g + 1)
                    wait_from(dve, added, s + g)
                    v.tensor_tensor(aggr[:, bass.ds(w, 1), :].rearrange("p o d -> p (o d)"), aggr[:, bass.ds(w, 1), :].rearrange("p o d -> p (o d)"),
                                    c.banks[g % 4][0:P, 0:D], ALU.add).then_inc(added, 1)
                v.memset(aggr[:, :, :], 0.0).then_inc(zeroed, 1)
                make_hot(0, 0)
                make_hot(0, 1)
                dve.wait_ge(zeroed, 1)
                for g in range(2, RING):
                    make_hot(0, g)
                    add(0, g - 2)
                with dve.Fori(RING, TILES - RING + 1, RING) as s:
                    for g in range(RING):
                        make_hot(s, g)
                        add(s - RING if g < 2 else s, g - 2 if g >= 2 else g + RING - 2)
                for g in (RING - 2, RING - 1):
                    add(TILES - RING, g)


def gnn_out_stage(c, aggr, selfp):
    nc, A = c.nc, c.A
    with ExitStack() as scope:
        gamma, normed = c.sb(scope, "go_gamma", [P, D]), c.sb(scope, "go_normed", [P, 2, D])
        landed, order_s, var_ready, std_ready, x_order, var2_ready, std2_ready, added = c.sem(
            *("go_" + n for n in ("landed", "order", "var", "std", "x_order", "var2", "std2", "added")))
        with nc.Block() as block:
            @block.sync
            def _(sp):
                sp.dma_start(gamma[:, :], row_bcast(A["L0_gnn_ln_gamma"][LAYERS - 1], P)).then_inc(landed, 16)

            @block.vector
            def _(dve):
                v = nc.vector
                with dve.Fori(0, WIN) as t:
                    v.bn_stats(c.stats[:, t, :], aggr[:, t, :]).then_inc(order_s, 1)
                dve.wait_ge(order_s, WIN)
                order = Order(dve, order_s)
                order.k = WIN
                c.finish_stats(order, var_ready, std_ready)
                dve.wait_ge(landed, 16)

                def step(t, b):
                    order = Order(dve, x_order, t, 4)
                    n = normed[:, b, :]
                    order.then(v.tensor_scalar(n, aggr[:, t, :], col(c.rstd, t), col(c.nmr, t), ALU.mult, ALU.add))
                    order.then(v.tensor_tensor(n, n, gamma[:, :], ALU.mult))
                    order.then(v.tensor_tensor(n, n, selfp[:, t, :], ALU.add))
                    order.then(v.tensor_tensor(c.X[:, t, :], c.X[:, t, :], n, ALU.add))
                    v.bn_stats(c.stats[:, t, :], c.X[:, t, :]).then_inc(added, 1)
                over_tiles(dve, step)
                dve.wait_ge(added, WIN)
                order = Order(dve, order_s)
                order.k = WIN + STATS_STEPS
                c.finish_stats(order, var2_ready, std2_ready)

            @block.scalar
            def _(act):
                c.root(act, var_ready, std_ready)
                c.root(act, var2_ready, std2_ready)


STATS_STEPS = 8


def slice_stage(c):
    nc, A, banks = c.nc, c.A, c.banks
    with ExitStack() as scope:
        def sb(name, shape, dt=F32):
            return c.sb(scope, "sl_" + name, shape, dt)

        W = sb("weights", [P, WIN, INNER])
        logit_w = sb("logit_w", [128, 2, INNER])
        logit_b = sb("logit_b", [1, INNER])
        M = sb("M", [128, 4, D])
        b_out = sb("b_out", [1, D])
        with ExitStack() as prep:
            def pb(name, shape, dt=F32):
                return c.sb(prep, "slp_" + name, shape, dt)

            w_x, w_xT = pb("w_x", [128, 2, INNER]), pb("w_xT", [128, 4, D])
            pair = pb("pair", [128, 128])
            b_x, b_slice = pb("b_x", [128, 4]), pb("b_slice", [1, SD])
            inv_temp = pb("inv_temp", [128, HEADS])
            landed, cleared, order_s, turned, copied, made = c.sem(*("slp_" + n for n in ("landed", "cleared", "order", "turned", "copied", "made")))
            with nc.Block() as block:
                @block.sync
                def _(sp):
                    sp.dma_start(w_x[:, :, :], A["L0_ffn_W_x"].rearrange("(k p) n -> p k n", k=2)).then_inc(landed, 16)
                    with nc.allow_non_contiguous_dma(reason="512 floats, once"):
                        sp.dma_start(b_x[:, :], A["L0_ffn_b_x"].rearrange("(k p) -> p k", p=128)).then_inc(landed, 16)
                    sp.dma_start(b_slice[:, :], A["L0_ffn_b_slice"].unsqueeze(0)).then_inc(landed, 16)
                    sp.dma_start(inv_temp[:, :], row_bcast(A["L0_ffn_temperature"].rearrange("a h b e -> (a h b e)"), 128)).then_inc(landed, 16)
                    sp.dma_start(b_out[:, :], A["L0_ffn_b_out"].unsqueeze(0)).then_inc(landed, 16)
                    sp.wait_ge(cleared, 1)
                    for i in range(2):
                        sp.dma_start(pair[i * SD:(i + 1) * SD, i * SD:(i + 1) * SD], A["L0_ffn_W_slice"]).then_inc(landed, 16)

                @block.tensor
                def _(pe):
                    pe.wait_ge(landed, 112)
                    for k in range(2):
                        for a in range(4):
                            nc.tensor.transpose(banks[k][:, a * 128:a * 128 + 128], w_x[:, k, a * 128:a * 128 + 128], c.ident[:, :]).then_inc(turned, 1)
                    pe.wait_ge(copied, 2)
                    for k in range(2):
                        for a in range(4):
                            nc.tensor.matmul(banks[2 + k][:, a * 128:a * 128 + 128], w_xT[:, a, k * 128:k * 128 + 128], pair[:, :],
                                             start=(a == 0), stop=True, skip_group_check=True)
                    for a in range(4):
                        last = nc.tensor.matmul(banks[4][0:1, a * 128:a * 128 + 128], b_x[:, a:a + 1], pair[:, :],
                                                start=(a == 0), stop=True, skip_group_check=True)
                    last.then_inc(made, 1)

                @block.scalar
                def _(act):
                    for k in range(2):
                        act.wait_ge(turned, 4 * k + 4)
                        nc.scalar.activation(w_xT[:, :, k * 128:k * 128 + 128], banks[k][:, :].rearrange("p (a n) -> p a n", a=4), ACT.Copy).then_inc(copied, 1)

                @block.vector
                def _(dve):
                    v, order = nc.vector, Order(dve, order_s)
                    v.memset(pair[:, :], 0.0).then_inc(cleared, 1)
                    dve.wait_ge(landed, 112)
                    order.then(v.tensor_scalar(inv_temp[:, :], inv_temp[:, :], 0.1, 5.0, ALU.max, ALU.min))
                    order.then(v.reciprocal(inv_temp[:, :], inv_temp[:, :]))
                    dve.wait_ge(made, 1)
                    by_head = "p (h g) -> p h g"
                    for k in range(2):
                        v.tensor_tensor(logit_w[:, k, :].rearrange(by_head, h=HEADS), banks[2 + k][:, :].rearrange(by_head, h=HEADS),
                                        inv_temp[:, :].unsqueeze(2).to_broadcast([128, HEADS, SD]), ALU.mult)
                    order.then(v.tensor_tensor(logit_b[:, :].rearrange(by_head, h=HEADS), banks[4][0:1, :].rearrange(by_head, h=HEADS),
                                               b_slice[:, :].unsqueeze(1).to_broadcast([1, HEADS, SD]), ALU.add))
                    order.then(v.tensor_tensor(logit_b[:, :].rearrange(by_head, h=HEADS), logit_b[:, :].rearrange(by_head, h=HEADS),
                                               inv_temp[0:1, :].unsqueeze(2).to_broadcast([1, HEADS, SD]), ALU.mult))

        with ExitStack() as s1:
            def qb(name, shape, dt=F32):
                return c.sb(s1, "sla_" + name, shape, dt)

            h, hT = qb("h", [P, 2, D]), qb("hT", [128, 2, 2, P])
            e, w = qb("e", [P, 2, INNER]), qb("w", [P, 2, INNER])
            peak, total = qb("peak", [P, 2, HEADS]), qb("total", [P, 2, HEADS])
            order_s, h_ready, turned, t_ready, logits, e_ready, exped, r_ready, w_ready, w_kept, pooled = c.sem(
                *("sla_" + n for n in ("order", "h_ready", "turned", "t_ready", "logits", "e_ready", "exped", "r_ready", "w_ready", "w_kept", "pooled")))
            by_head = "p (h g) -> p h g"
            with nc.Block() as block:
                @block.vector
                def _(dve):
                    v = nc.vector
                    for i in (4, 5, 6):
                        v.memset(banks[i][:, :], 0.0)

                    def make_h(t, b):
                        wait_from(dve, pooled, t - 1)
                        c.normalised(h[:, b, :], t).then_inc(h_ready, 1)

                    def softmax(t, b):
                        order = Order(dve, order_s, t, 2)
                        dve.wait_ge(logits, t + 1)
                        p, eb = banks[2 + b][0:P, :].rearrange(by_head, h=HEADS), e[:, b, :].rearrange(by_head, h=HEADS)
                        order.then(v.tensor_reduce(peak[:, b, :], p, AX.X, ALU.max))
                        wait_from(dve, w_ready, t - 1)
                        v.tensor_tensor(eb, p, peak[:, b, :].unsqueeze(2).to_broadcast([P, HEADS, SD]), ALU.subtract).then_inc(e_ready, 1)
                        dve.wait_ge(exped, t + 1)
                        order.then(v.tensor_reduce(total[:, b, :], eb, AX.X, ALU.add))
                        v.reciprocal(total[:, b, :], total[:, b, :]).then_inc(r_ready, 1)
                    over_tiles(dve, softmax, make_h)

                @block.gpsimd
                def _(pool):
                    def weights(t, b):
                        pool.wait_ge(r_ready, t + 1)
                        wait_from(pool, pooled, t - 1)
                        wait_from(pool, w_kept, t - 1)
                        nc.gpsimd.tensor_tensor(w[:, b, :].rearrange(by_head, h=HEADS), e[:, b, :].rearrange(by_head, h=HEADS),
                                                total[:, b, :].unsqueeze(2).to_broadcast([P, HEADS, SD]), ALU.mult).then_inc(w_ready, 1)
                    over_tiles(pool, weights)

                @block.scalar
                def _(act):
                    def copy_t(t, b):
                        act.wait_ge(turned, t + 1)
                        wait_from(act, logits, t - 1)
                        nc.scalar.activation(hT[:, b, :, :], banks[b][:, 0:256].rearrange("p (k n) -> p k n", k=2)[:, :, 0:P], ACT.Copy).then_inc(t_ready, 1)

                    def exp(t, b):
                        act.wait_ge(e_ready, t + 1)
                        nc.scalar.activation(e[:, b, :], e[:, b, :], ACT.Exp).then_inc(exped, 1)
                        act.wait_ge(w_ready, t + 1)
                        nc.scalar.activation(W[:, t, :], w[:, b, :], ACT.Copy).then_inc(w_kept, 1)
                    over_tiles(act, exp, copy_t)

                @block.tensor
                def _(pe):
                    def head(t, b):
                        pe.wait_ge(h_ready, t + 1)
                        wait_from(pe, t_ready, t - 1)
                        for k in range(2):
                            last = nc.tensor.transpose(banks[b][:, k * 128:k * 128 + P], h[:, b, k * 128:(k + 1) * 128], c.ident[0:P, 0:P])
                        last.then_inc(turned, 1)
                        pe.wait_ge(t_ready, t + 1)
                        wait_from(pe, e_ready, t - 1)
                        for k in range(2):
                            nc.tensor.matmul(banks[2 + b][0:P, :], hT[:, b, k, :], logit_w[:, k, :], start=(k == 0), stop=False)
                        nc.tensor.matmul(banks[2 + b][0:P, :], c.ones[0:1, 0:P], logit_b[:, :], start=False, stop=True).then_inc(logits, 1)

                    def pool_x(t, b):
                        pe.wait_ge(w_ready, t + 1)
                        for a in range(4):
                            wa = w[:, b, a * 128:(a + 1) * 128]
                            nc.tensor.matmul(banks[4 + a // 2][:, (a % 2) * D:(a % 2 + 1) * D], wa, h[:, b, :], start=False, stop=False, skip_group_check=True)
                            last = nc.tensor.matmul(banks[6][:, a:a + 1], wa, c.ones[0:P, 0:1], start=False, stop=False, skip_group_check=True)
                        last.then_inc(pooled, 1)
                    over_tiles(pe, pool_x, head)

        with ExitStack() as s2:
            def rb(name, shape, dt=F32):
                return c.sb(s2, "slb_" + name, shape, dt)

            w_fx, b_fx = rb("w_fx", [128, 2, INNER]), rb("b_fx", [1, INNER])
            w_qkv = rb("w_qkv", [SD, 3, SD])
            w_out = rb("w_out", [SD, HEADS, D])
            inv, share = rb("inv", [128, 4]), rb("share", [128, 4])
            U, UT, shareT = rb("U", [128, 4, D]), rb("UT", [128, 2, INNER]), rb("shareT", [1, INNER])
            tokT, qkvT = rb("tokT", [SD, INNER]), rb("qkvT", [SD, 3, INNER])
            attn, attnT = rb("attn", [SD, HEADS, SD]), rb("attnT", [SD, INNER])
            peak, total, vw = rb("peak", [SD, HEADS]), rb("total", [SD, HEADS]), rb("vw", [SD, HEADS, D])
            landed, order_s, act_done, pe_done = c.sem(*("slb_" + n for n in ("landed", "dve_steps", "act_steps", "pe_steps")))
            with nc.Block() as block:
                @block.sync
                def _(sp):
                    sp.dma_start(w_fx[:, :, :], A["L0_ffn_W_fx"].rearrange("(k p) n -> p k n", k=2)).then_inc(landed, 16)
                    sp.dma_start(b_fx[:, :], A["L0_ffn_b_fx"].unsqueeze(0)).then_inc(landed, 16)
                    for i, n in enumerate("qkv"):
                        sp.dma_start(w_qkv[:, i, :], A[f"L0_ffn_W_{n}"]).then_inc(landed, 16)
                    sp.dma_start(w_out[:, :, :], A["L0_ffn_W_out"].rearrange("(h c) n -> c h n", c=SD)).then_inc(landed, 16)

                @block.vector
                def _(dve):
                    v, order = nc.vector, Order(dve, order_s)
                    order.then(v.tensor_scalar(inv[:, :], banks[6][:, 0:4], 1e-5, None, ALU.add))
                    order.then(v.reciprocal(inv[:, :], inv[:, :]))
                    order.then(v.tensor_tensor(share[:, :], inv[:, :], banks[6][:, 0:4], ALU.mult))
                    for a in range(4):
                        order.then(v.tensor_scalar(U[:, a, :], banks[4 + a // 2][:, (a % 2) * D:(a % 2 + 1) * D], inv[:, a:a + 1], None, ALU.mult))
                    assert order.k == 7
                    dve.wait_ge(pe_done, 4)
                    scores = banks[7][0:SD, :].rearrange("p (h g) -> p h g", h=HEADS)
                    order.then(v.tensor_reduce(peak[:, :], scores, AX.X, ALU.max))
                    order.then(v.tensor_tensor(attn[:, :, :], scores, peak[:, :].unsqueeze(2).to_broadcast([SD, HEADS, SD]), ALU.subtract))
                    dve.wait_ge(act_done, 6)
                    order.then(v.tensor_reduce(total[:, :], attn[:, :, :], AX.X, ALU.add))
                    order.then(v.reciprocal(total[:, :], total[:, :]))
                    order.then(v.tensor_tensor(attn[:, :, :], attn[:, :, :], total[:, :].unsqueeze(2).to_broadcast([SD, HEADS, SD]), ALU.mult))
                    assert order.k == 12
                    dve.wait_ge(pe_done, 5)
                    for i in range(4):
                        order.then(v.tensor_copy(vw[:, 2 * i:2 * i + 2, :].rearrange("p a d -> p (a d)"), banks[i][0:SD, :]))

                @block.scalar
                def _(act):
                    act.wait_ge(pe_done, 1)
                    for k in range(2):
                        nc.scalar.activation(UT[:, k, :], banks[k][:, :], ACT.Copy).then_inc(act_done, 1)
                    nc.scalar.activation(shareT[:, :], banks[2][0:1, :], ACT.Copy).then_inc(act_done, 1)
                    act.wait_ge(pe_done, 2)
                    nc.scalar.activation(tokT[:, :], banks[3][0:SD, :], ACT.Copy).then_inc(act_done, 1)
                    act.wait_ge(pe_done, 3)
                    for i in range(3):
                        last = nc.scalar.activation(qkvT[:, i, :], banks[4 + i][0:SD, :], ACT.Copy)
                    last.then_inc(act_done, 1)
                    act.wait_ge(order_s, 9)
                    nc.scalar.activation(attn[:, :, :], attn[:, :, :], ACT.Exp, scale=float(SD) ** -0.5).then_inc(act_done, 1)
                    act.wait_ge(pe_done, 6)
                    nc.scalar.activation(attnT[:, :], banks[4][0:SD, :], ACT.Copy).then_inc(act_done, 1)
                    act.wait_ge(pe_done, 7)
                    for i in range(2):
                        nc.scalar.activation(M[:, 2 * i:2 * i + 2, :].rearrange("p a d -> p (a d)"), banks[5 + i][:, :], ACT.Copy).then_inc(act_done, 1)

                @block.tensor
                def _(pe):
                    mm = nc.tensor.matmul
                    pe.wait_ge(order_s, 7)
                    for k in range(2):
                        for a in range(4):
                            nc.tensor.transpose(banks[k][:, a * 128:a * 128 + 128], U[:, a, k * 128:k * 128 + 128], c.ident[:, :])
                    for a in range(4):
                        last = nc.tensor.transpose(banks[2][0:1, a * 128:a * 128 + 128], share[:, a:a + 1], c.ident[:, :])
                    last.then_inc(pe_done, 1)
                    pe.wait_ge(act_done, 3)
                    pe.wait_ge(landed, 96)
                    for h in range(HEADS):
                        at, o = slice(h * SD, (h + 1) * SD), banks[3][0:SD, h * SD:(h + 1) * SD]
                        for k in range(2):
                            mm(o, w_fx[:, k, at], UT[:, k, at], start=(h == 0 and k == 0), stop=False, skip_group_check=True)
                        last = mm(o, b_fx[0:1, at], shareT[0:1, at], start=False, stop=True, skip_group_check=True)
                    last.then_inc(pe_done, 1)
                    pe.wait_ge(act_done, 4)
                    for i in range(3):
                        last = mm(banks[4 + i][0:SD, :], w_qkv[:, i, :], tokT[:, :], start=True, stop=True)
                    last.then_inc(pe_done, 1)
                    pe.wait_ge(act_done, 5)
                    for h in range(HEADS):
                        at = slice(h * SD, (h + 1) * SD)
                        last = mm(banks[7][0:SD, at], qkvT[:, 0, at], qkvT[:, 1, at], start=(h == 0), stop=True, skip_group_check=True)
                    last.then_inc(pe_done, 1)
                    for h in range(HEADS):
                        last = mm(banks[h // 2][0:SD, (h % 2) * D:(h % 2 + 1) * D], qkvT[:, 2, h * SD:(h + 1) * SD], w_out[:, h, :],
                                  start=(h % 2 == 0), stop=True, skip_group_check=True)
                    last.then_inc(pe_done, 1)
                    pe.wait_ge(order_s, 12)
                    for h in range(HEADS):
                        last = nc.tensor.transpose(banks[4][0:SD, h * SD:(h + 1) * SD], attn[:, h, :], c.ident[0:SD, 0:SD])
                    last.then_inc(pe_done, 1)
                    pe.wait_ge(act_done, 7)
                    pe.wait_ge(order_s, 16)
                    for h in range(HEADS):
                        a = h // 2
                        last = mm(banks[5 + a // 2][(h % 2) * SD:(h % 2 + 1) * SD, (a % 2) * D:(a % 2 + 1) * D],
                                  attnT[:, h * SD:(h + 1) * SD], vw[:, h, :], start=(a % 2 == 0), stop=True, skip_group_check=True)
                    last.then_inc(pe_done, 1)

        with ExitStack() as s3:
            w, wT = c.sb(s3, "slc_w", [P, 2, INNER]), c.sb(s3, "slc_wT", [128, 2, 4, P])
            order_s, w_ready, turned, t_ready, products, added, var_ready, std_ready = c.sem(
                *("slc_" + n for n in ("order", "w_ready", "turned", "t_ready", "products", "added", "var", "std")))
            with nc.Block() as block:
                @block.gpsimd
                def _(pool):
                    def stage(t, b):
                        wait_from(pool, turned, t - 1)
                        nc.gpsimd.tensor_copy(w[:, b, :], W[:, t, :]).then_inc(w_ready, 1)
                    over_tiles(pool, stage)

                @block.tensor
                def _(pe):
                    def turn(t, b):
                        pe.wait_ge(w_ready, t + 1)
                        wait_from(pe, t_ready, t - 1)
                        for a in range(4):
                            last = nc.tensor.transpose(banks[b][:, a * 128:a * 128 + P], w[:, b, a * 128:(a + 1) * 128], c.ident[0:P, 0:P])
                        last.then_inc(turned, 1)

                    def multiply(t, b):
                        pe.wait_ge(t_ready, t + 1)
                        wait_from(pe, added, t - 1)
                        o = banks[2 + b][0:P, 0:D]
                        for a in range(4):
                            nc.tensor.matmul(o, wT[:, b, a, :], M[:, a, :], start=(a == 0), stop=False)
                        nc.tensor.matmul(o, c.ones[0:1, 0:P], b_out[:, :], start=False, stop=True).then_inc(products, 1)
                    over_tiles(pe, multiply, turn)

                @block.scalar
                def _(act):
                    def copy_t(t, b):
                        act.wait_ge(turned, t + 1)
                        wait_from(act, products, t - 1)
                        nc.scalar.activation(wT[:, b, :, :], banks[b][:, :].rearrange("p (a n) -> p a n", a=4)[:, :, 0:P], ACT.Copy).then_inc(t_ready, 1)
                    over_tiles(act, copy_t)
                    c.root(act, var_ready, std_ready)

                @block.vector
                def _(dve):
                    def add(t, b):
                        dve.wait_ge(products, t + 1)
                        nc.vector.tensor_tensor(c.X[:, t, :], c.X[:, t, :], banks[2 + b][0:P, 0:D], ALU.add).then_inc(added, 1)
                        dve.wait_ge(added, t + 1)
                        nc.vector.bn_stats(c.stats[:, t, :], c.X[:, t, :]).then_inc(order_s, 1)
                    over_tiles(dve, add)
                    dve.wait_ge(order_s, WIN)
                    order = Order(dve, order_s)
                    order.k = WIN
                    c.finish_stats(order, var_ready, std_ready)


def attention_stage(c):
    nc, A, banks = c.nc, c.A, c.banks
    KV = 128 + 4
    with ExitStack() as scope:
        def sb(name, shape, dt=F32):
            return c.sb(scope, "at_" + name, shape, dt)

        Q = sb("Q", [P, WIN, D])
        rms = sb("rms", [P, WIN])
        kv = sb("kv", [128, 2, KV])
        w_out, b_out = sb("w_out", [128, 2, D]), sb("b_out", [1, D])
        XTW = GD * GH + GH
        XT = sb("XT", [P, WIN, XTW])
        AL = sb("AL", [P, WIN, GH])
        ends = sb("ends", [P, 2, WIN], I32)
        table_x = nc.dram_tensor("table_x", [N, XTW], F32, kind="Internal").ap()
        table_l = nc.dram_tensor("table_l", [N, GH], F32, kind="Internal").ap()
        tx, tl = (t.rearrange("(p t) d -> p t d", t=WIN) for t in (table_x, table_l))

        with ExitStack() as s1:
            def qb(name, shape, dt=F32):
                return c.sb(s1, "ata_" + name, shape, dt)

            w_qkv, w_n1 = qb("w_qkv", [128, 2, 3 * D]), qb("w_n1", [128, 2])
            w_x = qb("w_x", [128, 2, XTW + GH])
            a_row = qb("a_row", [128, 2, D])
            prod = qb("prod", [128, 2, D])
            h, hT, xt = qb("h", [P, 2, D]), qb("hT", [128, 2, 2, P]), qb("xt", [P, 2, XTW + GH])
            e, m = qb("e", [P, 2, 2 * D]), qb("m", [P, 2, 2 * D])
            k_, v_ = qb("k", [P, 2, D]), qb("v", [P, 2, 2, 129])
            (landed, order_s, ms_ready, rms_std, h_ready, turned, t_ready, products, xt_ready, v_ready, e_ready, exped,
             kq_ready, summed, sums_order) = c.sem(
                *("ata_" + n for n in ("landed", "order", "ms", "rms_std", "h_ready", "turned", "t_ready", "products", "xt_ready",
                                       "v_ready", "e_ready", "exped", "kq_ready", "summed", "sums_order")))
            stored = [c.sem(f"ata_stored{i}") for i in range(2)]
            with nc.Block() as block:
                @block.sync
                def _(sp):
                    sp.dma_start(w_qkv[:, :, :], A["L1_mix_w_qkv"].rearrange("(k p) n -> p k n", k=2)).then_inc(landed, 16)
                    sp.dma_start(w_x[:, :, 0:D], A["L1_gnn_weight"].rearrange("(k p) n -> p k n", k=2)).then_inc(landed, 16)
                    for i, n in enumerate("rl"):
                        sp.dma_start(a_row[:, i, :], row_bcast(A[f"L1_gnn_attn_{n}"].rearrange("h d -> (h d)"), 128)).then_inc(landed, 16)
                    with nc.allow_non_contiguous_dma(reason="256 floats, once"):
                        sp.dma_start(w_n1[:, :], A["L1_mix_w_norm1"].rearrange("(k p) -> p k", p=128)).then_inc(landed, 16)
                    sp.dma_start(w_out[:, :, :], A["L1_mix_w_out"].rearrange("(k p) n -> p k n", k=2)).then_inc(landed, 16)
                    sp.dma_start(b_out[:, :], A["L1_mix_b_out"].unsqueeze(0)).then_inc(landed, 16)
                    for i, n in enumerate(("src", "dst")):
                        sp.dma_start(ends[:, i, :], A[n][0:N].rearrange("(p t) -> p t", t=WIN)).then_inc(landed, 16)

                    def step(t, b):
                        sp.wait_ge(xt_ready, t + 1)
                        sp.dma_start(tx[:, t, :], xt[:, b, 0:XTW]).then_inc(stored[b], 16)
                        sp.dma_start(tl[:, t, :], xt[:, b, XTW:XTW + GH]).then_inc(stored[b], 16)
                    over_tiles(sp, step)
                    sp.wait_ge(stored[0], 32 * (WIN // 2 + 1))
                    sp.wait_ge(stored[1], 32 * (WIN // 2))

                @block.vector
                def _(dve):
                    v, order = nc.vector, Order(dve, order_s)
                    order.then(v.tensor_scalar(rms[:, :], c.fin[:, 3, :], -LN_EPS, None, ALU.add))
                    order.then(v.tensor_tensor(rms[:, :], rms[:, :], c.rstd[:, :], ALU.mult))
                    order.then(v.tensor_tensor(rms[:, :], rms[:, :], c.rstd[:, :], ALU.mult))
                    v.tensor_scalar(rms[:, :], rms[:, :], RMS_EPS, None, ALU.add).then_inc(ms_ready, 1)
                    dve.wait_ge(rms_std, 1)
                    order.then(v.reciprocal(rms[:, :], rms[:, :]))
                    order.then(v.memset(v_[:, :, :, :], 1.0))
                    order.then(v.memset(banks[6][:, :], 0.0))
                    dve.wait_ge(landed, 144)
                    for k in range(2):
                        order.then(v.tensor_scalar(w_qkv[:, k, :], w_qkv[:, k, :], w_n1[:, k:k + 1], None, ALU.mult))
                        for i in range(2):
                            order.then(v.tensor_tensor(prod[:, i, :], w_x[:, k, 0:D], a_row[:, i, :], ALU.mult))
                            order.then(v.tensor_reduce(w_x[:, k, D + GH * i:D + GH * i + GH], prod[:, i, :].rearrange("p (h d) -> p h d", h=GH), AX.X, ALU.add))
                    dve.sem_inc(sums_order, 1)

                    def make_h(t, b):
                        wait_from(dve, turned, t - 1)
                        c.normalised(h[:, b, :], t).then_inc(h_ready, 1)

                    def elu(t, b):
                        dve.wait_ge(products, t + 1)
                        wait_from(dve, kq_ready, 2 * t - 2)
                        r = col(rms, t)
                        qk = banks[4 + b][0:P, :]
                        v.tensor_scalar(e[:, b, :], qk, r, 0.0, ALU.mult, ALU.min)
                        v.tensor_scalar(m[:, b, :], qk, r, 0.0, ALU.mult, ALU.max).then_inc(e_ready, 1)
                    over_tiles(dve, elu, make_h)

                @block.gpsimd
                def _(pool):
                    def join(t, b):
                        pool.wait_ge(exped, t + 1)
                        nc.gpsimd.tensor_tensor(Q[:, t, :], e[:, b, 0:D], m[:, b, 0:D], ALU.add).then_inc(kq_ready, 1)
                        wait_from(pool, summed, t - 1)
                        nc.gpsimd.tensor_tensor(k_[:, b, :], e[:, b, D:2 * D], m[:, b, D:2 * D], ALU.add).then_inc(kq_ready, 1)
                    over_tiles(pool, join)

                @block.scalar
                def _(act):
                    act.wait_ge(ms_ready, 1)
                    nc.scalar.activation(rms[:, :], rms[:, :], ACT.Sqrt).then_inc(rms_std, 1)

                    def copy_t(t, b):
                        act.wait_ge(turned, t + 1)
                        wait_from(act, products, t - 1)
                        nc.scalar.activation(hT[:, b, :, :], banks[b][:, 0:256].rearrange("p (k n) -> p k n", k=2)[:, :, 0:P], ACT.Copy).then_inc(t_ready, 1)

                    def spread(t, b):
                        act.wait_ge(products, t + 1)
                        wait_from(act, summed, t - 1)
                        nc.scalar.activation(v_[:, b, :, 0:128], banks[b][0:P, D:2 * D].rearrange("p (a n) -> p a n", a=2), ACT.Identity, scale=col(rms, t)).then_inc(v_ready, 1)
                        if not isinstance(t, int) or t >= 2:
                            act.wait_ge(stored[b], t * 16 - 16 * b)
                        nc.scalar.activation(xt[:, b, :], banks[2 + b][0:P, 0:XTW + GH], ACT.Copy).then_inc(xt_ready, 1)
                        act.wait_ge(e_ready, t + 1)
                        nc.scalar.activation(e[:, b, :], e[:, b, :], ACT.Exp).then_inc(exped, 1)
                    over_tiles(act, spread, copy_t)

                @block.tensor
                def _(pe):
                    mm = nc.tensor.matmul

                    def head(t, b):
                        pe.wait_ge(h_ready, t + 1)
                        wait_from(pe, v_ready, t - 1)
                        for k in range(2):
                            last = nc.tensor.transpose(banks[b][:, k * 128:k * 128 + P], h[:, b, k * 128:(k + 1) * 128], c.ident[0:P, 0:P])
                        last.then_inc(turned, 1)
                        pe.wait_ge(t_ready, t + 1)
                        wait_from(pe, xt_ready, t - 1)
                        wait_from(pe, e_ready, t - 1)
                        for k in range(2):
                            mm(banks[2 + b][0:P, 0:XTW + GH], hT[:, b, k, :], w_x[:, k, :], start=(k == 0), stop=(k == 1))
                        for k in range(2):
                            mm(banks[4 + b][0:P, :], hT[:, b, k, :], w_qkv[:, k, 0:2 * D], start=(k == 0), stop=(k == 1))
                        for k in range(2):
                            last = mm(banks[b][0:P, D:2 * D], hT[:, b, k, :], w_qkv[:, k, 2 * D:3 * D], start=(k == 0), stop=(k == 1), skip_group_check=True)
                        last.then_inc(products, 1)

                    def sums(t, b):
                        pe.wait_ge(kq_ready, 2 * t + 2)
                        pe.wait_ge(v_ready, t + 1)
                        for a in range(2):
                            last = mm(banks[6][:, 129 * a:129 * a + 129], k_[:, b, a * 128:a * 128 + 128], v_[:, b, a, :], start=False, stop=False, skip_group_check=True)
                        last.then_inc(summed, 1)
                    pe.wait_ge(sums_order, 1)
                    over_tiles(pe, sums, head)

        H = sb("H", [P, WIN, D])
        with ExitStack() as s2:
            def rb(name, shape, dt=F32):
                return c.sb(s2, "atb_" + name, shape, dt)

            q, qT, z = rb("q", [P, 2, D]), rb("qT", [128, 2, 2, P]), rb("z", [P, 2, 2, 4])
            att, aT = rb("att", [P, 2, D]), rb("aT", [128, 2, 2, P])
            (kv_ready, q_ready, turned, t_ready, products, att_ready, turned2, t2_ready, products2, order_s, h_order, added, got_x, got_l) = c.sem(
                *("atb_" + n for n in ("kv_ready", "q_ready", "turned", "t_ready", "products", "att_ready", "turned2", "t2_ready", "products2",
                                       "order", "h_order", "added", "got_x", "got_l")))
            with nc.Block() as block:
                @block.gpsimd
                def _(pool):
                    def stage(t, b):
                        wait_from(pool, turned, t - 1)
                        nc.gpsimd.tensor_copy(q[:, b, :], Q[:, t, :]).then_inc(q_ready, 1)
                    over_tiles(pool, stage)
                    for t in range(WIN):
                        nc.gpsimd.indirect_dma_start(AL[:, t, :], None, table_l, bass.IndirectOffsetOnAxis(ap=ends[:, 0, t:t + 1], axis=0)).then_inc(got_l, 16)
                        nc.gpsimd.indirect_dma_start(XT[:, t, :], None, table_x, bass.IndirectOffsetOnAxis(ap=ends[:, 1, t:t + 1], axis=0)).then_inc(got_x, 16)
                    pool.wait_ge(got_l, 16 * WIN)
                    pool.wait_ge(got_x, 16 * WIN)

                @block.tensor
                def _(pe):
                    mm = nc.tensor.matmul

                    def turn(t, b):
                        pe.wait_ge(q_ready, t + 1)
                        wait_from(pe, t_ready, t - 1)
                        for k in range(2):
                            last = nc.tensor.transpose(banks[b][:, k * 128:k * 128 + P], q[:, b, k * 128:(k + 1) * 128], c.ident[0:P, 0:P])
                        last.then_inc(turned, 1)
                        pe.wait_ge(t_ready, t + 1)
                        wait_from(pe, att_ready, 2 * t - 2)
                        for a in range(2):
                            last = mm(banks[2 + b][0:P, KV * a:KV * a + KV], qT[:, b, a, :], kv[:, a, :], start=(a == 0), stop=True, skip_group_check=True)
                        last.then_inc(products, 1)

                    def out(t, b):
                        pe.wait_ge(att_ready, 2 * t + 2)
                        wait_from(pe, t2_ready, t - 1)
                        for k in range(2):
                            last = nc.tensor.transpose(banks[4 + b][:, k * 128:k * 128 + P], att[:, b, k * 128:(k + 1) * 128], c.ident[0:P, 0:P])
                        last.then_inc(turned2, 1)
                        pe.wait_ge(t2_ready, t + 1)
                        wait_from(pe, added, t - 1)
                        o = banks[6 + b][0:P, 0:D]
                        for k in range(2):
                            mm(o, aT[:, b, k, :], w_out[:, k, :], start=(k == 0), stop=False)
                        mm(o, c.ones[0:1, 0:P], b_out[:, :], start=False, stop=True).then_inc(products2, 1)
                    pe.wait_ge(kv_ready, 1)
                    over_tiles(pe, out, turn)

                @block.scalar
                def _(act):
                    def copy_q(t, b):
                        act.wait_ge(turned, t + 1)
                        wait_from(act, products, t - 1)
                        nc.scalar.activation(qT[:, b, :, :], banks[b][:, 0:256].rearrange("p (k n) -> p k n", k=2)[:, :, 0:P], ACT.Copy).then_inc(t_ready, 1)

                    def copy_a(t, b):
                        act.wait_ge(turned2, t + 1)
                        wait_from(act, products2, t - 1)
                        nc.scalar.activation(aT[:, b, :, :], banks[4 + b][:, 0:256].rearrange("p (k n) -> p k n", k=2)[:, :, 0:P], ACT.Copy).then_inc(t2_ready, 1)
                    over_tiles(act, copy_a, copy_q)

                @block.vector
                def _(dve):
                    v, order = nc.vector, Order(dve, order_s)
                    for a in range(2):
                        order.then(v.tensor_tensor(kv[:, a, 0:128], c.blocks[:, :], banks[6][:, 129 * a:129 * a + 128], ALU.mult))
                        order.then(v.tensor_scalar(kv[:, a, 128:KV], c.heads[:, :], banks[6][:, 129 * a + 128:129 * a + 129], None, ALU.mult))
                    dve.sem_inc(kv_ready, 1)
                    start = order.k

                    def divide(t, b):
                        order = Order(dve, order_s, t, 2)
                        order.start = order.start + start
                        dve.wait_ge(products, t + 1)
                        wait_from(dve, turned2, t - 1)
                        p = banks[2 + b][0:P, 0:2 * KV].rearrange("p (a n) -> p a n", a=2)
                        order.then(v.tensor_scalar(z[:, b, :, :], p[:, :, 128:KV], 1e-6, None, ALU.add))
                        order.then(v.reciprocal(z[:, b, :, :], z[:, b, :, :]))
                        for a in range(2):
                            v.tensor_tensor(att[:, b, a * 128:a * 128 + 128].rearrange("p (h e) -> p h e", e=HC), p[:, a, 0:128].rearrange("p (h e) -> p h e", e=HC),
                                            z[:, b, a, :].unsqueeze(2).to_broadcast([P, 4, HC]), ALU.mult).then_inc(att_ready, 1)

                    def add(t, b):
                        order = Order(dve, h_order, t, 1)
                        order.then(c.normalised(H[:, t, :], t))
                        dve.wait_ge(products2, t + 1)
                        v.tensor_tensor(H[:, t, :], H[:, t, :], banks[6 + b][0:P, 0:D], ALU.add).then_inc(added, 1)
                        dve.wait_ge(added, t + 1)
                        v.bn_stats(c.stats[:, t, :], H[:, t, :])
                    over_tiles(dve, add, divide)

        with ExitStack() as s3:
            def ub(name, shape, dt=F32):
                return c.sb(s3, "atc_" + name, shape, dt)

            score, peak, msg, part = ub("score", [P, WIN, GH]), ub("peak", [P, WIN]), ub("msg", [P, WIN, GD]), ub("part", [P, WIN, GD])
            rs, w_n2, g = ub("rs", [P, WIN]), ub("w_n2", [P, D]), ub("g", [P, 2, D])
            scaled = ub("scaled", [P, 2, D])
            landed, order_s, s_ready, exped, ms_ready, rooted, scaled_ready, g_ready, g_used, x_order, added, var_ready, std_ready, rs_ready = c.sem(
                *("atc_" + n for n in ("landed", "order", "s_ready", "exped", "ms", "rooted", "scaled_ready", "g_ready", "g_used", "x_order", "added", "var", "std", "rs_ready")))
            with nc.Block() as block:
                @block.sync
                def _(sp):
                    sp.dma_start(w_n2[:, :], row_bcast(A["L1_mix_w_norm2"], P)).then_inc(landed, 16)

                @block.vector
                def _(dve):
                    v, order = nc.vector, Order(dve, order_s)
                    m0, s0, m1, s1 = (c.stats[:, :, i] for i in (1, 2, 4, 5))
                    a, b_, s, _unused = (c.fin[:, i, :] for i in range(4))
                    order.then(v.tensor_tensor(a, m0, m0, ALU.mult))
                    order.then(v.tensor_tensor(b_, m1, m1, ALU.mult))
                    order.then(v.tensor_tensor(a, a, b_, ALU.add))
                    order.then(v.tensor_tensor(s, s0, s1, ALU.add))
                    order.then(v.tensor_scalar(a, a, 0.5, RMS_EPS, ALU.mult, ALU.add))
                    v.scalar_tensor_tensor(out=rs[:, :], in0=s, scalar=1.0 / D, in1=a, op0=ALU.mult, op1=ALU.add).then_inc(ms_ready, 1)
                    dve.wait_ge(rooted, 1)
                    v.reciprocal(rs[:, :], rs[:, :]).then_inc(rs_ready, 1)
                    order.then(v.tensor_tensor(score[:, :, :], AL[:, :, :], XT[:, :, GD * GH:XTW], ALU.add))
                    order.then(v.scalar_tensor_tensor(out=score[:, :, :], in0=score[:, :, :], scalar=0.01, in1=score[:, :, :], op0=ALU.mult, op1=ALU.max))
                    order.then(v.tensor_reduce(peak[:, :], score[:, :, :], AX.X, ALU.max))
                    v.tensor_tensor(score[:, :, :], score[:, :, :], peak[:, :].unsqueeze(2).to_broadcast([P, WIN, GH]), ALU.subtract).then_inc(s_ready, 1)
                    dve.wait_ge(exped, 1)
                    order.then(v.tensor_reduce(peak[:, :], score[:, :, :], AX.X, ALU.add))
                    order.then(v.reciprocal(peak[:, :], peak[:, :]))
                    order.then(v.tensor_tensor(score[:, :, :], score[:, :, :], peak[:, :].unsqueeze(2).to_broadcast([P, WIN, GH]), ALU.mult))
                    for h in range(GH):
                        out = msg if h == 0 else part
                        order.then(v.tensor_tensor(out[:, :, :], XT[:, :, h * GD:(h + 1) * GD], score[:, :, h:h + 1].to_broadcast([P, WIN, GD]), ALU.mult))
                        if h:
                            order.then(v.tensor_tensor(msg[:, :, :], msg[:, :, :], part[:, :, :], ALU.add))

                    def add(t, b):
                        order = Order(dve, x_order, t, 3)
                        x = c.X[:, t, :]
                        order.then(v.tensor_tensor(x, x, H[:, t, :], ALU.add))
                        order.then(v.tensor_tensor(x.rearrange("p (h d) -> p h d", h=GH), x.rearrange("p (h d) -> p h d", h=GH),
                                                   msg[:, t, :].unsqueeze(1).to_broadcast([P, GH, GD]), ALU.add))
                        dve.wait_ge(g_ready, t + 1)
                        order.then(v.tensor_tensor(x, x, g[:, b, :], ALU.add))
                        v.bn_stats(c.stats[:, t, :], x).then_inc(added, 1)
                    over_tiles(dve, add)
                    dve.wait_ge(added, WIN)
                    c.finish_stats(order, var_ready, std_ready)

                @block.gpsimd
                def _(pool):
                    def scale(t, b):
                        pool.wait_ge(scaled_ready, t + 1)
                        wait_from(pool, added, t - 1)
                        nc.gpsimd.tensor_tensor(g[:, b, :], scaled[:, b, :], w_n2[:, :], ALU.mult).then_inc(g_ready, 1)
                    pool.wait_ge(landed, 16)
                    over_tiles(pool, scale)

                @block.scalar
                def _(act):
                    act.wait_ge(ms_ready, 1)
                    nc.scalar.activation(rs[:, :], rs[:, :], ACT.Sqrt).then_inc(rooted, 1)
                    act.wait_ge(s_ready, 1)
                    nc.scalar.activation(score[:, :, :], score[:, :, :], ACT.Exp).then_inc(exped, 1)

                    def scale(t, b):
                        wait_from(act, g_ready, t - 1)
                        nc.scalar.activation(scaled[:, b, :], H[:, t, :], ACT.Copy, scale=col(rs, t)).then_inc(scaled_ready, 1)
                    act.wait_ge(rs_ready, 1)
                    over_tiles(act, scale)
                    c.root(act, var_ready, std_ready)


def router(c, scope, XN, WF):
    nc, A, banks = c.nc, c.A, c.banks
    with ExitStack() as s1:
        def sb(name, shape, dt=F32):
            return c.sb(s1, "ro_" + name, shape, dt)

        h, xT = sb("h", [P, 2, D]), sb("xT", [128, 2, 2, P])
        affine = sb("affine", [128, 2, 2])
        w_r, b_r = sb("w_r", [128, 2, EXPERTS]), sb("b_r", [1, EXPERTS])
        logit, top, index = sb("logit", [P, 2, EXPERTS]), sb("top", [P, 2, 8]), sb("index", [P, 2, 8], U32)
        tops, picks = sb("tops", [P, WIN, 2]), sb("picks", [P, WIN, 2])
        w1, w2, part = sb("w1", [P, WIN]), sb("w2", [P, WIN]), sb("part", [P, WIN, EXPERTS])
        (landed, order_s, h_ready, turned, t_ready, kept, logits, late_s, gap_ready, exped, passed) = c.sem(
            *("ro_" + n for n in ("landed", "order", "h_ready", "turned", "t_ready", "kept", "logits", "late", "gap", "exped", "passed")))
        with nc.Block() as block:
            @block.sync
            def _(sp):
                with nc.allow_non_contiguous_dma(reason="512 floats, once"):
                    for i, n in enumerate(("L1_ffn_gamma", "L1_ffn_beta")):
                        sp.dma_start(affine[:, i, :], A[n].rearrange("(k p) -> p k", p=128)).then_inc(landed, 16)
                sp.dma_start(w_r[:, :, :], A["L1_ffn_Wr"].rearrange("(k p) n -> p k n", k=2)).then_inc(landed, 16)
                sp.dma_start(b_r[:, :], A["L1_ffn_br"].unsqueeze(0)).then_inc(landed, 16)

            @block.vector
            def _(dve):
                v = nc.vector

                def make_h(t, b):
                    wait_from(dve, turned, t - 1)
                    c.normalised(h[:, b, :], t).then_inc(h_ready, 1)

                def best(t, b):
                    order = Order(dve, order_s, t, 5)
                    dve.wait_ge(logits, t + 1)
                    order.then(v.tensor_copy(logit[:, b, :], banks[2 + b][0:P, 0:EXPERTS]))
                    dve.sem_inc(passed, 1)
                    order.then(v.max(top[:, b, :], logit[:, b, :]))
                    dve.sem_inc(passed, 1)
                    order.then(v.max_index(index[:, b, :], top[:, b, :], logit[:, b, :]))
                    order.then(v.tensor_scalar(tops[:, t, :], top[:, b, 0:2], 1.0, None, ALU.mult))
                    order.then(v.tensor_scalar(picks[:, t, :], index[:, b, 0:2], 1.0, None, ALU.mult))
                over_tiles(dve, best, make_h)
                order = Order(dve, late_s)
                v.tensor_tensor(w1[:, :], tops[:, :, 1], tops[:, :, 0], ALU.subtract).then_inc(gap_ready, 1)
                dve.wait_ge(exped, 1)
                order.then(v.tensor_scalar(w1[:, :], w2[:, :], 1.0, None, ALU.add))
                order.then(v.reciprocal(w1[:, :], w1[:, :]))
                order.then(v.tensor_tensor(w2[:, :], w2[:, :], w1[:, :], ALU.mult))
                shape = [P, WIN, EXPERTS]
                for i, w in enumerate((w1, w2)):
                    o = (WF, part)[i][:, :, :]
                    order.then(v.tensor_tensor(o, c.iota_f[0:P, 0:EXPERTS].unsqueeze(1).to_broadcast(shape), picks[:, :, i:i + 1].to_broadcast(shape), ALU.is_equal))
                    order.then(v.tensor_tensor(o, o, w[:, :].unsqueeze(2).to_broadcast(shape), ALU.mult))
                order.then(v.tensor_tensor(WF[:, :, :], WF[:, :, :], part[:, :, :], ALU.add))

            @block.gpsimd
            def _(pool):
                def keep(t, b):
                    pool.wait_ge(t_ready, 2 * t + 2)
                    nc.gpsimd.tensor_copy(XN[:, :, bass.ds(t * P, P)], xT[:, b, :, :]).then_inc(kept, 1)
                over_tiles(pool, keep)

            @block.scalar
            def _(act):
                def copy_t(t, b):
                    act.wait_ge(turned, t + 1)
                    wait_from(act, logits, t - 1)
                    wait_from(act, kept, t - 1)
                    for k in range(2):
                        nc.scalar.activation(xT[:, b, k, :], banks[b][:, k * 128:k * 128 + P], ACT.Identity,
                                             bias=affine[:, 1, k:k + 1], scale=affine[:, 0, k:k + 1]).then_inc(t_ready, 1)
                act.wait_ge(landed, 64)
                over_tiles(act, copy_t)
                act.wait_ge(gap_ready, 1)
                nc.scalar.activation(w2[:, :], w1[:, :], ACT.Exp).then_inc(exped, 1)

            @block.tensor
            def _(pe):
                def turn(t, b):
                    pe.wait_ge(h_ready, t + 1)
                    wait_from(pe, t_ready, 2 * t - 2)
                    for k in range(2):
                        last = nc.tensor.transpose(banks[b][:, k * 128:k * 128 + P], h[:, b, k * 128:(k + 1) * 128], c.ident[0:P, 0:P])
                    last.then_inc(turned, 1)

                def route(t, b):
                    pe.wait_ge(t_ready, 2 * t + 2)
                    wait_from(pe, order_s, 5 * t - 9)
                    o = banks[2 + b][0:P, 0:EXPERTS]
                    for k in range(2):
                        nc.tensor.matmul(o, xT[:, b, k, :], w_r[:, k, :], start=(k == 0), stop=False)
                    nc.tensor.matmul(o, c.ones[0:1, 0:P], b_r[:, :], start=False, stop=True).then_inc(logits, 1)
                pe.wait_ge(landed, 64)
                over_tiles(pe, route, turn)


def expert_stage(c):
    nc, A, banks = c.nc, c.A, c.banks
    KH = HID // 128
    with ExitStack() as scope:
        def sb(name, shape, dt=F32):
            return c.sb(scope, "ex_" + name, shape, dt)

        XN, WF = sb("XN", [128, 2, N]), sb("WF", [P, WIN, EXPERTS])
        router(c, scope, XN, WF)
        w1, w2 = sb("w1", [128, EXPERTS, 2, HID]), sb("w2", [128, EXPERTS, KH, D])
        b1 = sb("b1", [128, EXPERTS, KH])
        b2 = sb("b2", [1, EXPERTS, D])
        hid = sb("hid", [128, 2, KH, GROUP * P])
        landed, up, hid_ready, down, added, stored = c.sem(*("ex_" + n for n in ("landed", "up", "hid_ready", "down", "added", "stored")))
        GROUPS, REST = WIN // GROUP, WIN % GROUP

        def over_groups(engine, step):
            step(0, GROUP, 0)
            with engine.Fori(1, GROUPS) as i:
                step(i, GROUP, 0)
            step(GROUPS, REST, 0)

        with nc.Block() as block:
            @block.sync
            def _(sp):
                for e in range(EXPERTS):
                    sp.dma_start(w1[:, e, :, :], A["L1_ffn_W1"][e].rearrange("(k p) n -> p k n", k=2)).then_inc(landed, 16)
                    sp.dma_start(w2[:, e, :, :], A["L1_ffn_W2"][e].rearrange("(k p) n -> p k n", k=KH)).then_inc(landed, 16)
                with nc.allow_non_contiguous_dma(reason="4096 floats, once"):
                    for e in range(EXPERTS):
                        sp.dma_start(b1[:, e, :], A["L1_ffn_b1"][e].rearrange("(k p) -> p k", p=128)).then_inc(landed, 16)
                sp.dma_start(b2[:, :, :], A["L1_ffn_b2"].unsqueeze(0)).then_inc(landed, 16)
                sp.wait_ge(added, WIN * EXPERTS)
                sp.dma_start(c.out.rearrange("(p t) d -> p t d", t=WIN), c.X[:, :, :]).then_inc(stored, 16)
                sp.wait_ge(stored, 16)

            @block.tensor
            def _(pe):
                mm = nc.tensor.matmul
                pe.wait_ge(landed, 16 * (3 * EXPERTS + 1))

                def step(g, tiles, _b):
                    n, n0, d0 = tiles * P, g * (EXPERTS * KH), g * (EXPERTS * GROUP)

                    def ups(e):
                        for k in range(KH):
                            i = e * KH + k
                            wait_from(pe, hid_ready, n0 + i - 1)
                            for q in range(2):
                                last = mm(banks[i % 2][:, 0:n], w1[:, e, q, k * 128:(k + 1) * 128], XN[:, q, bass.ds(g * GROUP * P, n)], start=(q == 0), stop=(q == 1))
                            last.then_inc(up, 1)

                    def downs(e):
                        pe.wait_ge(hid_ready, n0 + (e + 1) * KH)
                        for t in range(tiles):
                            i = e * tiles + t
                            wait_from(pe, added, d0 + i - 3)
                            o = banks[4 + i % 4][0:P, 0:D]
                            for k in range(KH):
                                mm(o, hid[:, e % 2, k, t * P:(t + 1) * P], w2[:, e, k, :], start=(k == 0), stop=False)
                            mm(o, c.ones[0:1, 0:P], b2[:, e, :], start=False, stop=True).then_inc(down, 1)
                    ups(0)
                    for e in range(EXPERTS):
                        if e + 1 < EXPERTS:
                            ups(e + 1)
                        downs(e)
                over_groups(pe, step)

            @block.scalar
            def _(act):
                act.wait_ge(landed, 16 * (3 * EXPERTS + 1))

                def step(g, tiles, _b):
                    n, n0, d0 = tiles * P, g * (EXPERTS * KH), g * (EXPERTS * GROUP)
                    for e in range(EXPERTS):
                        wait_from(act, down, d0 + (e - 1) * tiles if e >= 2 or not isinstance(g, int) or g > 0 else 0)
                        for k in range(KH):
                            i = e * KH + k
                            act.wait_ge(up, n0 + i + 1)
                            nc.scalar.activation(hid[:, e % 2, k, 0:n], banks[i % 2][:, 0:n], ACT.Gelu, bias=b1[:, e, k:k + 1]).then_inc(hid_ready, 1)
                over_groups(act, step)

            @block.vector
            def _(dve):
                def step(g, tiles, _b):
                    d0 = g * (EXPERTS * GROUP)
                    for e in range(EXPERTS):
                        for t in range(tiles):
                            i = e * tiles + t
                            x = c.X[:, bass.ds(g * GROUP + t, 1), :].rearrange("p o d -> p (o d)")
                            w = WF[:, bass.ds(g * GROUP + t, 1), e:e + 1].rearrange("p o e -> p (o e)")
                            dve.wait_ge(down, d0 + i + 1)
                            if e:
                                dve.wait_ge(added, d0 + i + 1 - tiles)
                            nc.vector.scalar_tensor_tensor(out=x, in0=banks[4 + i % 4][0:P, 0:D], scalar=w, in1=x, op0=ALU.mult, op1=ALU.add).then_inc(added, 1)
                over_groups(dve, step)


def build(nc, A, out):
    with ExitStack() as keep:
        c = Chip(nc, A, out, keep)
        table_y = nc.dram_tensor("table_y", [RELS * N, D], F32, kind="Internal").ap()
        load_stage(c)
        with ExitStack() as graph:
            mixer = c.sb(graph, "mixer", [128, 2, D // 2])
            mix0_stage(c, mixer)
            slot_row = c.sb(graph, "slot_row", [128, TILES], I32)
            slot_dst = c.sb(graph, "slot_dst", [128, TILES])
            slot_win = c.sb(graph, "slot_win", [1, TILES], I32)
            sort_stage(c, slot_row, slot_dst, slot_win)
            aggr, selfp = c.sb(graph, "aggr", [P, WIN, D]), c.sb(graph, "selfp", [P, WIN, D])
            for layer in range(LAYERS):
                message_stage(c, layer, aggr, selfp, mixer, table_y)
                gather_stage(c, layer, aggr, table_y, slot_row, slot_dst, slot_win)
            gnn_out_stage(c, aggr, selfp)
        c.recycle()
        slice_stage(c)
        c.recycle()
        attention_stage(c)
        expert_stage(c)


def constants():
    import numpy as np
    head = np.arange(128) // HC
    return {
        "c_ident": np.eye(128, dtype=np.float32),
        "c_tri": np.triu(np.ones((128, 128), np.float32), 1),
        "c_iota": np.tile(np.arange(TILES, dtype=np.float16), (128, 1)),
        "c_iota_f": np.tile(np.arange(128, dtype=np.float32), (128, 1)),
        "c_blocks": (head[:, None] == head[None, :]).astype(np.float32),
        "c_heads": (head[:, None] == np.arange(4)[None, :]).astype(np.float32),
    }


def kernel(**inputs):
    import numpy as np
    import concourse.bacc as bacc
    from concourse.bass_utils import run_bass_kernel_spmd

    nc = bacc.Bacc("TRN2", target_bir_lowering=False, num_devices=1)
    arrays, handles = {}, {}
    for name, a in {**inputs, **constants()}.items():
        a = np.ascontiguousarray(a)
        arrays[f"in_{name}"] = a
        handles[name] = nc.dram_tensor(f"in_{name}", a.shape, mybir.dt.from_np(a.dtype), kind="ExternalInput").ap()
    out = nc.dram_tensor("out_0", (N, D), F32, kind="ExternalOutput").ap()
    build(nc, handles, out)
    return run_bass_kernel_spmd(nc, [arrays], core_ids=[0]).results[0]["out_0"]
```

```python
from contextlib import ExitStack

import concourse.bass as bass
from concourse import mybir

ALU = mybir.AluOpType
ACT = mybir.ActivationFunctionType
AX = mybir.AxisListType
F32 = mybir.dt.float32
F16 = mybir.dt.float16
I32 = mybir.dt.int32
U32 = mybir.dt.uint32

N = 3125
D = 256
E = 50000
WIN = 25
P = N // WIN
RELS = 2
LAYERS = 3
EC = E // P
SLOT = 128
TILES = (E + WIN * (SLOT - 1)) // SLOT
RING = 16
HALF = RING // 2
QUAD = 4
TILES += -TILES % RING
HEADS = 8
HC = D // HEADS
SD = 64
INNER = HEADS * SD
GH, GD = 4, 64
EXPERTS, HID = 8, 512
PICKS = 2
TOKEN_TILES = (PICKS * N + EXPERTS * (SLOT - 1)) // SLOT
TOKEN_TILES += TOKEN_TILES % 2
LN_EPS = 1e-5
ZEROS = 1024
RMS_EPS = 1e-6
ROUND = 1.5 * 2 ** 23


class Order:

    def __init__(self, engine, semaphore, tile=0, per=0):
        self.engine, self.semaphore, self.start, self.per, self.k = engine, semaphore, tile * per, per, 0

    def then(self, instruction):
        instruction.then_inc(self.semaphore, 1)
        self.k += 1
        self.engine.wait_ge(self.semaphore, self.start + self.k)

    def close(self):
        assert self.k == self.per, (self.k, self.per)


def wait_from(engine, semaphore, value):
    if isinstance(value, int) and value <= 0:
        return
    engine.wait_ge(semaphore, value)


def over_tiles(engine, *steps, count=WIN):
    steps = [s if isinstance(s, tuple) else (s, 0) for s in steps]
    most = max(lead for _, lead in steps)

    def round_(t, b, python):
        for step, lead in steps:
            if not python or 0 <= t + lead < count:
                step(t + lead, (b + lead) % 2)

    for t in range(-most, 2):
        round_(t, t % 2, True)
    pairs = (count - most - 2) // 2
    with engine.Fori(2, 2 + 2 * pairs - 1, 2) as i:
        round_(i, 0, False)
        round_(i + 1, 1, False)
    for t in range(2 + 2 * pairs, count):
        round_(t, t % 2, True)


def col(ap, t):
    return ap[:, bass.ds(t, 1)]


class Chip:

    def __init__(self, nc, A, out, keep):
        self.nc, self.A, self.out, self.keep = nc, A, out, keep
        self.X = self.sb(keep, "X", [P, WIN, D])
        self.ident = self.sb(keep, "ident", [128, 128])
        self.tri = self.sb(keep, "tri", [128, 128])
        self.ones = self.sb(keep, "ones", [128, 128])
        self.zeros = self.sb(keep, "zeros", [128, ZEROS])
        self.iota = self.sb(keep, "iota", [128, TILES], F16)
        self.iota_f = self.sb(keep, "iota_f", [128, 128])
        self.blocks = self.sb(keep, "blocks", [128, 128])
        self.heads = self.sb(keep, "heads", [128, 4])
        self.rstd = self.sb(keep, "rstd", [P, WIN])
        self.nmr = self.sb(keep, "nmr", [P, WIN])
        self.stats = self.sb(keep, "stats", [P, WIN, 6])
        self.fin = self.sb(keep, "fin", [P, 4, WIN])
        self.banks = [keep.enter_context(nc.psum_tensor(f"bank{i}", [128, 512], F32)) for i in range(8)]
        self.sems = []

    def sb(self, scope, name, shape, dt=F32):
        return scope.enter_context(self.nc.sbuf_tensor(name, shape, dt))

    def sem(self, *names):
        got = [self.nc.alloc_semaphore(name=n) for n in names]
        self.sems += got
        return got[0] if len(got) == 1 else got

    def recycle(self):
        self.nc.clear_and_free_semaphores(self.sems)
        self.nc.all_engine_barrier()
        self.sems = []

    def normalised(self, out, t):
        return self.nc.vector.tensor_scalar(out, self.X[:, t, :], col(self.rstd, t), col(self.nmr, t), ALU.mult, ALU.add)

    def finish_stats(self, order, var_ready, std_ready, base=0):
        v, fin = self.nc.vector, self.fin
        m0, s0, m1, s1 = (self.stats[:, :, i] for i in (1, 2, 4, 5))
        mean2, d, s, var = (fin[:, i, :] for i in range(4))
        order.then(v.tensor_tensor(mean2, m0, m1, ALU.add))
        order.then(v.tensor_tensor(d, m0, m1, ALU.subtract))
        order.then(v.tensor_tensor(s, s0, s1, ALU.add))
        order.then(v.tensor_tensor(d, d, d, ALU.mult))
        order.then(v.tensor_scalar(d, d, 0.25, LN_EPS, ALU.mult, ALU.add))
        order.then(v.scalar_tensor_tensor(out=var, in0=s, scalar=1.0 / D, in1=d, op0=ALU.mult, op1=ALU.add))
        v.tensor_scalar(mean2, mean2, -0.5, None, ALU.mult).then_inc(var_ready, 1)
        order.engine.wait_ge(std_ready, 1)
        order.then(v.reciprocal(self.rstd[:, :], self.rstd[:, :]))
        order.engine.wait_ge(var_ready, 1)
        order.then(v.tensor_tensor(self.nmr[:, :], mean2, self.rstd[:, :], ALU.mult))

    def root(self, act, var_ready, std_ready):
        act.wait_ge(var_ready, 1)
        self.nc.scalar.activation(self.rstd[:, :], self.fin[:, 3, :], ACT.Sqrt).then_inc(std_ready, 1)


def tile_stats(c, dve, order, source):
    start, group = order.k, 5
    with dve.Fori(0, WIN - group + 1, group) as t:
        for i in range(group):
            c.nc.vector.bn_stats(c.stats[:, t + i, :], source[:, t + i, :]).then_inc(order.semaphore, 1)
    order.k = start + WIN
    dve.wait_ge(order.semaphore, order.start + order.k)


def row_bcast(vector, rows):
    return vector.unsqueeze(0).to_broadcast([rows, vector.shape[0]])


def load_stage(c, table_xs):
    nc, A = c.nc, c.A
    x_landed, landed, order_s, var_ready, std_ready, zeroed = c.sem("x_landed", "consts_landed", "load_order", "load_var", "load_std", "load_zeroed")
    c.filled = c.sem("table_filled")
    with nc.Block() as block:
        @block.gpsimd
        def _(pool):
            pool.dma_start(c.X[:, :, :], A["x"].rearrange("(p t) d -> p t d", t=WIN)).then_inc(x_landed, 16)

        @block.sync
        def _(sp):
            pairs = [(c.ident, "c_ident"), (c.tri, "c_tri"), (c.iota, "c_iota"), (c.iota_f, "c_iota_f"),
                     (c.blocks, "c_blocks"), (c.heads, "c_heads")]
            for buffer, name in pairs:
                sp.dma_start(buffer[:, :], A[name]).then_inc(landed, 16)
            sp.wait_ge(landed, 16 * len(pairs))
            sp.wait_ge(zeroed, 1)
            rows = table_xs.rearrange("(p j) d -> p (j d)", p=128)
            width = rows.shape[1] // ZEROS
            sp.dma_start(rows.rearrange("p (z w) -> p z w", w=ZEROS), c.zeros[:, :].unsqueeze(1).to_broadcast([128, width, ZEROS])).then_inc(c.filled, 16)

        @block.vector
        def _(dve):
            nc.vector.memset(c.ones[:, :], 1.0)
            nc.vector.memset(c.zeros[:, :], 0.0).then_inc(zeroed, 1)
            dve.wait_ge(x_landed, 16)
            order = Order(dve, order_s)
            tile_stats(c, dve, order, c.X)
            c.finish_stats(order, var_ready, std_ready)

        @block.scalar
        def _(act):
            c.root(act, var_ready, std_ready)


def mix0_stage(c, mixer):
    nc, A = c.nc, c.A
    with ExitStack() as scope:
        def sb(*a):
            return c.sb(scope, *a)

        xn, xc, sq = sb("mx_xn", [P, WIN, D]), sb("mx_xc", [P, WIN, D]), sb("mx_sq", [P, WIN, D])
        neg_mean, rz = sb("mx_neg_mean", [P, WIN * HEADS]), sb("mx_rz", [P, WIN * HEADS])
        z = sb("mx_z", [P, 2, 2, 129])
        kcol = sb("mx_kcol", [128, 2, 2])
        vrow = sb("mx_vrow", [128, 2, D])
        u = sb("mx_u", [128, 2])
        srow = sb("mx_srow", [128, D])
        landed, order_s, xc_ready, sq_ready, ss_ready, std_ready, z_ready, z_used, zeroed, g_ready = c.sem(
            *("mx_" + n for n in ("landed", "order", "xc_ready", "sq_ready", "ss_ready", "std_ready", "z_ready", "z_used", "zeroed", "g_ready")))
        heads = "p t (h e) -> p (t h) e"
        xn_h, xc_h, sq_h = (b[:, :, :].rearrange(heads, h=HEADS) for b in (xn, xc, sq))
        with nc.Block() as block:
            @block.sync
            def _(sp):
                with nc.allow_non_contiguous_dma(reason="512 floats, once"):
                    for i, n in enumerate(("L0_mix_kln_weight", "L0_mix_kln_bias")):
                        sp.dma_start(kcol[:, :, i], A[n].rearrange("(a h) o e -> (h o e) a", a=2)).then_inc(landed, 16)
                for i, n in enumerate(("L0_mix_vln_weight", "L0_mix_vln_bias")):
                    sp.dma_start(vrow[:, i, :], row_bcast(A[n].rearrange("h o e -> (h o e)"), 128)).then_inc(landed, 16)
                sp.wait_ge(c.filled, 16)

            @block.vector
            def _(dve):
                v = nc.vector
                v.memset(c.banks[0][:, :], 0.0).then_inc(zeroed, 1)
                v.memset(c.banks[1][:, :], 0.0).then_inc(zeroed, 1)
                v.memset(z[:, :, :, :], 1.0).then_inc(zeroed, 1)
                with dve.Fori(0, WIN) as t:
                    c.normalised(xn[:, t, :], t).then_inc(order_s, 1)
                dve.wait_ge(order_s, WIN)
                order = Order(dve, order_s)
                order.k = WIN
                order.then(v.tensor_reduce(neg_mean[:, :], xn_h, AX.X, ALU.add))
                order.then(v.tensor_scalar(neg_mean[:, :], neg_mean[:, :], -1.0 / HC, None, ALU.mult))
                v.tensor_tensor(xc_h, xn_h, neg_mean[:, :].unsqueeze(2).to_broadcast([P, WIN * HEADS, HC]), ALU.add).then_inc(xc_ready, 1)
                dve.wait_ge(sq_ready, 1)
                order.then(v.tensor_reduce(rz[:, :], sq_h, AX.X, ALU.add))
                v.tensor_scalar(rz[:, :], rz[:, :], 1.0 / (HC - 1), None, ALU.mult).then_inc(ss_ready, 1)
                dve.wait_ge(std_ready, 1)
                order.then(v.tensor_scalar(rz[:, :], rz[:, :], LN_EPS, None, ALU.add))
                order.then(v.reciprocal(rz[:, :], rz[:, :]))
                dve.wait_ge(zeroed, 3)

                def step(t, b):
                    wait_from(dve, z_used, t - 1)
                    for k in range(2):
                        last = v.tensor_tensor(z[:, b, k, 0:128].rearrange("p (h e) -> p h e", e=HC),
                                               xc[:, t, k * 128:(k + 1) * 128].rearrange("p (h e) -> p h e", e=HC),
                                               rz[:, bass.ds(t * HEADS + 4 * k, 4)].unsqueeze(2).to_broadcast([P, 4, HC]), ALU.mult)
                        last.then_inc(z_ready, 1)
                over_tiles(dve, step)
                dve.wait_ge(g_ready, 1)
                dve.wait_ge(landed, 64)
                order.then(v.tensor_copy(srow[:, :], c.banks[1][:, 0:D]))
                for k in range(2):
                    gram, s_col = c.banks[0][:, 129 * k:129 * k + 128], c.banks[0][:, 129 * k + 128:129 * k + 129]
                    m, cols = mixer[:, k, :], slice(128 * k, 128 * k + 128)
                    kw, kb = kcol[:, k, 0:1], kcol[:, k, 1:2]
                    order.then(v.tensor_scalar(m, srow[:, cols], kb, None, ALU.mult))
                    order.then(v.scalar_tensor_tensor(out=m, in0=gram, scalar=kw, in1=m, op0=ALU.mult, op1=ALU.add))
                    order.then(v.tensor_tensor(m, m, vrow[:, 0, cols], ALU.mult))
                    order.then(v.tensor_scalar(u[:, 0:1], s_col, kw, None, ALU.mult))
                    order.then(v.scalar_tensor_tensor(out=u[:, 1:2], in0=kb, scalar=float(N), in1=u[:, 0:1], op0=ALU.mult, op1=ALU.add))
                    order.then(v.scalar_tensor_tensor(out=m, in0=vrow[:, 1, cols], scalar=u[:, 1:2], in1=m, op0=ALU.mult, op1=ALU.add))
                    order.then(v.scalar_tensor_tensor(out=m, in0=m, scalar=1.0 / N, in1=c.blocks[:, :], op0=ALU.mult, op1=ALU.mult))

            @block.scalar
            def _(act):
                act.wait_ge(xc_ready, 1)
                nc.scalar.activation(sq[:, :, :], xc[:, :, :], ACT.Square).then_inc(sq_ready, 1)
                act.wait_ge(ss_ready, 1)
                nc.scalar.activation(rz[:, :], rz[:, :], ACT.Sqrt).then_inc(std_ready, 1)

            @block.tensor
            def _(pe):
                pe.wait_ge(zeroed, 3)

                def step(t, b):
                    pe.wait_ge(z_ready, 2 * t + 2)
                    for k in range(2):
                        zk = z[:, b, k, :]
                        nc.tensor.matmul(c.banks[0][:, 129 * k:129 * k + 129], zk[:, 0:128], zk, start=False, stop=False, skip_group_check=True)
                        last = nc.tensor.matmul(c.banks[1][:, 128 * k:128 * k + 128], c.ones[0:P, :], zk[:, 0:128], start=False, stop=False, skip_group_check=True)
                    last.then_inc(z_used, 1)
                over_tiles(pe, step)
                pe.wait_ge(z_used, WIN)
                pe.sem_inc(g_ready, 1)


def sort_stage(c, slot_row, slot_dst, slot_win):
    nc, A = c.nc, c.A
    with ExitStack() as scope:
        def sb(name, shape, dt=F32):
            return c.sb(scope, "so_" + name, shape, dt)

        masks = sb("masks", [P, WIN, EC], F16)
        raw = sb("raw", [P, 3, EC], I32)
        win, row, rank, code_hi, code_lo, tmp, tile_of, row_of, zero = (
            sb(n, [P, EC])[:, :] for n in ("win", "row", "rank", "code_hi", "code_lo", "tmp", "tile_of", "row_of", "zero"))
        scan, ones = sb("scan", [P, WIN, EC]), sb("ones", [P, 1])
        counts, ntile, base = sb("counts", [P, WIN]), sb("ntile", [P, WIN]), sb("base", [P, WIN])
        cum, own = sb("cum", [P, WIN + 1]), sb("own", [1, TILES])
        landed, order_s, counted, summed, ranked = c.sem("so_landed", "so_order", "so_counted", "so_summed", "so_ranked")
        with nc.Block() as block:
            @block.sync
            def _(sp):
                for i, n in enumerate(("dst", "src", "edge_type_2")):
                    sp.dma_start(raw[:, i, :], A[n].rearrange("(p j) -> p j", j=EC)).then_inc(landed, 16)

            @block.vector
            def _(dve):
                v, order = nc.vector, Order(dve, order_s)
                order.then(v.memset(zero, 0.0))
                order.then(v.memset(ones[:, :], 1.0))
                dve.wait_ge(landed, 48)
                order.then(v.tensor_copy(rank, raw[:, 0, :]))
                order.then(v.tensor_scalar(tmp, rank, 1.0 / WIN, -(WIN - 1) / 2 / WIN, ALU.mult, ALU.add))
                order.then(v.tensor_scalar(row, tmp, ROUND, ROUND, ALU.add, ALU.subtract))
                order.then(v.scalar_tensor_tensor(out=win, in0=row, scalar=-float(WIN), in1=rank, op0=ALU.mult, op1=ALU.add))
                order.then(v.tensor_copy(code_lo, raw[:, 1, :]))
                order.then(v.tensor_copy(tmp, raw[:, 2, :]))
                order.then(v.tensor_scalar(tmp, tmp, 0.0, float(N), ALU.not_equal, ALU.mult))
                order.then(v.tensor_tensor(code_lo, code_lo, tmp, ALU.add))
                order.then(v.tensor_scalar(tmp, code_lo, 1.0 / 8, -3.5 / 8, ALU.mult, ALU.add))
                order.then(v.tensor_scalar(code_hi, tmp, ROUND, ROUND, ALU.add, ALU.subtract))
                order.then(v.scalar_tensor_tensor(out=code_lo, in0=code_hi, scalar=-8.0, in1=code_lo, op0=ALU.mult, op1=ALU.add))
                order.then(v.tensor_scalar(code_lo, code_lo, 128.0, 1.0, ALU.mult, ALU.add))
                order.then(v.tensor_tensor(code_lo, code_lo, row, ALU.add))
                for w in range(WIN):
                    v.tensor_scalar(masks[:, w, :], win, float(w), 0.0, ALU.is_equal, ALU.add,
                                    accum_out=counts[:, w:w + 1]).then_inc(counted, 1)
                dve.wait_ge(counted, WIN)
                dve.wait_ge(summed, 1)
                totals, before = c.banks[0][0:P, 0:WIN], c.banks[1][0:P, 0:WIN]
                order.then(v.tensor_scalar(ntile[:, :], totals, 1.0 / SLOT, (SLOT / 2 - 0.5) / SLOT, ALU.mult, ALU.add))
                order.then(v.tensor_scalar(ntile[:, :], ntile[:, :], ROUND, ROUND, ALU.add, ALU.subtract))
                order.then(v.memset(cum[:, 0:1], 0.0))
                order.then(v.tensor_tensor_scan(cum[:, 1:WIN + 1], ntile[:, :], zero[:, 0:WIN], 0.0, ALU.add, ALU.add))
                order.then(v.scalar_tensor_tensor(out=base[:, :], in0=cum[:, 0:WIN], scalar=float(SLOT), in1=before, op0=ALU.mult, op1=ALU.add))
                flat = "p w e -> p (w e)"
                order.then(v.tensor_tensor_scan(scan[:, :, :].rearrange(flat), masks[:, :, :].rearrange(flat), ones[:, 0:1].to_broadcast([P, WIN * EC]),
                                                0.0, ALU.add, ALU.mult))
                order.then(v.tensor_scalar(base[:, :], base[:, :], -1.0, None, ALU.add))
                order.then(v.tensor_tensor(base[:, 1:WIN], base[:, 1:WIN], scan[:, 0:WIN - 1, EC - 1], ALU.subtract))
                for w in range(WIN):
                    v.scalar_tensor_tensor(out=scan[:, w, :], in0=scan[:, w, :], scalar=base[:, w:w + 1], in1=masks[:, w, :], op0=ALU.add, op1=ALU.mult).then_inc(ranked, 1)
                dve.wait_ge(ranked, WIN)
                order.then(v.tensor_reduce(rank, scan[:, :, :].rearrange("p w e -> p e w"), AX.X, ALU.add))
                order.then(v.tensor_scalar(tmp, rank, 1.0 / SLOT, -(SLOT - 1) / 2 / SLOT, ALU.mult, ALU.add))
                order.then(v.tensor_scalar(tile_of, tmp, ROUND, ROUND, ALU.add, ALU.subtract))
                order.then(v.scalar_tensor_tensor(out=row_of, in0=tile_of, scalar=-float(SLOT), in1=rank, op0=ALU.mult, op1=ALU.add))
                order.then(v.memset(own[:, :], 0.0))
                for w in range(WIN - 1):
                    order.then(v.scalar_tensor_tensor(out=own[:, :], in0=c.iota[0:1, :], scalar=cum[0:1, w + 1:w + 2], in1=own[:, :], op0=ALU.is_ge, op1=ALU.add))
                order.then(v.tensor_copy(slot_win[:, :], own[:, :]))

            @block.tensor
            def _(pe):
                pe.wait_ge(counted, WIN)
                nc.tensor.matmul(c.banks[0][0:P, 0:WIN], c.ones[0:P, 0:P], counts[:, :], start=True, stop=True)
                nc.tensor.matmul(c.banks[1][0:P, 0:WIN], c.tri[0:P, 0:P], counts[:, :], start=True, stop=True).then_inc(summed, 1)

        G = 4
        rows16, hi16, lo16 = (sb(n, [P, EC], F16) for n in ("rows16", "hi16", "lo16"))
        hot_row, hot_hi, hot_lo = (sb(n, [P, 2, G, SLOT], F16) for n in ("hot_row", "hot_hi", "hot_lo"))
        hot_tile = sb("hot_tile", [P, 2, G, TILES], F16)
        hi, lo, mid = (sb(n, [128, TILES])[:, :] for n in ("hi", "lo", "mid"))
        cast_s, rows_ready, tiles_ready, hi_ready, lo_ready, hots_used, zeroed, moved, move_order = c.sem(
            *("mv_" + n for n in ("cast", "rows_ready", "tiles_ready", "hi_ready", "lo_ready", "hots_used", "zeroed", "moved", "order")))
        QUADS = EC // G
        wide = [P, G, SLOT]
        with nc.Block() as block:
            @block.vector
            def _(dve):
                v = nc.vector
                v.memset(c.banks[0][:, :], 0.0).then_inc(zeroed, 1)
                v.memset(c.banks[1][:, :], 0.0).then_inc(zeroed, 1)
                for to, of in ((rows16, row_of), (hi16, code_hi), (lo16, code_lo)):
                    v.tensor_copy(to[:, :], of).then_inc(cast_s, 1)
                dve.wait_ge(cast_s, 3)

                def hots(q, b):
                    wait_from(dve, hi_ready, G * q - G)
                    wait_from(dve, lo_ready, q - 1)
                    v.tensor_tensor(hot_row[:, b, :, :], c.iota[0:P, 0:SLOT].unsqueeze(1).to_broadcast(wide),
                                    rows16[:, bass.ds(q * G, G)].unsqueeze(2).to_broadcast(wide), ALU.is_equal).then_inc(rows_ready, 1)
                    wait_from(dve, hots_used, q - 1)
                    for g in range(G):
                        last = v.tensor_scalar(hot_tile[:, b, g, :], c.iota[0:P, :], col(tile_of, q * G + g), None, ALU.is_equal)
                    last.then_inc(tiles_ready, 1)
                over_tiles(dve, hots, count=QUADS)
                dve.wait_ge(moved, 1)
                order = Order(dve, move_order)
                order.then(v.tensor_copy(hi, c.banks[0][:, 0:TILES]))
                order.then(v.tensor_copy(lo, c.banks[1][:, 0:TILES]))
                order.then(v.tensor_scalar(mid, lo, 1.0 / 128, -63.5 / 128, ALU.mult, ALU.add))
                order.then(v.tensor_scalar(mid, mid, ROUND, ROUND, ALU.add, ALU.subtract))
                order.then(v.scalar_tensor_tensor(out=lo, in0=mid, scalar=-128.0, in1=lo, op0=ALU.mult, op1=ALU.add))
                order.then(v.tensor_scalar(slot_dst[:, :], lo, -1.0, None, ALU.add))
                order.then(v.scalar_tensor_tensor(out=hi, in0=hi, scalar=8.0, in1=mid, op0=ALU.mult, op1=ALU.add))
                order.then(v.tensor_copy(slot_row[:, :], hi))

            @block.scalar
            def _(act):
                def codes(q, b):
                    act.wait_ge(rows_ready, q + 1)
                    wait_from(act, hots_used, q - 1)
                    for g in range(G):
                        nc.scalar.activation(hot_hi[:, b, g, :], hot_row[:, b, g, :], ACT.Copy, scale=col(code_hi, q * G + g)).then_inc(hi_ready, 1)
                over_tiles(act, codes, count=QUADS)

            @block.gpsimd
            def _(pool):
                def codes(q, b):
                    pool.wait_ge(rows_ready, q + 1)
                    wait_from(pool, hots_used, q - 1)
                    nc.gpsimd.tensor_tensor(hot_lo[:, b, :, :], hot_row[:, b, :, :], lo16[:, bass.ds(q * G, G)].unsqueeze(2).to_broadcast(wide), ALU.mult).then_inc(lo_ready, 1)
                pool.wait_ge(cast_s, 3)
                over_tiles(pool, codes, count=QUADS)

            @block.tensor
            def _(pe):
                pe.wait_ge(zeroed, 2)

                def add(q, b):
                    pe.wait_ge(tiles_ready, q + 1)
                    pe.wait_ge(lo_ready, q + 1)
                    for g in range(G):
                        pe.wait_ge(hi_ready, G * q + g + 1)
                        nc.tensor.matmul(c.banks[0][:, 0:TILES], hot_hi[:, b, g, :], hot_tile[:, b, g, :], start=False, stop=False, skip_group_check=True)
                        last = nc.tensor.matmul(c.banks[1][:, 0:TILES], hot_lo[:, b, g, :], hot_tile[:, b, g, :], start=False, stop=False, skip_group_check=True)
                    last.then_inc(hots_used, 1)
                over_tiles(pe, add, count=QUADS)
                pe.wait_ge(hots_used, QUADS)
                pe.sem_inc(moved, 1)


def message_stage(c, layer, aggr, selfp, mixer, table_y):
    nc, A, first = c.nc, c.A, layer == 0
    n_ = lambda name: f"me{layer}_{name}"
    with ExitStack() as scope:
        def sb(name, shape, dt=F32):
            return c.sb(scope, n_(name), shape, dt)

        w_rel, w_self = sb("w_rel", [128, 2, RELS * D]), sb("w_self", [128, 2, D])
        bias = sb("bias", [P, 2, D])
        gamma = sb("gamma", [P, D])
        h, normed, own = sb("h", [P, 2, D]), sb("normed", [P, 2, D]), sb("own", [P, 2, D])
        loads = RELS + 3 + (not first)
        hT, y = sb("hT", [128, 2, 2, P]), sb("y", [P, 2, RELS * D])
        ty = table_y.rearrange("(r p t) d -> p r t d", r=RELS, t=WIN)
        landed, order_s, var_ready, std_ready, n_ready, h_ready, turned, t_ready, products, y_ready, kept, normed_s, scaled_s, bias_s = c.sem(
            *(n_(n) for n in ("landed", "order", "var", "std", "n_ready", "h_ready", "turned", "t_ready", "products", "y_ready", "kept", "normed", "scaled", "bias")))
        y_stored = [c.sem(n_(f"y_stored{i}")) for i in range(2)]
        with nc.Block() as block:
            @block.sync
            def _(sp):
                for r in range(RELS):
                    sp.dma_start(w_rel[:, :, r * D:(r + 1) * D], A["L0_gnn_W"][layer, r].rearrange("(k p) n -> p k n", k=2)).then_inc(landed, 16)
                sp.dma_start(w_self[:, :, :], A["L0_gnn_loop_w"][layer].rearrange("(k p) n -> p k n", k=2)).then_inc(landed, 16)
                for i, n in enumerate(("L0_gnn_bias", "L0_gnn_ln_beta")):
                    sp.dma_start(bias[:, i, :], row_bcast(A[n][layer], P)).then_inc(landed, 16)
                if not first:
                    sp.dma_start(gamma[:, :], row_bcast(A["L0_gnn_ln_gamma"][layer - 1], P)).then_inc(landed, 16)

                def step(t, b):
                    sp.wait_ge(y_ready, t + 1)
                    sp.dma_start(ty[:, :, t, :], y[:, b, :].rearrange("p (r d) -> p r d", r=RELS)).then_inc(y_stored[b], 16)
                over_tiles(sp, step)
                sp.wait_ge(y_stored[0], 16 * (WIN // 2 + 1))
                sp.wait_ge(y_stored[1], 16 * (WIN // 2))

            @block.vector
            def _(dve):
                v = nc.vector
                if not first:
                    order = Order(dve, order_s)
                    tile_stats(c, dve, order, aggr)
                    c.finish_stats(order, var_ready, std_ready)

                def first_h(t, b):
                    wait_from(dve, turned, t - 1)
                    c.normalised(h[:, b, :], t).then_inc(h_ready, 1)

                def norm(t, b):
                    wait_from(dve, n_ready, t - 1)
                    v.tensor_scalar(normed[:, b, :], aggr[:, t, :], col(c.rstd, t), col(c.nmr, t), ALU.mult, ALU.add).then_inc(normed_s, 1)

                def scale(t, b):
                    dve.wait_ge(normed_s, t + 1)
                    v.tensor_tensor(normed[:, b, :], normed[:, b, :], gamma[:, :], ALU.mult).then_inc(scaled_s, 1)

                def add_self(t, b):
                    dve.wait_ge(scaled_s, t + 1)
                    wait_from(dve, turned, t - 1)
                    v.tensor_tensor(h[:, b, :], normed[:, b, :], selfp[:, t, :], ALU.add).then_inc(n_ready, 1)

                def norm_own(t, b):
                    wait_from(dve, scaled_s, t - 1)
                    c.normalised(own[:, b, :], t).then_inc(normed_s, 1)

                def add_h(t, b):
                    dve.wait_ge(normed_s, t + 1)
                    v.tensor_tensor(c.X[:, t, :], c.X[:, t, :], own[:, b, :], ALU.add).then_inc(scaled_s, 1)

                def keep(t, b):
                    dve.wait_ge(products, t + 1)
                    last = v.tensor_tensor(selfp[:, t, :], bias[:, 0, :], c.banks[4 + b][0:P, 0:D], ALU.add)
                    if first:
                        dve.wait_ge(scaled_s, t + 1)
                        last = v.tensor_tensor(c.X[:, t, :], c.X[:, t, :], c.banks[4 + b][0:P, D:2 * D], ALU.add)
                    last.then_inc(kept, 1)
                dve.wait_ge(landed, 16 * loads)
                v.tensor_tensor(bias[:, 0, :], bias[:, 0, :], bias[:, 1, :], ALU.add).then_inc(bias_s, 1)
                dve.wait_ge(bias_s, 1)
                if first:
                    over_tiles(dve, (first_h, 2), (add_h, 1), (norm_own, 2), keep)
                else:
                    over_tiles(dve, (add_self, 3), (scale, 4), (norm, 5), keep)

            @block.scalar
            def _(act):
                if not first:
                    c.root(act, var_ready, std_ready)

                def relu(t, b):
                    act.wait_ge(n_ready, t + 1)
                    nc.scalar.activation(h[:, b, :], h[:, b, :], ACT.Relu).then_inc(h_ready, 1)

                def copy_t(t, b):
                    act.wait_ge(turned, t + 1)
                    wait_from(act, products, t - 1)
                    nc.scalar.activation(hT[:, b, :, :], c.banks[b][:, 0:256].rearrange("p (k n) -> p k n", k=2)[:, :, 0:P], ACT.Copy).then_inc(t_ready, 1)

                def copy_y(t, b):
                    act.wait_ge(products, t + 1)
                    if not isinstance(t, int) or t >= 2:
                        act.wait_ge(y_stored[b], t * 8 - 8 * b)
                    nc.scalar.activation(y[:, b, :], c.banks[2 + b][0:P, :], ACT.Copy).then_inc(y_ready, 1)
                over_tiles(act, (copy_t, 1), *([] if first else [(relu, 2)]), copy_y)

            @block.tensor
            def _(pe):
                def turn(t, b):
                    pe.wait_ge(h_ready, t + 1)
                    wait_from(pe, t_ready, t - 1)
                    for k in range(2):
                        last = nc.tensor.transpose(c.banks[b][:, k * 128:k * 128 + P], h[:, b, k * 128:(k + 1) * 128], c.ident[0:P, 0:P])
                    last.then_inc(turned, 1)

                def multiply(t, b):
                    pe.wait_ge(t_ready, t + 1)
                    wait_from(pe, y_ready, t - 1)
                    wait_from(pe, kept, t - 1)
                    for k in range(2):
                        nc.tensor.matmul(c.banks[2 + b][0:P, :], hT[:, b, k, :], w_rel[:, k, :], start=(k == 0), stop=(k == 1))
                    own = c.banks[4 + b][0:P, 0:D]
                    for k in range(2):
                        last = nc.tensor.matmul(own, hT[:, b, k, :], w_self[:, k, :], start=(k == 0), stop=(k == 1), skip_group_check=True)
                    if first:
                        for k in range(2):
                            last = nc.tensor.matmul(c.banks[4 + b][0:P, D + 128 * k:D + 128 * k + 128], hT[:, b, k, :], mixer[:, k, :],
                                                    start=False, stop=True, skip_group_check=True)
                    last.then_inc(products, 1)
                pe.wait_ge(landed, 16 * loads)
                over_tiles(pe, (turn, 1), multiply)


def gather_stage(c, layer, aggr, table_y, slot_row, slot_dst, slot_win):
    nc = c.nc
    n_ = lambda name: f"ga{layer}_{name}"
    with ExitStack() as scope:
        def sb(name, shape, dt=F32):
            return c.sb(scope, n_(name), shape, dt)

        index = sb("index", [128, 2, HALF], I32)
        got, hot = sb("got", [128, RING, D]), sb("hot", [128, RING, P])
        index_ready, released, summed, hot_ready, added, zeroed = c.sem(
            *(n_(n) for n in ("index_ready", "released", "summed", "hot_ready", "added", "zeroed")))
        gathered = [c.sem(n_(f"gathered{g}")) for g in range(RING)]
        with nc.Block() as block:
            @block.gpsimd
            def _(pool):
                def half(s, k):
                    pool.wait_ge(index_ready, s + HALF)
                    pool.sem_inc(released, 1)
                    for g in range(HALF):
                        nc.gpsimd.indirect_dma_start(got[:, k * HALF + g, :], None, table_y,
                                                     bass.IndirectOffsetOnAxis(ap=index[:, k, g:g + 1], axis=0)).then_inc(gathered[k * HALF + g], 16)
                half(0, 0)
                half(HALF, 1)
                with pool.Fori(RING, TILES - RING + 1, RING) as s:
                    half(s, 0)
                    half(s + HALF, 1)

            @block.scalar
            def _(act):
                def stage(s, k):
                    wait_from(act, summed, s - HALF)
                    nc.scalar.activation(index[:, k, :], slot_row[:, bass.ds(s, HALF)], ACT.Copy).then_inc(index_ready, HALF)
                stage(0, 0)
                stage(HALF, 1)
                with act.Fori(RING, TILES - RING + 1, RING) as s:
                    stage(s, 0)
                    stage(s + HALF, 1)

            @block.tensor
            def _(pe):
                def total(s, g):
                    if g % QUAD == 0:
                        pe.wait_ge(hot_ready, s + g + QUAD)
                        wait_from(pe, added, s + g + QUAD - RING)
                    pe.wait_ge(gathered[g], s + 16)
                    nc.tensor.matmul(c.banks[g // 2][0:P, D * (g % 2):D * (g % 2) + D], hot[:, g, :], got[:, g, :], start=(g % 2 == 0), stop=True,
                                     skip_group_check=True).then_inc(summed, 1)
                for g in range(RING):
                    total(0, g)
                with pe.Fori(RING, TILES - RING + 1, RING) as s:
                    for g in range(RING):
                        total(s, g)

            @block.vector
            def _(dve):
                v = nc.vector

                def make_hots(s, q):
                    wide = [128, QUAD, P]
                    g = QUAD * q % RING
                    v.tensor_tensor(hot[:, g:g + QUAD, :], c.iota_f[:, 0:P].unsqueeze(1).to_broadcast(wide),
                                    slot_dst[:, bass.ds(s + QUAD * q, QUAD)].unsqueeze(2).to_broadcast(wide), ALU.is_equal).then_inc(hot_ready, QUAD)

                def adds(s, q):
                    dve.wait_ge(summed, s + QUAD * q + QUAD)
                    for g in range(QUAD * q, QUAD * q + QUAD):
                        w = dve.value_load(slot_win[0:1, bass.ds(s + g, 1)], min_val=0, max_val=WIN - 1)
                        wait_from(dve, added, s + g)
                        v.tensor_tensor(aggr[:, bass.ds(w, 1), :].rearrange("p o d -> p (o d)"), aggr[:, bass.ds(w, 1), :].rearrange("p o d -> p (o d)"),
                                        c.banks[g // 2][0:P, D * (g % 2):D * (g % 2) + D], ALU.add).then_inc(added, 1)
                v.memset(aggr[:, :, :], 0.0).then_inc(zeroed, 1)
                make_hots(0, 0)
                make_hots(0, 1)
                dve.wait_ge(zeroed, 1)
                QUADS_RING = RING // QUAD
                for q in range(QUADS_RING):
                    make_hots(0, q + 2)
                    adds(0, q)
                with dve.Fori(RING, TILES - 2 * RING + 1, RING) as s:
                    for q in range(QUADS_RING):
                        make_hots(s, q + 2)
                        adds(s, q)
                for q in range(QUADS_RING):
                    if q + 2 < QUADS_RING:
                        make_hots(TILES - RING, q + 2)
                    adds(TILES - RING, q)


def gnn_out_stage(c, aggr, selfp):
    nc, A = c.nc, c.A
    with ExitStack() as scope:
        gamma, normed = c.sb(scope, "go_gamma", [P, D]), c.sb(scope, "go_normed", [P, 2, D])
        scaled = c.sb(scope, "go_scaled", [P, 2, D])
        landed, order_s, var_ready, std_ready, rstd_ready, var2_ready, std2_ready, self_added, normed_s, scaled_s, added = c.sem(
            *("go_" + n for n in ("landed", "order", "var", "std", "rstd", "var2", "std2", "self_added", "normed", "scaled", "added")))
        PART = 5
        with nc.Block() as block:
            @block.sync
            def _(sp):
                sp.dma_start(gamma[:, :], row_bcast(A["L0_gnn_ln_gamma"][LAYERS - 1], P)).then_inc(landed, 16)

            @block.gpsimd
            def _(pool):
                for t in range(0, WIN, PART):
                    x = c.X[:, t:t + PART, :]
                    nc.gpsimd.tensor_tensor(x, x, selfp[:, t:t + PART, :], ALU.add).then_inc(self_added, PART)

            @block.vector
            def _(dve):
                v = nc.vector
                order = Order(dve, order_s)
                tile_stats(c, dve, order, aggr)
                c.finish_stats(order, var_ready, std_ready)
                dve.sem_inc(rstd_ready, 1)
                dve.wait_ge(landed, 16)

                def scale(t, b):
                    dve.wait_ge(normed_s, t + 1)
                    wait_from(dve, added, t - 1)
                    v.tensor_tensor(scaled[:, b, :], normed[:, b, :], gamma[:, :], ALU.mult).then_inc(scaled_s, 1)

                def add(t, b):
                    dve.wait_ge(scaled_s, t + 1)
                    dve.wait_ge(self_added, t + 1)
                    v.tensor_tensor(c.X[:, t, :], c.X[:, t, :], scaled[:, b, :], ALU.add).then_inc(added, 1)

                def stats(t, b):
                    dve.wait_ge(added, t + 1)
                    v.bn_stats(c.stats[:, t, :], c.X[:, t, :]).then_inc(order_s, 1)
                over_tiles(dve, (scale, 2), (add, 1), stats)
                order.k += WIN
                dve.wait_ge(order_s, order.k)
                c.finish_stats(order, var2_ready, std2_ready)

            @block.scalar
            def _(act):
                c.root(act, var_ready, std_ready)

                def norm(t, b):
                    wait_from(act, scaled_s, t - 1)
                    nc.scalar.activation(normed[:, b, :], aggr[:, t, :], ACT.Identity, scale=col(c.rstd, t), bias=col(c.nmr, t)).then_inc(normed_s, 1)
                act.wait_ge(rstd_ready, 1)
                over_tiles(act, norm)
                c.root(act, var2_ready, std2_ready)


def slice_stage(c):
    nc, A, banks = c.nc, c.A, c.banks
    with ExitStack() as scope:
        def sb(name, shape, dt=F32):
            return c.sb(scope, "sl_" + name, shape, dt)

        W = sb("weights", [P, WIN, INNER])
        logit_w = sb("logit_w", [128, 2, INNER])
        logit_rows = sb("logit_rows", [P, INNER])
        M = sb("M", [128, 4, D])
        b_out = sb("b_out", [P, D])
        with ExitStack() as prep:
            def pb(name, shape, dt=F32):
                return c.sb(prep, "slp_" + name, shape, dt)

            w_x, w_xT = pb("w_x", [128, 2, INNER]), pb("w_xT", [128, 4, D])
            pair = pb("pair", [128, 128])
            b_x, b_slice = pb("b_x", [128, 4]), pb("b_slice", [1, SD])
            logit_b = pb("logit_b", [1, INNER])
            inv_temp = pb("inv_temp", [128, HEADS])
            landed, cleared, order_s, turned, copied, made = c.sem(*("slp_" + n for n in ("landed", "cleared", "order", "turned", "copied", "made")))
            with nc.Block() as block:
                @block.sync
                def _(sp):
                    sp.dma_start(w_x[:, :, :], A["L0_ffn_W_x"].rearrange("(k p) n -> p k n", k=2)).then_inc(landed, 16)
                    with nc.allow_non_contiguous_dma(reason="512 floats, once"):
                        sp.dma_start(b_x[:, :], A["L0_ffn_b_x"].rearrange("(k p) -> p k", p=128)).then_inc(landed, 16)
                    sp.dma_start(b_slice[:, :], A["L0_ffn_b_slice"].unsqueeze(0)).then_inc(landed, 16)
                    sp.dma_start(inv_temp[:, :], row_bcast(A["L0_ffn_temperature"].rearrange("a h b e -> (a h b e)"), 128)).then_inc(landed, 16)
                    sp.dma_start(b_out[:, :], row_bcast(A["L0_ffn_b_out"], P)).then_inc(landed, 16)
                    sp.wait_ge(cleared, 1)
                    for i in range(2):
                        sp.dma_start(pair[i * SD:(i + 1) * SD, i * SD:(i + 1) * SD], A["L0_ffn_W_slice"]).then_inc(landed, 16)

                @block.tensor
                def _(pe):
                    pe.wait_ge(landed, 112)
                    for k in range(2):
                        for a in range(4):
                            nc.tensor.transpose(banks[k][:, a * 128:a * 128 + 128], w_x[:, k, a * 128:a * 128 + 128], c.ident[:, :]).then_inc(turned, 1)
                    pe.wait_ge(copied, 2)
                    for k in range(2):
                        for a in range(4):
                            nc.tensor.matmul(banks[2 + k][:, a * 128:a * 128 + 128], w_xT[:, a, k * 128:k * 128 + 128], pair[:, :],
                                             start=(a == 0), stop=True, skip_group_check=True)
                    for a in range(4):
                        last = nc.tensor.matmul(banks[4][0:1, a * 128:a * 128 + 128], b_x[:, a:a + 1], pair[:, :],
                                                start=(a == 0), stop=True, skip_group_check=True)
                    last.then_inc(made, 1)
                    pe.wait_ge(order_s, 4)
                    nc.tensor.matmul(banks[5][0:P, :], c.ones[0:1, 0:P], logit_b[:, :], start=True, stop=True).then_inc(made, 1)

                @block.scalar
                def _(act):
                    for k in range(2):
                        act.wait_ge(turned, 4 * k + 4)
                        nc.scalar.activation(w_xT[:, :, k * 128:k * 128 + 128], banks[k][:, :].rearrange("p (a n) -> p a n", a=4), ACT.Copy).then_inc(copied, 1)

                @block.vector
                def _(dve):
                    v, order = nc.vector, Order(dve, order_s)
                    v.memset(pair[:, :], 0.0).then_inc(cleared, 1)
                    dve.wait_ge(landed, 112)
                    order.then(v.tensor_scalar(inv_temp[:, :], inv_temp[:, :], 0.1, 5.0, ALU.max, ALU.min))
                    order.then(v.reciprocal(inv_temp[:, :], inv_temp[:, :]))
                    dve.wait_ge(made, 1)
                    by_head = "p (h g) -> p h g"
                    for k in range(2):
                        v.tensor_tensor(logit_w[:, k, :].rearrange(by_head, h=HEADS), banks[2 + k][:, :].rearrange(by_head, h=HEADS),
                                        inv_temp[:, :].unsqueeze(2).to_broadcast([128, HEADS, SD]), ALU.mult)
                    order.then(v.tensor_tensor(logit_b[:, :].rearrange(by_head, h=HEADS), banks[4][0:1, :].rearrange(by_head, h=HEADS),
                                               b_slice[:, :].unsqueeze(1).to_broadcast([1, HEADS, SD]), ALU.add))
                    order.then(v.tensor_tensor(logit_b[:, :].rearrange(by_head, h=HEADS), logit_b[:, :].rearrange(by_head, h=HEADS),
                                               inv_temp[0:1, :].unsqueeze(2).to_broadcast([1, HEADS, SD]), ALU.mult))
                    assert order.k == 4
                    dve.wait_ge(made, 2)
                    order.then(v.tensor_copy(logit_rows[:, :], banks[5][0:P, :]))

        with ExitStack() as s1:
            def qb(name, shape, dt=F32):
                return c.sb(s1, "sla_" + name, shape, dt)

            HN = qb("HN", [P, WIN, D])
            h, hT = qb("h", [P, 2, D]), qb("hT", [128, 2, 2, P])
            e, w = qb("e", [P, 2, INNER]), qb("w", [P, 2, INNER])
            peak, total = qb("peak", [P, 2, HEADS]), qb("total", [P, 2, HEADS])
            order_s, total_s, hn_ready, h_ready, turned, t_ready, logits, e_ready, exped, r_ready, w_ready, w_kept, pooled, zeroed = c.sem(
                *("sla_" + n for n in ("order", "total", "hn_ready", "h_ready", "turned", "t_ready", "logits", "e_ready", "exped", "r_ready", "w_ready", "w_kept",
                                       "pooled", "zeroed")))
            by_head = "p (h g) -> p h g"
            with nc.Block() as block:
                @block.vector
                def _(dve):
                    v = nc.vector
                    for i in (4, 5, 6):
                        v.memset(banks[i][:, :], 0.0).then_inc(zeroed, 1)

                    def make_h(t, b):
                        c.normalised(HN[:, t, :], t).then_inc(hn_ready, 1)

                    def shift(t, b):
                        order = Order(dve, order_s, t, 2)
                        dve.wait_ge(logits, t + 1)
                        wait_from(dve, w_ready, t - 1)
                        eb = e[:, b, :].rearrange(by_head, h=HEADS)
                        order.then(v.tensor_tensor(e[:, b, :], banks[2 + b][0:P, :], logit_rows[:, :], ALU.add))
                        order.then(v.tensor_reduce(peak[:, b, :], eb, AX.X, ALU.max))
                        v.tensor_tensor(eb, eb, peak[:, b, :].unsqueeze(2).to_broadcast([P, HEADS, SD]), ALU.subtract).then_inc(e_ready, 1)

                    def sum_up(t, b):
                        order = Order(dve, total_s, t, 1)
                        dve.wait_ge(exped, t + 1)
                        order.then(v.tensor_reduce(total[:, b, :], e[:, b, :].rearrange(by_head, h=HEADS), AX.X, ALU.add))
                        v.reciprocal(total[:, b, :], total[:, b, :]).then_inc(r_ready, 1)
                    over_tiles(dve, (shift, 2), (sum_up, 1), (make_h, 5))

                @block.gpsimd
                def _(pool):
                    def weights(t, b):
                        pool.wait_ge(r_ready, t + 1)
                        wait_from(pool, pooled, t - 1)
                        wait_from(pool, w_kept, t - 1)
                        nc.gpsimd.tensor_tensor(w[:, b, :].rearrange(by_head, h=HEADS), e[:, b, :].rearrange(by_head, h=HEADS),
                                                total[:, b, :].unsqueeze(2).to_broadcast([P, HEADS, SD]), ALU.mult).then_inc(w_ready, 1)
                    over_tiles(pool, weights)

                @block.scalar
                def _(act):
                    def copy_h(t, b):
                        act.wait_ge(hn_ready, t + 1)
                        wait_from(act, turned, t - 1)
                        nc.scalar.activation(h[:, b, :], HN[:, t, :], ACT.Copy).then_inc(h_ready, 1)

                    def copy_t(t, b):
                        act.wait_ge(turned, t + 1)
                        wait_from(act, logits, t - 1)
                        nc.scalar.activation(hT[:, b, :, :], banks[b][:, 0:256].rearrange("p (k n) -> p k n", k=2)[:, :, 0:P], ACT.Copy).then_inc(t_ready, 1)

                    def exp(t, b):
                        act.wait_ge(e_ready, t + 1)
                        nc.scalar.activation(e[:, b, :], e[:, b, :], ACT.Exp).then_inc(exped, 1)

                    def keep(t, b):
                        act.wait_ge(w_ready, t + 1)
                        nc.scalar.activation(W[:, t, :], w[:, b, :], ACT.Copy).then_inc(w_kept, 1)
                    over_tiles(act, (exp, 2), (copy_t, 3), (copy_h, 4), keep)

                @block.tensor
                def _(pe):
                    def turn(t, b):
                        pe.wait_ge(h_ready, t + 1)
                        wait_from(pe, t_ready, t - 1)
                        for k in range(2):
                            last = nc.tensor.transpose(banks[b][:, k * 128:k * 128 + P], h[:, b, k * 128:(k + 1) * 128], c.ident[0:P, 0:P])
                        last.then_inc(turned, 1)

                    def logit(t, b):
                        pe.wait_ge(t_ready, t + 1)
                        wait_from(pe, order_s, 2 * t - 3)
                        for k in range(2):
                            last = nc.tensor.matmul(banks[2 + b][0:P, :], hT[:, b, k, :], logit_w[:, k, :], start=(k == 0), stop=(k == 1))
                        last.then_inc(logits, 1)

                    def pool_x(t, b):
                        pe.wait_ge(w_ready, t + 1)
                        for a in range(4):
                            wa = w[:, b, a * 128:(a + 1) * 128]
                            nc.tensor.matmul(banks[4 + a // 2][:, (a % 2) * D:(a % 2 + 1) * D], wa, HN[:, t, :], start=False, stop=False, skip_group_check=True)
                            last = nc.tensor.matmul(banks[6][:, a:a + 1], wa, c.ones[0:P, 0:1], start=False, stop=False, skip_group_check=True)
                        last.then_inc(pooled, 1)
                    pe.wait_ge(zeroed, 3)
                    over_tiles(pe, (logit, 2), (turn, 3), pool_x)

        with ExitStack() as s2:
            def rb(name, shape, dt=F32):
                return c.sb(s2, "slb_" + name, shape, dt)

            w_fx, b_fx = rb("w_fx", [128, 2, INNER]), rb("b_fx", [1, INNER])
            w_qkv = rb("w_qkv", [SD, 3, SD])
            w_out = rb("w_out", [SD, HEADS, D])
            inv, share = rb("inv", [128, 4]), rb("share", [128, 4])
            U, UT, shareT = rb("U", [128, 4, D]), rb("UT", [128, 2, INNER]), rb("shareT", [1, INNER])
            tokT, qkvT = rb("tokT", [SD, INNER]), rb("qkvT", [SD, 3, INNER])
            attn, attnT = rb("attn", [SD, HEADS, SD]), rb("attnT", [SD, INNER])
            peak, total, vw = rb("peak", [SD, HEADS]), rb("total", [SD, HEADS]), rb("vw", [SD, HEADS, D])
            landed, order_s, act_done, pe_done = c.sem(*("slb_" + n for n in ("landed", "dve_steps", "act_steps", "pe_steps")))
            with nc.Block() as block:
                @block.sync
                def _(sp):
                    sp.dma_start(w_fx[:, :, :], A["L0_ffn_W_fx"].rearrange("(k p) n -> p k n", k=2)).then_inc(landed, 16)
                    sp.dma_start(b_fx[:, :], A["L0_ffn_b_fx"].unsqueeze(0)).then_inc(landed, 16)
                    for i, n in enumerate("qkv"):
                        sp.dma_start(w_qkv[:, i, :], A[f"L0_ffn_W_{n}"]).then_inc(landed, 16)
                    sp.dma_start(w_out[:, :, :], A["L0_ffn_W_out"].rearrange("(h c) n -> c h n", c=SD)).then_inc(landed, 16)

                @block.vector
                def _(dve):
                    v, order = nc.vector, Order(dve, order_s)
                    order.then(v.tensor_scalar(inv[:, :], banks[6][:, 0:4], 1e-5, None, ALU.add))
                    order.then(v.reciprocal(inv[:, :], inv[:, :]))
                    order.then(v.tensor_tensor(share[:, :], inv[:, :], banks[6][:, 0:4], ALU.mult))
                    for a in range(4):
                        order.then(v.tensor_scalar(U[:, a, :], banks[4 + a // 2][:, (a % 2) * D:(a % 2 + 1) * D], inv[:, a:a + 1], None, ALU.mult))
                    assert order.k == 7
                    dve.wait_ge(pe_done, 4)
                    scores = banks[7][0:SD, :].rearrange("p (h g) -> p h g", h=HEADS)
                    order.then(v.tensor_reduce(peak[:, :], scores, AX.X, ALU.max))
                    order.then(v.tensor_tensor(attn[:, :, :], scores, peak[:, :].unsqueeze(2).to_broadcast([SD, HEADS, SD]), ALU.subtract))
                    dve.wait_ge(act_done, 6)
                    order.then(v.tensor_reduce(total[:, :], attn[:, :, :], AX.X, ALU.add))
                    order.then(v.reciprocal(total[:, :], total[:, :]))
                    order.then(v.tensor_tensor(attn[:, :, :], attn[:, :, :], total[:, :].unsqueeze(2).to_broadcast([SD, HEADS, SD]), ALU.mult))
                    assert order.k == 12
                    dve.wait_ge(pe_done, 5)
                    for i in range(4):
                        order.then(v.tensor_copy(vw[:, 2 * i:2 * i + 2, :].rearrange("p a d -> p (a d)"), banks[i][0:SD, :]))

                @block.scalar
                def _(act):
                    act.wait_ge(pe_done, 1)
                    for k in range(2):
                        nc.scalar.activation(UT[:, k, :], banks[k][:, :], ACT.Copy).then_inc(act_done, 1)
                    nc.scalar.activation(shareT[:, :], banks[2][0:1, :], ACT.Copy).then_inc(act_done, 1)
                    act.wait_ge(pe_done, 2)
                    nc.scalar.activation(tokT[:, :], banks[3][0:SD, :], ACT.Copy).then_inc(act_done, 1)
                    act.wait_ge(pe_done, 3)
                    for i in range(3):
                        last = nc.scalar.activation(qkvT[:, i, :], banks[4 + i][0:SD, :], ACT.Copy)
                    last.then_inc(act_done, 1)
                    act.wait_ge(order_s, 9)
                    nc.scalar.activation(attn[:, :, :], attn[:, :, :], ACT.Exp, scale=float(SD) ** -0.5).then_inc(act_done, 1)
                    act.wait_ge(pe_done, 6)
                    nc.scalar.activation(attnT[:, :], banks[4][0:SD, :], ACT.Copy).then_inc(act_done, 1)
                    act.wait_ge(pe_done, 7)
                    for i in range(2):
                        nc.scalar.activation(M[:, 2 * i:2 * i + 2, :].rearrange("p a d -> p (a d)"), banks[5 + i][:, :], ACT.Copy).then_inc(act_done, 1)

                @block.tensor
                def _(pe):
                    mm = nc.tensor.matmul
                    pe.wait_ge(order_s, 7)
                    for k in range(2):
                        for a in range(4):
                            nc.tensor.transpose(banks[k][:, a * 128:a * 128 + 128], U[:, a, k * 128:k * 128 + 128], c.ident[:, :])
                    for a in range(4):
                        last = nc.tensor.transpose(banks[2][0:1, a * 128:a * 128 + 128], share[:, a:a + 1], c.ident[:, :])
                    last.then_inc(pe_done, 1)
                    pe.wait_ge(act_done, 3)
                    pe.wait_ge(landed, 96)
                    for h in range(HEADS):
                        at, o = slice(h * SD, (h + 1) * SD), banks[3][0:SD, h * SD:(h + 1) * SD]
                        for k in range(2):
                            mm(o, w_fx[:, k, at], UT[:, k, at], start=(h == 0 and k == 0), stop=False, skip_group_check=True)
                        last = mm(o, b_fx[0:1, at], shareT[0:1, at], start=False, stop=True, skip_group_check=True)
                    last.then_inc(pe_done, 1)
                    pe.wait_ge(act_done, 4)
                    for i in range(3):
                        last = mm(banks[4 + i][0:SD, :], w_qkv[:, i, :], tokT[:, :], start=True, stop=True)
                    last.then_inc(pe_done, 1)
                    pe.wait_ge(act_done, 5)
                    for h in range(HEADS):
                        at = slice(h * SD, (h + 1) * SD)
                        last = mm(banks[7][0:SD, at], qkvT[:, 0, at], qkvT[:, 1, at], start=(h == 0), stop=True, skip_group_check=True)
                    last.then_inc(pe_done, 1)
                    for h in range(HEADS):
                        last = mm(banks[h // 2][0:SD, (h % 2) * D:(h % 2 + 1) * D], qkvT[:, 2, h * SD:(h + 1) * SD], w_out[:, h, :],
                                  start=(h % 2 == 0), stop=True, skip_group_check=True)
                    last.then_inc(pe_done, 1)
                    pe.wait_ge(order_s, 12)
                    for h in range(HEADS):
                        last = nc.tensor.transpose(banks[4][0:SD, h * SD:(h + 1) * SD], attn[:, h, :], c.ident[0:SD, 0:SD])
                    last.then_inc(pe_done, 1)
                    pe.wait_ge(act_done, 7)
                    pe.wait_ge(order_s, 16)
                    for h in range(HEADS):
                        a = h // 2
                        last = mm(banks[5 + a // 2][(h % 2) * SD:(h % 2 + 1) * SD, (a % 2) * D:(a % 2 + 1) * D],
                                  attnT[:, h * SD:(h + 1) * SD], vw[:, h, :], start=(a % 2 == 0), stop=True, skip_group_check=True)
                    last.then_inc(pe_done, 1)

        with ExitStack() as s3:
            w, wT = c.sb(s3, "slc_w", [P, 2, INNER]), c.sb(s3, "slc_wT", [128, 2, 4, P])
            order_s, biased, w_ready, turned, t_ready, products, added, var_ready, std_ready = c.sem(
                *("slc_" + n for n in ("order", "biased", "w_ready", "turned", "t_ready", "products", "added", "var", "std")))
            with nc.Block() as block:
                @block.gpsimd
                def _(pool):
                    def stage(t, b):
                        wait_from(pool, turned, t - 1)
                        nc.gpsimd.tensor_copy(w[:, b, :], W[:, t, :]).then_inc(w_ready, 1)
                    over_tiles(pool, stage)

                @block.tensor
                def _(pe):
                    def turn(t, b):
                        pe.wait_ge(w_ready, t + 1)
                        wait_from(pe, t_ready, t - 1)
                        for a in range(4):
                            last = nc.tensor.transpose(banks[b][:, a * 128:a * 128 + P], w[:, b, a * 128:(a + 1) * 128], c.ident[0:P, 0:P])
                        last.then_inc(turned, 1)

                    def multiply(t, b):
                        pe.wait_ge(t_ready, t + 1)
                        wait_from(pe, added, t - 1)
                        o = banks[2 + b][0:P, 0:D]
                        for a in range(4):
                            last = nc.tensor.matmul(o, wT[:, b, a, :], M[:, a, :], start=(a == 0), stop=(a == 3))
                        last.then_inc(products, 1)
                    over_tiles(pe, (turn, 1), multiply)

                @block.scalar
                def _(act):
                    def copy_t(t, b):
                        act.wait_ge(turned, t + 1)
                        wait_from(act, products, t - 1)
                        nc.scalar.activation(wT[:, b, :, :], banks[b][:, :].rearrange("p (a n) -> p a n", a=4)[:, :, 0:P], ACT.Copy).then_inc(t_ready, 1)
                    over_tiles(act, copy_t)
                    c.root(act, var_ready, std_ready)

                @block.vector
                def _(dve):
                    def add_bias(t, b):
                        nc.vector.tensor_tensor(c.X[:, t, :], c.X[:, t, :], b_out[:, :], ALU.add).then_inc(biased, 1)

                    def add(t, b):
                        dve.wait_ge(products, t + 1)
                        dve.wait_ge(biased, t + 1)
                        nc.vector.tensor_tensor(c.X[:, t, :], c.X[:, t, :], banks[2 + b][0:P, 0:D], ALU.add).then_inc(added, 1)

                    def stats(t, b):
                        dve.wait_ge(added, t + 1)
                        nc.vector.bn_stats(c.stats[:, t, :], c.X[:, t, :]).then_inc(order_s, 1)
                    over_tiles(dve, (add, 1), (add_bias, 2), stats)
                    dve.wait_ge(order_s, WIN)
                    order = Order(dve, order_s)
                    order.k = WIN
                    c.finish_stats(order, var_ready, std_ready)


def attention_stage(c):
    nc, A, banks = c.nc, c.A, c.banks
    KV = 128 + 4
    with ExitStack() as scope:
        def sb(name, shape, dt=F32):
            return c.sb(scope, "at_" + name, shape, dt)

        Q = sb("Q", [P, WIN, D])
        rms = sb("rms", [P, WIN])
        kv = sb("kv", [128, 2, KV])
        w_out, b_out = sb("w_out", [128, 2, D]), sb("b_out", [1, D])
        XTW = GD * GH + GH
        XT = sb("XT", [P, WIN, XTW])
        AL = sb("AL", [P, WIN, GH])
        ends = sb("ends", [P, 2, WIN], I32)
        table_x = nc.dram_tensor("table_x", [N, XTW], F32, kind="Internal").ap()
        table_l = nc.dram_tensor("table_l", [N, GH], F32, kind="Internal").ap()
        tx, tl = (t.rearrange("(p t) d -> p t d", t=WIN) for t in (table_x, table_l))

        with ExitStack() as s1:
            def qb(name, shape, dt=F32):
                return c.sb(s1, "ata_" + name, shape, dt)

            w_qkv, w_n1 = qb("w_qkv", [128, 2, 3 * D]), qb("w_n1", [128, 2])
            w_x = qb("w_x", [128, 2, XTW + GH])
            a_row = qb("a_row", [128, 2, D])
            prod = qb("prod", [128, 2, D])
            h, hT, xt = qb("h", [P, 2, D]), qb("hT", [128, 2, 2, P]), qb("xt", [P, 2, XTW + GH])
            e, m = qb("e", [P, 2, 2 * D]), qb("m", [P, 2, 2 * D])
            k_, v_ = qb("k", [P, 2, D]), qb("v", [P, 2, 2, 129])
            (landed, order_s, ms_ready, rms_std, h_ready, turned, t_ready, qk_done, xt_done, products, xt_ready, v_ready, e_ready, exped,
             kq_ready, summed, sums_order) = c.sem(
                *("ata_" + n for n in ("landed", "order", "ms", "rms_std", "h_ready", "turned", "t_ready", "qk_done", "xt_done", "products", "xt_ready",
                                       "v_ready", "e_ready", "exped", "kq_ready", "summed", "sums_order")))
            stored = [c.sem(f"ata_stored{i}") for i in range(2)]
            with nc.Block() as block:
                @block.sync
                def _(sp):
                    sp.dma_start(w_qkv[:, :, :], A["L1_mix_w_qkv"].rearrange("(k p) n -> p k n", k=2)).then_inc(landed, 16)
                    sp.dma_start(w_x[:, :, 0:D], A["L1_gnn_weight"].rearrange("(k p) n -> p k n", k=2)).then_inc(landed, 16)
                    for i, n in enumerate("rl"):
                        sp.dma_start(a_row[:, i, :], row_bcast(A[f"L1_gnn_attn_{n}"].rearrange("h d -> (h d)"), 128)).then_inc(landed, 16)
                    with nc.allow_non_contiguous_dma(reason="256 floats, once"):
                        sp.dma_start(w_n1[:, :], A["L1_mix_w_norm1"].rearrange("(k p) -> p k", p=128)).then_inc(landed, 16)
                    sp.dma_start(w_out[:, :, :], A["L1_mix_w_out"].rearrange("(k p) n -> p k n", k=2)).then_inc(landed, 16)
                    sp.dma_start(b_out[:, :], A["L1_mix_b_out"].unsqueeze(0)).then_inc(landed, 16)
                    for i, n in enumerate(("src", "dst")):
                        sp.dma_start(ends[:, i, :], A[n][0:N].rearrange("(p t) -> p t", t=WIN)).then_inc(landed, 16)

                    def step(t, b):
                        sp.wait_ge(xt_ready, t + 1)
                        sp.dma_start(tx[:, t, :], xt[:, b, 0:XTW]).then_inc(stored[b], 16)
                        sp.dma_start(tl[:, t, :], xt[:, b, XTW:XTW + GH]).then_inc(stored[b], 16)
                    over_tiles(sp, step)
                    sp.wait_ge(stored[0], 32 * (WIN // 2 + 1))
                    sp.wait_ge(stored[1], 32 * (WIN // 2))

                @block.vector
                def _(dve):
                    v, order = nc.vector, Order(dve, order_s)
                    order.then(v.tensor_scalar(rms[:, :], c.fin[:, 3, :], -LN_EPS, None, ALU.add))
                    order.then(v.tensor_tensor(rms[:, :], rms[:, :], c.rstd[:, :], ALU.mult))
                    order.then(v.tensor_tensor(rms[:, :], rms[:, :], c.rstd[:, :], ALU.mult))
                    v.tensor_scalar(rms[:, :], rms[:, :], RMS_EPS, None, ALU.add).then_inc(ms_ready, 1)
                    dve.wait_ge(rms_std, 1)
                    order.then(v.reciprocal(rms[:, :], rms[:, :]))
                    order.then(v.memset(v_[:, :, :, :], 1.0))
                    order.then(v.memset(banks[6][:, :], 0.0))
                    dve.wait_ge(landed, 144)
                    for k in range(2):
                        order.then(v.tensor_scalar(w_qkv[:, k, :], w_qkv[:, k, :], w_n1[:, k:k + 1], None, ALU.mult))
                        for i in range(2):
                            order.then(v.tensor_tensor(prod[:, i, :], w_x[:, k, 0:D], a_row[:, i, :], ALU.mult))
                            order.then(v.tensor_reduce(w_x[:, k, D + GH * i:D + GH * i + GH], prod[:, i, :].rearrange("p (h d) -> p h d", h=GH), AX.X, ALU.add))
                    dve.sem_inc(sums_order, 1)

                    def make_h(t, b):
                        wait_from(dve, turned, t - 1)
                        c.normalised(h[:, b, :], t).then_inc(h_ready, 1)

                    def elu(t, b):
                        dve.wait_ge(qk_done, t + 1)
                        wait_from(dve, kq_ready, 2 * t - 2)
                        r = col(rms, t)
                        qk = banks[4 + b][0:P, :]
                        v.tensor_scalar(e[:, b, :], qk, r, 0.0, ALU.mult, ALU.min)
                        v.tensor_scalar(m[:, b, :], qk, r, 0.0, ALU.mult, ALU.max).then_inc(e_ready, 1)
                    over_tiles(dve, (elu, 2), (make_h, 4))

                @block.gpsimd
                def _(pool):
                    def join(t, b):
                        pool.wait_ge(exped, t + 1)
                        nc.gpsimd.tensor_tensor(Q[:, t, :], e[:, b, 0:D], m[:, b, 0:D], ALU.add).then_inc(kq_ready, 1)
                        wait_from(pool, summed, t - 1)
                        nc.gpsimd.tensor_tensor(k_[:, b, :], e[:, b, D:2 * D], m[:, b, D:2 * D], ALU.add).then_inc(kq_ready, 1)
                    over_tiles(pool, join)

                @block.scalar
                def _(act):
                    act.wait_ge(ms_ready, 1)
                    nc.scalar.activation(rms[:, :], rms[:, :], ACT.Sqrt).then_inc(rms_std, 1)

                    def copy_t(t, b):
                        act.wait_ge(turned, t + 1)
                        wait_from(act, products, t - 1)
                        nc.scalar.activation(hT[:, b, :, :], banks[b][:, 0:256].rearrange("p (k n) -> p k n", k=2)[:, :, 0:P], ACT.Copy).then_inc(t_ready, 1)

                    def copy_xt(t, b):
                        act.wait_ge(xt_done, t + 1)
                        if not isinstance(t, int) or t >= 2:
                            act.wait_ge(stored[b], t * 16 - 16 * b)
                        nc.scalar.activation(xt[:, b, :], banks[2 + b][0:P, 0:XTW + GH], ACT.Copy).then_inc(xt_ready, 1)

                    def exp(t, b):
                        act.wait_ge(e_ready, t + 1)
                        nc.scalar.activation(e[:, b, :], e[:, b, :], ACT.Exp).then_inc(exped, 1)

                    def copy_v(t, b):
                        act.wait_ge(products, t + 1)
                        wait_from(act, summed, t - 1)
                        nc.scalar.activation(v_[:, b, :, 0:128], banks[7][0:P, 0:D].rearrange("p (a n) -> p a n", a=2), ACT.Identity, scale=col(rms, t)).then_inc(v_ready, 1)
                    over_tiles(act, (copy_t, 3), (copy_xt, 2), (exp, 2), (copy_v, 2))

                @block.tensor
                def _(pe):
                    mm = nc.tensor.matmul

                    def turn(t, b):
                        pe.wait_ge(h_ready, t + 1)
                        wait_from(pe, t_ready, t - 1)
                        for k in range(2):
                            last = nc.tensor.transpose(banks[b][:, k * 128:k * 128 + P], h[:, b, k * 128:(k + 1) * 128], c.ident[0:P, 0:P])
                        last.then_inc(turned, 1)

                    def multiply(t, b):
                        pe.wait_ge(t_ready, t + 1)
                        wait_from(pe, e_ready, t - 1)
                        for k in range(2):
                            last = mm(banks[4 + b][0:P, :], hT[:, b, k, :], w_qkv[:, k, 0:2 * D], start=(k == 0), stop=(k == 1))
                        last.then_inc(qk_done, 1)
                        wait_from(pe, xt_ready, t - 1)
                        for k in range(2):
                            last = mm(banks[2 + b][0:P, 0:XTW + GH], hT[:, b, k, :], w_x[:, k, :], start=(k == 0), stop=(k == 1))
                        last.then_inc(xt_done, 1)
                        wait_from(pe, v_ready, t)
                        for k in range(2):
                            last = mm(banks[7][0:P, 0:D], hT[:, b, k, :], w_qkv[:, k, 2 * D:3 * D], start=(k == 0), stop=(k == 1))
                        last.then_inc(products, 1)

                    def sums(t, b):
                        pe.wait_ge(kq_ready, 2 * t + 2)
                        pe.wait_ge(v_ready, t + 1)
                        for a in range(2):
                            last = mm(banks[6][:, 129 * a:129 * a + 129], k_[:, b, a * 128:a * 128 + 128], v_[:, b, a, :], start=False, stop=False, skip_group_check=True)
                        last.then_inc(summed, 1)
                    pe.wait_ge(sums_order, 1)
                    over_tiles(pe, (turn, 3), (multiply, 2), sums)

        H = sb("H", [P, WIN, D])
        with ExitStack() as s2:
            def rb(name, shape, dt=F32):
                return c.sb(s2, "atb_" + name, shape, dt)

            q, qT, z = rb("q", [P, 2, D]), rb("qT", [128, 2, 2, P]), rb("z", [P, 2, 2, 4])
            att, aT = rb("att", [P, 2, D]), rb("aT", [128, 2, 2, P])
            (kv_ready, q_ready, turned, t_ready, products, att_ready, turned2, t2_ready, products2, order_s, normed, added, got_x, got_l) = c.sem(
                *("atb_" + n for n in ("kv_ready", "q_ready", "turned", "t_ready", "products", "att_ready", "turned2", "t2_ready", "products2",
                                       "order", "normed", "added", "got_x", "got_l")))
            with nc.Block() as block:
                @block.gpsimd
                def _(pool):
                    for t in range(WIN):
                        nc.gpsimd.indirect_dma_start(AL[:, t, :], None, table_l, bass.IndirectOffsetOnAxis(ap=ends[:, 0, t:t + 1], axis=0)).then_inc(got_l, 16)
                        nc.gpsimd.indirect_dma_start(XT[:, t, :], None, table_x, bass.IndirectOffsetOnAxis(ap=ends[:, 1, t:t + 1], axis=0)).then_inc(got_x, 16)
                    pool.wait_ge(got_l, 16 * WIN)
                    pool.wait_ge(got_x, 16 * WIN)

                @block.tensor
                def _(pe):
                    mm = nc.tensor.matmul

                    def turn(t, b):
                        pe.wait_ge(q_ready, t + 1)
                        wait_from(pe, t_ready, t - 1)
                        for k in range(2):
                            last = nc.tensor.transpose(banks[b][:, k * 128:k * 128 + P], q[:, b, k * 128:(k + 1) * 128], c.ident[0:P, 0:P])
                        last.then_inc(turned, 1)

                    def multiply(t, b):
                        pe.wait_ge(t_ready, t + 1)
                        wait_from(pe, att_ready, 2 * t - 2)
                        for a in range(2):
                            last = mm(banks[2 + b][0:P, KV * a:KV * a + KV], qT[:, b, a, :], kv[:, a, :], start=(a == 0), stop=True, skip_group_check=True)
                        last.then_inc(products, 1)

                    def turn_att(t, b):
                        pe.wait_ge(att_ready, 2 * t + 2)
                        wait_from(pe, t2_ready, t - 1)
                        for k in range(2):
                            last = nc.tensor.transpose(banks[4 + b][:, k * 128:k * 128 + P], att[:, b, k * 128:(k + 1) * 128], c.ident[0:P, 0:P])
                        last.then_inc(turned2, 1)

                    def out(t, b):
                        pe.wait_ge(t2_ready, t + 1)
                        wait_from(pe, added, t - 1)
                        o = banks[6 + b][0:P, 0:D]
                        for k in range(2):
                            mm(o, aT[:, b, k, :], w_out[:, k, :], start=(k == 0), stop=False)
                        mm(o, c.ones[0:1, 0:P], b_out[:, :], start=False, stop=True).then_inc(products2, 1)
                    pe.wait_ge(kv_ready, 1)
                    over_tiles(pe, (turn_att, 2), (multiply, 3), (out, 1), (turn, 4))

                @block.scalar
                def _(act):
                    def stage_q(t, b):
                        wait_from(act, turned, t - 1)
                        nc.scalar.activation(q[:, b, :], Q[:, t, :], ACT.Copy).then_inc(q_ready, 1)

                    def norm(t, b):
                        nc.scalar.activation(H[:, t, :], c.X[:, t, :], ACT.Identity, scale=col(c.rstd, t), bias=col(c.nmr, t)).then_inc(normed, 1)

                    def copy_q(t, b):
                        act.wait_ge(turned, t + 1)
                        wait_from(act, products, t - 1)
                        nc.scalar.activation(qT[:, b, :, :], banks[b][:, 0:256].rearrange("p (k n) -> p k n", k=2)[:, :, 0:P], ACT.Copy).then_inc(t_ready, 1)

                    def copy_a(t, b):
                        act.wait_ge(turned2, t + 1)
                        wait_from(act, products2, t - 1)
                        nc.scalar.activation(aT[:, b, :, :], banks[4 + b][:, 0:256].rearrange("p (k n) -> p k n", k=2)[:, :, 0:P], ACT.Copy).then_inc(t2_ready, 1)
                    over_tiles(act, (copy_a, 2), (norm, 3), (copy_q, 4), (stage_q, 5))

                @block.vector
                def _(dve):
                    v, order = nc.vector, Order(dve, order_s)
                    for a in range(2):
                        order.then(v.tensor_tensor(kv[:, a, 0:128], c.blocks[:, :], banks[6][:, 129 * a:129 * a + 128], ALU.mult))
                        order.then(v.tensor_scalar(kv[:, a, 128:KV], c.heads[:, :], banks[6][:, 129 * a + 128:129 * a + 129], None, ALU.mult))
                    dve.sem_inc(kv_ready, 1)
                    start = order.k

                    def divide(t, b):
                        order = Order(dve, order_s, t, 2)
                        order.start = order.start + start
                        dve.wait_ge(products, t + 1)
                        wait_from(dve, turned2, t - 1)
                        p = banks[2 + b][0:P, 0:2 * KV].rearrange("p (a n) -> p a n", a=2)
                        order.then(v.tensor_scalar(z[:, b, :, :], p[:, :, 128:KV], 1e-6, None, ALU.add))
                        order.then(v.reciprocal(z[:, b, :, :], z[:, b, :, :]))
                        for a in range(2):
                            v.tensor_tensor(att[:, b, a * 128:a * 128 + 128].rearrange("p (h e) -> p h e", e=HC), p[:, a, 0:128].rearrange("p (h e) -> p h e", e=HC),
                                            z[:, b, a, :].unsqueeze(2).to_broadcast([P, 4, HC]), ALU.mult).then_inc(att_ready, 1)

                    def add(t, b):
                        dve.wait_ge(normed, t + 1)
                        dve.wait_ge(products2, t + 1)
                        v.tensor_tensor(H[:, t, :], H[:, t, :], banks[6 + b][0:P, 0:D], ALU.add).then_inc(added, 1)

                    def use(t, b):
                        dve.wait_ge(added, t + 1)
                        v.bn_stats(c.stats[:, t, :], H[:, t, :])
                        v.tensor_tensor(c.X[:, t, :], c.X[:, t, :], H[:, t, :], ALU.add)
                    over_tiles(dve, (divide, 3), (add, 1), use)

        with ExitStack() as s3:
            def ub(name, shape, dt=F32):
                return c.sb(s3, "atc_" + name, shape, dt)

            score, peak, msg, part = ub("score", [P, WIN, GH]), ub("peak", [P, WIN]), ub("msg", [P, WIN, GD]), ub("part", [P, WIN, GD])
            rs, w_n2, g = ub("rs", [P, WIN]), ub("w_n2", [P, D]), ub("g", [P, 2, D])
            scaled = ub("scaled", [P, 2, D])
            landed, order_s, s_ready, exped, ms_ready, rooted, scaled_ready, g_ready, msg_added, stats_made, added, var_ready, std_ready, rs_ready = c.sem(
                *("atc_" + n for n in ("landed", "order", "s_ready", "exped", "ms", "rooted", "scaled_ready", "g_ready", "msg_added", "stats_made", "added", "var", "std", "rs_ready")))
            with nc.Block() as block:
                @block.sync
                def _(sp):
                    sp.dma_start(w_n2[:, :], row_bcast(A["L1_mix_w_norm2"], P)).then_inc(landed, 16)

                @block.vector
                def _(dve):
                    v, order = nc.vector, Order(dve, order_s)
                    m0, s0, m1, s1 = (c.stats[:, :, i] for i in (1, 2, 4, 5))
                    a, b_, s = (c.fin[:, i, :] for i in range(3))
                    order.then(v.tensor_tensor(a, m0, m0, ALU.mult))
                    order.then(v.tensor_tensor(b_, m1, m1, ALU.mult))
                    order.then(v.tensor_tensor(a, a, b_, ALU.add))
                    order.then(v.tensor_tensor(s, s0, s1, ALU.add))
                    order.then(v.tensor_scalar(a, a, 0.5, RMS_EPS, ALU.mult, ALU.add))
                    v.scalar_tensor_tensor(out=rs[:, :], in0=s, scalar=1.0 / D, in1=a, op0=ALU.mult, op1=ALU.add).then_inc(ms_ready, 1)
                    dve.wait_ge(rooted, 1)
                    v.reciprocal(rs[:, :], rs[:, :]).then_inc(rs_ready, 1)
                    order.then(v.tensor_tensor(score[:, :, :], AL[:, :, :], XT[:, :, GD * GH:XTW], ALU.add))
                    order.then(v.scalar_tensor_tensor(out=score[:, :, :], in0=score[:, :, :], scalar=0.01, in1=score[:, :, :], op0=ALU.mult, op1=ALU.max))
                    order.then(v.tensor_reduce(peak[:, :], score[:, :, :], AX.X, ALU.max))
                    v.tensor_tensor(score[:, :, :], score[:, :, :], peak[:, :].unsqueeze(2).to_broadcast([P, WIN, GH]), ALU.subtract).then_inc(s_ready, 1)
                    dve.wait_ge(exped, 1)
                    order.then(v.tensor_reduce(peak[:, :], score[:, :, :], AX.X, ALU.add))
                    order.then(v.reciprocal(peak[:, :], peak[:, :]))
                    order.then(v.tensor_tensor(score[:, :, :], score[:, :, :], peak[:, :].unsqueeze(2).to_broadcast([P, WIN, GH]), ALU.mult))
                    for h in range(GH):
                        out = msg if h == 0 else part
                        order.then(v.tensor_tensor(out[:, :, :], XT[:, :, h * GD:(h + 1) * GD], score[:, :, h:h + 1].to_broadcast([P, WIN, GD]), ALU.mult))
                        if h:
                            order.then(v.tensor_tensor(msg[:, :, :], msg[:, :, :], part[:, :, :], ALU.add))

                    def add_msg(t, b):
                        x = c.X[:, t, :].rearrange("p (h d) -> p h d", h=GH)
                        v.tensor_tensor(x, x, msg[:, t, :].unsqueeze(1).to_broadcast([P, GH, GD]), ALU.add).then_inc(msg_added, 1)

                    def add_g(t, b):
                        dve.wait_ge(msg_added, t + 1)
                        dve.wait_ge(g_ready, t + 1)
                        v.tensor_tensor(c.X[:, t, :], c.X[:, t, :], g[:, b, :], ALU.add).then_inc(added, 1)

                    def stats(t, b):
                        dve.wait_ge(added, t + 1)
                        v.bn_stats(c.stats[:, t, :], c.X[:, t, :]).then_inc(stats_made, 1)
                    over_tiles(dve, (add_msg, 2), (add_g, 1), stats)
                    dve.wait_ge(stats_made, WIN)
                    c.finish_stats(order, var_ready, std_ready)

                @block.gpsimd
                def _(pool):
                    def scale(t, b):
                        pool.wait_ge(scaled_ready, t + 1)
                        wait_from(pool, added, t - 1)
                        nc.gpsimd.tensor_tensor(g[:, b, :], scaled[:, b, :], w_n2[:, :], ALU.mult).then_inc(g_ready, 1)
                    pool.wait_ge(landed, 16)
                    over_tiles(pool, scale)

                @block.scalar
                def _(act):
                    act.wait_ge(ms_ready, 1)
                    nc.scalar.activation(rs[:, :], rs[:, :], ACT.Sqrt).then_inc(rooted, 1)
                    act.wait_ge(s_ready, 1)
                    nc.scalar.activation(score[:, :, :], score[:, :, :], ACT.Exp).then_inc(exped, 1)

                    def scale(t, b):
                        wait_from(act, g_ready, t - 1)
                        nc.scalar.activation(scaled[:, b, :], H[:, t, :], ACT.Copy, scale=col(rs, t)).then_inc(scaled_ready, 1)
                    act.wait_ge(rs_ready, 1)
                    over_tiles(act, scale)
                    c.root(act, var_ready, std_ready)


def router_stage(c, pos, expert_of, share, weights_landed, load_weights, table_xs):
    nc, A, banks = c.nc, c.A, c.banks
    picks_n = PICKS * WIN
    with ExitStack() as scope:
        def sb(name, shape, dt=F32):
            return c.sb(scope, "ro_" + name, shape, dt)

        HN, h, xT = sb("HN", [P, WIN, D]), sb("h", [P, 2, D]), sb("xT", [128, 2, 2, P])
        affine = sb("affine", [128, 2, 2])
        w_r, b_r = sb("w_r", [128, 2, EXPERTS]), sb("b_r", [P, EXPERTS])
        logit, top, index = sb("logit", [P, 2, EXPERTS]), sb("top", [P, 2, 8]), sb("index", [P, 2, 8], U32)
        tops, picks = sb("tops", [P, PICKS, WIN]), sb("picks", [P, PICKS, WIN])
        mask, scan, zero = (sb(n, [P, EXPERTS, picks_n]) for n in ("mask", "scan", "zero"))
        counts, ntile, offset, place = sb("counts", [P, EXPERTS]), sb("ntile", [P, EXPERTS]), sb("offset", [P, EXPERTS]), sb("place", [P, picks_n])
        ends = sb("ends", [P, EXPERTS + 1])
        ended = sb("ended", [1, TOKEN_TILES])
        passed_e = sb("passed_e", [1, TOKEN_TILES, EXPERTS - 1])
        (landed, order_s, h_ready, turned, t_ready, kept, logits, late_s, gap_ready, exped, counted, summed, pos_ready, scattered, passed, made) = c.sem(
            *("ro_" + n for n in ("landed", "order", "h_ready", "turned", "t_ready", "kept", "logits", "late", "gap", "exped",
                                  "counted", "summed", "pos_ready", "scattered", "passed", "made")))
        with nc.Block() as block:
            @block.sync
            def _(sp):
                with nc.allow_non_contiguous_dma(reason="512 floats, once"):
                    for i, n in enumerate(("L1_ffn_gamma", "L1_ffn_beta")):
                        sp.dma_start(affine[:, i, :], A[n].rearrange("(k p) -> p k", p=128)).then_inc(landed, 16)
                sp.dma_start(w_r[:, :, :], A["L1_ffn_Wr"].rearrange("(k p) n -> p k n", k=2)).then_inc(landed, 16)
                sp.dma_start(b_r[:, :], row_bcast(A["L1_ffn_br"], P)).then_inc(landed, 16)
                load_weights(sp, weights_landed)

            @block.vector
            def _(dve):
                v = nc.vector

                def make_h(t, b):
                    wait_from(dve, kept, t - 1)
                    wait_from(dve, turned, t - 1)
                    c.normalised(h[:, b, :], t).then_inc(h_ready, 1)

                def best(t, b):
                    order = Order(dve, order_s, t, 5)
                    dve.wait_ge(logits, t + 1)
                    order.then(v.tensor_tensor(logit[:, b, :], banks[2 + b][0:P, 0:EXPERTS], b_r[:, :], ALU.add))
                    dve.sem_inc(passed, 1)
                    order.then(v.max(top[:, b, :], logit[:, b, :]))
                    dve.sem_inc(passed, 1)
                    order.then(v.max_index(index[:, b, :], top[:, b, :], logit[:, b, :]))
                    order.then(v.tensor_scalar(tops[:, :, bass.ds(t, 1)].rearrange("p k o -> p (k o)"), top[:, b, 0:2], 1.0, None, ALU.mult))
                    order.then(v.tensor_scalar(picks[:, :, bass.ds(t, 1)].rearrange("p k o -> p (k o)"), index[:, b, 0:2], 1.0, None, ALU.mult))
                v.memset(zero[:, :, :], 0.0).then_inc(made, 1)
                dve.wait_ge(landed, 64)
                over_tiles(dve, (make_h, 2), best)
                order = Order(dve, late_s)
                wide = [P, EXPERTS, picks_n]
                of_pick = picks[:, :, :].rearrange("p k t -> p (k t)").unsqueeze(1).to_broadcast(wide)
                order.then(v.tensor_tensor(mask[:, :, :], c.iota_f[0:P, 0:EXPERTS].unsqueeze(2).to_broadcast(wide), of_pick, ALU.is_equal))
                v.tensor_reduce(counts[:, :], mask[:, :, :], AX.X, ALU.add).then_inc(counted, 1)
                v.tensor_tensor(share[:, 0, :], tops[:, 1, :], tops[:, 0, :], ALU.subtract).then_inc(gap_ready, 1)
                dve.wait_ge(made, 1)
                flat = "p e k -> p (e k)"
                order.then(v.tensor_tensor_scan(scan[:, :, :].rearrange(flat), mask[:, :, :].rearrange(flat), zero[:, :, :].rearrange(flat), 0.0, ALU.add, ALU.add))
                dve.wait_ge(summed, 1)
                totals, before = banks[4][0:P, 0:EXPERTS], banks[5][0:P, 0:EXPERTS]
                order.then(v.tensor_scalar(ntile[:, :], totals, 1.0 / SLOT, (SLOT / 2 - 0.5) / SLOT, ALU.mult, ALU.add))
                order.then(v.tensor_scalar(ntile[:, :], ntile[:, :], ROUND, ROUND, ALU.add, ALU.subtract))
                order.then(v.memset(ends[:, 0:1], 0.0))
                order.then(v.tensor_tensor_scan(ends[:, 1:EXPERTS + 1], ntile[:, :], zero[:, 0, 0:EXPERTS], 0.0, ALU.add, ALU.add))
                order.then(v.scalar_tensor_tensor(out=offset[:, :], in0=ends[:, 0:EXPERTS], scalar=float(SLOT), in1=before, op0=ALU.mult, op1=ALU.add))
                order.then(v.tensor_scalar(offset[:, :], offset[:, :], -1.0, None, ALU.add))
                order.then(v.tensor_tensor(offset[:, 1:EXPERTS], offset[:, 1:EXPERTS], scan[:, 0:EXPERTS - 1, picks_n - 1], ALU.subtract))
                order.then(v.tensor_tensor(scan[:, :, :], scan[:, :, :], offset[:, :].unsqueeze(2).to_broadcast(wide), ALU.add))
                order.then(v.tensor_tensor(scan[:, :, :], scan[:, :, :], mask[:, :, :], ALU.mult))
                order.then(v.tensor_reduce(place[:, :], scan[:, :, :].rearrange("p e k -> p k e"), AX.X, ALU.add))
                v.tensor_copy(pos[:, :], place[:, :]).then_inc(pos_ready, 1)
                shape = [1, TOKEN_TILES, EXPERTS - 1]
                order.then(v.tensor_tensor(passed_e[:, :, :], c.iota_f[0:1, 0:TOKEN_TILES].unsqueeze(2).to_broadcast(shape),
                                           ends[0:1, 1:EXPERTS].unsqueeze(1).to_broadcast(shape), ALU.is_ge))
                order.then(v.tensor_reduce(ended[:, :], passed_e[:, :, :], AX.X, ALU.add))
                order.then(v.tensor_copy(expert_of[:, :], ended[:, :]))
                dve.wait_ge(exped, 1)
                order.then(v.tensor_scalar(share[:, 0, :], share[:, 1, :], 1.0, None, ALU.add))
                order.then(v.reciprocal(share[:, 0, :], share[:, 0, :]))
                order.then(v.tensor_tensor(share[:, 1, :], share[:, 1, :], share[:, 0, :], ALU.mult))

            @block.gpsimd
            def _(pool):
                def keep(t, b):
                    pool.wait_ge(h_ready, t + 1)
                    nc.gpsimd.tensor_copy(HN[:, t, :], h[:, b, :]).then_inc(kept, 1)
                over_tiles(pool, keep)
                pool.wait_ge(pos_ready, 1)
                pool.wait_ge(kept, WIN)
                for i in range(picks_n):
                    nc.gpsimd.indirect_dma_start(table_xs, bass.IndirectOffsetOnAxis(ap=pos[:, i:i + 1], axis=0), HN[:, i % WIN, :], None).then_inc(scattered, 16)
                pool.wait_ge(scattered, 16 * picks_n)

            @block.scalar
            def _(act):
                def copy_t(t, b):
                    act.wait_ge(turned, t + 1)
                    wait_from(act, logits, t - 1)
                    for k in range(2):
                        nc.scalar.activation(xT[:, b, k, :], banks[b][:, k * 128:k * 128 + P], ACT.Identity,
                                             bias=affine[:, 1, k:k + 1], scale=affine[:, 0, k:k + 1]).then_inc(t_ready, 1)
                act.wait_ge(landed, 64)
                over_tiles(act, copy_t)
                act.wait_ge(gap_ready, 1)
                nc.scalar.activation(share[:, 1, :], share[:, 0, :], ACT.Exp).then_inc(exped, 1)

            @block.tensor
            def _(pe):
                def turn(t, b):
                    pe.wait_ge(h_ready, t + 1)
                    wait_from(pe, t_ready, 2 * t - 2)
                    for k in range(2):
                        last = nc.tensor.transpose(banks[b][:, k * 128:k * 128 + P], h[:, b, k * 128:(k + 1) * 128], c.ident[0:P, 0:P])
                    last.then_inc(turned, 1)

                def route(t, b):
                    pe.wait_ge(t_ready, 2 * t + 2)
                    wait_from(pe, order_s, 5 * t - 9)
                    for k in range(2):
                        last = nc.tensor.matmul(banks[2 + b][0:P, 0:EXPERTS], xT[:, b, k, :], w_r[:, k, :], start=(k == 0), stop=(k == 1))
                    last.then_inc(logits, 1)
                pe.wait_ge(landed, 64)
                over_tiles(pe, (turn, 1), route)
                pe.wait_ge(counted, 1)
                nc.tensor.matmul(banks[4][0:P, 0:EXPERTS], c.ones[0:P, 0:P], counts[:, :], start=True, stop=True)
                nc.tensor.matmul(banks[5][0:P, 0:EXPERTS], c.tri[0:P, 0:P], counts[:, :], start=True, stop=True).then_inc(summed, 1)


def expert_stage(c, table_xs):
    nc, A, banks = c.nc, c.A, c.banks
    KH = HID // 128
    table_ys = nc.dram_tensor("table_ys", [TOKEN_TILES * SLOT, D], F32, kind="Internal").ap()
    xs_tiles, ys_tiles = (t.rearrange("(j p) d -> p j d", p=SLOT) for t in (table_xs, table_ys))
    with ExitStack() as scope:
        def sb(name, shape, dt=F32):
            return c.sb(scope, "ex_" + name, shape, dt)

        w1, w2 = sb("w1", [128, EXPERTS, 2, HID]), sb("w2", [128, EXPERTS, KH, D])
        b1, b2 = sb("b1", [SLOT, EXPERTS * HID]), sb("b2", [SLOT, EXPERTS * D])
        affine = sb("affine", [128, 2, 2])
        pos, expert_of = sb("pos", [P, PICKS * WIN], I32), sb("expert_of", [1, TOKEN_TILES], I32)
        share = sb("share", [P, PICKS, WIN])
        weights_landed = c.sem("ex_weights")
        WEIGHTS = 2 * EXPERTS + 4

        def load_weights(sp, s):
            for e in range(EXPERTS):
                sp.dma_start(w1[:, e, :, :], A["L1_ffn_W1"][e].rearrange("(k p) n -> p k n", k=2)).then_inc(s, 16)
                sp.dma_start(w2[:, e, :, :], A["L1_ffn_W2"][e].rearrange("(k p) n -> p k n", k=KH)).then_inc(s, 16)
            for b, n in ((b1, "L1_ffn_b1"), (b2, "L1_ffn_b2")):
                sp.dma_start(b[:, :], row_bcast(A[n].rearrange("e h -> (e h)"), SLOT)).then_inc(s, 16)
            with nc.allow_non_contiguous_dma(reason="512 floats, once"):
                for i, n in enumerate(("L1_ffn_gamma", "L1_ffn_beta")):
                    sp.dma_start(affine[:, i, :], A[n].rearrange("(k p) -> p k", p=128)).then_inc(s, 16)
        router_stage(c, pos, expert_of, share, weights_landed, load_weights, table_xs)

        with ExitStack() as s1:
            def tb(name, shape, dt=F32):
                return c.sb(s1, "ex_" + name, shape, dt)

            xs, xT = tb("xs", [SLOT, 2, D]), tb("xT", [128, 2, 2, SLOT])
            hid, hT, y = tb("hid", [SLOT, 2, HID]), tb("hT", [128, 2, KH, SLOT]), tb("y", [SLOT, 2, D])
            turned, t_ready, up_done, biased, gelu_done, h_turned, ht_ready, down_done, y_ready = c.sem(
                *("ex_" + n for n in ("turned", "t_ready", "up_done", "biased", "gelu_done", "h_turned", "ht_ready", "down_done", "y_ready")))
            loaded, stored = ([c.sem(f"ex_{n}{i}") for i in range(2)] for n in ("loaded", "stored"))

            def expert(engine, j):
                return engine.value_load(expert_of[0:1, bass.ds(j, 1)], min_val=0, max_val=EXPERTS - 1)

            with nc.Block() as block:
                @block.sync
                def _(sp):
                    def load(j, b):
                        wait_from(sp, turned, j - 1)
                        sp.dma_start(xs[:, b, :], xs_tiles[:, j, :]).then_inc(loaded[b], 16)

                    def store(j, b):
                        sp.wait_ge(y_ready, j + 1)
                        sp.dma_start(ys_tiles[:, j, :], y[:, b, :]).then_inc(stored[b], 16)
                    over_tiles(sp, (load, 5), store, count=TOKEN_TILES)
                    for s in stored:
                        sp.wait_ge(s, 16 * (TOKEN_TILES // 2))

                @block.tensor
                def _(pe):
                    mm = nc.tensor.matmul

                    def turn_x(j, b):
                        pe.wait_ge(loaded[b], 8 * j - 8 * b + 16)
                        wait_from(pe, t_ready, 2 * j - 2)
                        for k in range(2):
                            last = nc.tensor.transpose(banks[b][:, k * 128:k * 128 + SLOT], xs[:, b, k * 128:(k + 1) * 128], c.ident[:, :])
                        last.then_inc(turned, 1)

                    def up(j, b):
                        e = expert(pe, j)
                        pe.wait_ge(t_ready, 2 * j + 2)
                        wait_from(pe, biased, j - 1)
                        for k in range(2):
                            last = mm(banks[2 + b][:, :], xT[:, b, k, :], w1[:, bass.ds(e, 1), k, :].rearrange("p o n -> p (o n)"), start=(k == 0), stop=(k == 1))
                        last.then_inc(up_done, 1)

                    def turn_h(j, b):
                        pe.wait_ge(gelu_done, j + 1)
                        wait_from(pe, ht_ready, j - 1)
                        for k in range(KH):
                            last = nc.tensor.transpose(banks[4 + b][:, k * SLOT:(k + 1) * SLOT], hid[:, b, k * 128:(k + 1) * 128], c.ident[:, :])
                        last.then_inc(h_turned, 1)

                    def down(j, b):
                        e = expert(pe, j)
                        pe.wait_ge(ht_ready, j + 1)
                        wait_from(pe, y_ready, j - 1)
                        for k in range(KH):
                            last = mm(banks[6 + b][:, 0:D], hT[:, b, k, :], w2[:, bass.ds(e, 1), k, :].rearrange("p o n -> p (o n)"), start=(k == 0), stop=(k == KH - 1))
                        last.then_inc(down_done, 1)
                    pe.wait_ge(weights_landed, 16 * WEIGHTS)
                    over_tiles(pe, (up, 2), (turn_h, 1), (turn_x, 3), down, count=TOKEN_TILES)

                @block.scalar
                def _(act):
                    def copy_x(j, b):
                        act.wait_ge(turned, j + 1)
                        wait_from(act, up_done, j - 1)
                        for k in range(2):
                            nc.scalar.activation(xT[:, b, k, :], banks[b][:, k * 128:k * 128 + SLOT], ACT.Identity,
                                                 bias=affine[:, 1, k:k + 1], scale=affine[:, 0, k:k + 1]).then_inc(t_ready, 1)

                    def gelu(j, b):
                        act.wait_ge(biased, j + 1)
                        nc.scalar.activation(hid[:, b, :], hid[:, b, :], ACT.Gelu).then_inc(gelu_done, 1)

                    def copy_h(j, b):
                        act.wait_ge(h_turned, j + 1)
                        wait_from(act, down_done, j - 1)
                        nc.scalar.activation(hT[:, b, :, :].rearrange("p k n -> p (k n)"), banks[4 + b][:, :], ACT.Copy).then_inc(ht_ready, 1)
                    act.wait_ge(weights_landed, 16 * WEIGHTS)
                    over_tiles(act, (copy_h, 1), (copy_x, 3), (gelu, 2), count=TOKEN_TILES)

                @block.vector
                def _(dve):
                    v = nc.vector

                    def add_b1(j, b):
                        e = expert(dve, j)
                        dve.wait_ge(up_done, j + 1)
                        wait_from(dve, h_turned, j - 1)
                        v.tensor_tensor(hid[:, b, :], b1[:, bass.ds(e * HID, HID)], banks[2 + b][:, :], ALU.add).then_inc(biased, 1)

                    def add_b2(j, b):
                        e = expert(dve, j)
                        dve.wait_ge(down_done, j + 1)
                        if not isinstance(j, int) or j >= 2:
                            dve.wait_ge(stored[b], j * 8 - 8 * b)
                        v.tensor_tensor(y[:, b, :], b2[:, bass.ds(e * D, D)], banks[6 + b][:, 0:D], ALU.add).then_inc(y_ready, 1)
                    dve.wait_ge(weights_landed, 16 * WEIGHTS)
                    over_tiles(dve, (add_b1, 2), add_b2, count=TOKEN_TILES)

        with ExitStack() as s2:
            GOT, PART = 10, 5
            got = c.sb(s2, "ex_got", [P, GOT, D])
            gathered = [c.sem(f"ex_gathered{i}") for i in range(GOT)]
            added, out_stored = c.sem("ex_added", "ex_out_stored")
            tokens = [(t, k) for g in range(0, WIN, PART) for k in range(PICKS) for t in range(g, g + PART)]
            with nc.Block() as block:
                @block.gpsimd
                def _(pool):
                    for i, (t, k) in enumerate(tokens):
                        wait_from(pool, added, i - GOT + 1)
                        nc.gpsimd.indirect_dma_start(got[:, i % GOT, :], None, table_ys,
                                                     bass.IndirectOffsetOnAxis(ap=pos[:, k * WIN + t:k * WIN + t + 1], axis=0)).then_inc(gathered[i % GOT], 16)

                @block.vector
                def _(dve):
                    for i, (t, k) in enumerate(tokens):
                        dve.wait_ge(gathered[i % GOT], 16 * (i // GOT + 1))
                        if k:
                            dve.wait_ge(added, i - PART + 1)
                        x = c.X[:, t, :]
                        nc.vector.scalar_tensor_tensor(out=x, in0=got[:, i % GOT, :], scalar=share[:, k, t:t + 1], in1=x, op0=ALU.mult, op1=ALU.add).then_inc(added, 1)

                @block.sync
                def _(sp):
                    out = c.out.rearrange("(p t) d -> p t d", t=WIN)
                    for g in range(0, WIN, PART):
                        sp.wait_ge(added, PICKS * (g + PART))
                        sp.dma_start(out[:, g:g + PART, :], c.X[:, g:g + PART, :]).then_inc(out_stored, 16)
                    sp.wait_ge(out_stored, 16 * (WIN // PART))


def build(nc, A, out):
    with ExitStack() as keep:
        c = Chip(nc, A, out, keep)
        table_y = nc.dram_tensor("table_y", [RELS * N, D], F32, kind="Internal").ap()
        table_xs = nc.dram_tensor("table_xs", [TOKEN_TILES * SLOT, D], F32, kind="Internal").ap()
        load_stage(c, table_xs)
        with ExitStack() as graph:
            mixer = c.sb(graph, "mixer", [128, 2, D // 2])
            mix0_stage(c, mixer)
            slot_row = c.sb(graph, "slot_row", [128, TILES], I32)
            slot_dst = c.sb(graph, "slot_dst", [128, TILES])
            slot_win = c.sb(graph, "slot_win", [1, TILES], I32)
            sort_stage(c, slot_row, slot_dst, slot_win)
            aggr, selfp = c.sb(graph, "aggr", [P, WIN, D]), c.sb(graph, "selfp", [P, WIN, D])
            for layer in range(LAYERS):
                message_stage(c, layer, aggr, selfp, mixer, table_y)
                gather_stage(c, layer, aggr, table_y, slot_row, slot_dst, slot_win)
            gnn_out_stage(c, aggr, selfp)
        c.recycle()
        slice_stage(c)
        c.recycle()
        attention_stage(c)
        c.recycle()
        expert_stage(c, table_xs)


def constants():
    import numpy as np
    head = np.arange(128) // HC
    return {
        "c_ident": np.eye(128, dtype=np.float32),
        "c_tri": np.triu(np.ones((128, 128), np.float32), 1),
        "c_iota": np.tile(np.arange(TILES, dtype=np.float16), (128, 1)),
        "c_iota_f": np.tile(np.arange(128, dtype=np.float32), (128, 1)),
        "c_blocks": (head[:, None] == head[None, :]).astype(np.float32),
        "c_heads": (head[:, None] == np.arange(4)[None, :]).astype(np.float32),
    }


def kernel(**inputs):
    import numpy as np
    import concourse.bacc as bacc
    from concourse.bass_utils import run_bass_kernel_spmd

    nc = bacc.Bacc("TRN2", target_bir_lowering=False, num_devices=1)
    arrays, handles = {}, {}
    for name, a in {**inputs, **constants()}.items():
        a = np.ascontiguousarray(a)
        arrays[f"in_{name}"] = a
        handles[name] = nc.dram_tensor(f"in_{name}", a.shape, mybir.dt.from_np(a.dtype), kind="ExternalInput").ap()
    out = nc.dram_tensor("out_0", (N, D), F32, kind="ExternalOutput").ap()
    build(nc, handles, out)
    return run_bass_kernel_spmd(nc, [arrays], core_ids=[0]).results[0]["out_0"]
```

```python
from contextlib import ExitStack

import concourse.bass as bass
from concourse import mybir

ALU = mybir.AluOpType
ACT = mybir.ActivationFunctionType
AX = mybir.AxisListType
F32 = mybir.dt.float32
F16 = mybir.dt.float16
I32 = mybir.dt.int32
U32 = mybir.dt.uint32

N = 3125
D = 256
E = 50000
WIN = 25
P = N // WIN
RELS = 2
LAYERS = 3
EC = E // P
SLOT = 128
TILES = (E + WIN * (SLOT - 1)) // SLOT
RING = 16
HALF = RING // 2
QUAD = 4
TILES += -TILES % RING
HEADS = 8
HC = D // HEADS
SD = 64
INNER = HEADS * SD
GH, GD = 4, 64
EXPERTS, HID = 8, 512
PICKS = 2
TOKEN_TILES = (PICKS * N + EXPERTS * (SLOT - 1)) // SLOT
TOKEN_TILES += TOKEN_TILES % 2
LN_EPS = 1e-5
ZEROS = 1024
RMS_EPS = 1e-6
ROUND = 1.5 * 2 ** 23


class Order:

    def __init__(self, engine, semaphore, tile=0, per=0):
        self.engine, self.semaphore, self.start, self.per, self.k = engine, semaphore, tile * per, per, 0

    def then(self, instruction):
        instruction.then_inc(self.semaphore, 1)
        self.k += 1
        self.engine.wait_ge(self.semaphore, self.start + self.k)

    def close(self):
        assert self.k == self.per, (self.k, self.per)


def wait_from(engine, semaphore, value):
    if isinstance(value, int) and value <= 0:
        return
    engine.wait_ge(semaphore, value)


def over_tiles(engine, *steps, count=WIN):
    steps = [s if isinstance(s, tuple) else (s, 0) for s in steps]
    most = max(lead for _, lead in steps)

    def round_(t, b, python):
        for step, lead in steps:
            if not python or 0 <= t + lead < count:
                step(t + lead, (b + lead) % 2)

    for t in range(-most, 2):
        round_(t, t % 2, True)
    pairs = (count - most - 2) // 2
    with engine.Fori(2, 2 + 2 * pairs - 1, 2) as i:
        round_(i, 0, False)
        round_(i + 1, 1, False)
    for t in range(2 + 2 * pairs, count):
        round_(t, t % 2, True)


def col(ap, t):
    return ap[:, bass.ds(t, 1)]


class Chip:

    def __init__(self, nc, A, out, keep):
        self.nc, self.A, self.out, self.keep = nc, A, out, keep
        self.X = self.sb(keep, "X", [P, WIN, D])
        self.ident = self.sb(keep, "ident", [128, 128])
        self.tri = self.sb(keep, "tri", [128, 128])
        self.ones = self.sb(keep, "ones", [128, 128])
        self.zeros = self.sb(keep, "zeros", [128, ZEROS])
        self.iota = self.sb(keep, "iota", [128, TILES], F16)
        self.iota_f = self.sb(keep, "iota_f", [128, 128])
        self.blocks = self.sb(keep, "blocks", [128, 128])
        self.heads = self.sb(keep, "heads", [128, 4])
        self.rstd = self.sb(keep, "rstd", [P, WIN])
        self.nmr = self.sb(keep, "nmr", [P, WIN])
        self.stats = self.sb(keep, "stats", [P, WIN, 6])
        self.fin = self.sb(keep, "fin", [P, 4, WIN])
        self.banks = [keep.enter_context(nc.psum_tensor(f"bank{i}", [128, 512], F32)) for i in range(8)]
        self.sems = []

    def sb(self, scope, name, shape, dt=F32):
        return scope.enter_context(self.nc.sbuf_tensor(name, shape, dt))

    def sem(self, *names):
        got = [self.nc.alloc_semaphore(name=n) for n in names]
        self.sems += got
        return got[0] if len(got) == 1 else got

    def recycle(self):
        self.nc.clear_and_free_semaphores(self.sems)
        self.nc.all_engine_barrier()
        self.sems = []

    def normalised(self, out, t):
        return self.nc.vector.tensor_scalar(out, self.X[:, t, :], col(self.rstd, t), col(self.nmr, t), ALU.mult, ALU.add)

    def finish_stats(self, order, var_ready, std_ready, base=0):
        v, fin = self.nc.vector, self.fin
        m0, s0, m1, s1 = (self.stats[:, :, i] for i in (1, 2, 4, 5))
        mean2, d, s, var = (fin[:, i, :] for i in range(4))
        order.then(v.tensor_tensor(mean2, m0, m1, ALU.add))
        order.then(v.tensor_tensor(d, m0, m1, ALU.subtract))
        order.then(v.tensor_tensor(s, s0, s1, ALU.add))
        order.then(v.tensor_tensor(d, d, d, ALU.mult))
        order.then(v.tensor_scalar(d, d, 0.25, LN_EPS, ALU.mult, ALU.add))
        order.then(v.scalar_tensor_tensor(out=var, in0=s, scalar=1.0 / D, in1=d, op0=ALU.mult, op1=ALU.add))
        v.tensor_scalar(mean2, mean2, -0.5, None, ALU.mult).then_inc(var_ready, 1)
        order.engine.wait_ge(std_ready, 1)
        order.then(v.reciprocal(self.rstd[:, :], self.rstd[:, :]))
        order.engine.wait_ge(var_ready, 1)
        order.then(v.tensor_tensor(self.nmr[:, :], mean2, self.rstd[:, :], ALU.mult))

    def root(self, act, var_ready, std_ready):
        act.wait_ge(var_ready, 1)
        self.nc.scalar.activation(self.rstd[:, :], self.fin[:, 3, :], ACT.Sqrt).then_inc(std_ready, 1)


def tile_stats(c, dve, order, source):
    for t in range(WIN):
        c.nc.vector.bn_stats(c.stats[:, t, :], source[:, t, :]).then_inc(order.semaphore, 1)
    order.k += WIN
    dve.wait_ge(order.semaphore, order.start + order.k)


def row_bcast(vector, rows):
    return vector.unsqueeze(0).to_broadcast([rows, vector.shape[0]])


def load_stage(c, sort, table_xs):
    nc, A = c.nc, c.A
    x_landed, landed, order_s, var_ready, std_ready, zeroed = c.sem("x_landed", "consts_landed", "load_order", "load_var", "load_std", "load_zeroed")
    c.filled = c.sem("table_filled")
    with nc.Block() as block:
        @block.gpsimd
        def _(pool):
            pool.dma_start(c.X[:, :, :], A["x"].rearrange("(p t) d -> p t d", t=WIN)).then_inc(x_landed, 16)

        @block.sync
        def _(sp):
            sort.load(sp)
            pairs = [(c.ident, "c_ident"), (c.tri, "c_tri"), (c.iota, "c_iota"), (c.iota_f, "c_iota_f"),
                     (c.blocks, "c_blocks"), (c.heads, "c_heads")]
            for buffer, name in pairs:
                sp.dma_start(buffer[:, :], A[name]).then_inc(landed, 16)
            sp.wait_ge(landed, 16 * len(pairs))
            sp.wait_ge(zeroed, 1)
            rows = table_xs.rearrange("(p j) d -> p (j d)", p=128)
            width = rows.shape[1] // ZEROS
            sp.dma_start(rows.rearrange("p (z w) -> p z w", w=ZEROS), c.zeros[:, :].unsqueeze(1).to_broadcast([128, width, ZEROS])).then_inc(c.filled, 16)

        @block.vector
        def _(dve):
            nc.vector.memset(c.ones[:, :], 1.0)
            nc.vector.memset(c.zeros[:, :], 0.0).then_inc(zeroed, 1)
            sort.count(dve)
            dve.wait_ge(x_landed, 16)
            order = Order(dve, order_s)
            tile_stats(c, dve, order, c.X)
            c.finish_stats(order, var_ready, std_ready)

        @block.tensor
        def _(pe):
            pe.wait_ge(landed, 96)
            pe.wait_ge(zeroed, 1)
            sort.sum_counts(pe)

        @block.scalar
        def _(act):
            c.root(act, var_ready, std_ready)


def mix0_stage(c, mixer):
    nc, A = c.nc, c.A
    PART = 5
    with ExitStack() as scope:
        def sb(*a):
            return c.sb(scope, *a)

        xn, xc, sq = (sb("mx_" + n, [P, 2, PART, D]) for n in ("xn", "xc", "sq"))
        neg_mean, rz = sb("mx_neg_mean", [P, 2, PART * HEADS]), sb("mx_rz", [P, 2, PART * HEADS])
        z = sb("mx_z", [P, 2, 2 * PART, 129])
        kcol = sb("mx_kcol", [128, 2, 2])
        vrow = sb("mx_vrow", [128, 2, D])
        u = sb("mx_u", [128, 2])
        srow = sb("mx_srow", [128, D])
        landed, order_s, xn_ready, xc_ready, sq_ready, ss_ready, std_ready, z_ready, z_used, zeroed, g_ready = c.sem(
            *("mx_" + n for n in ("landed", "order", "xn_ready", "xc_ready", "sq_ready", "ss_ready", "std_ready", "z_ready", "z_used", "zeroed", "g_ready")))
        PARTS = WIN // PART

        def by_head(buffer, g):
            return buffer[:, g % 2, :, :].rearrange("p t (h e) -> p (t h) e", h=HEADS)
        with nc.Block() as block:
            @block.sync
            def _(sp):
                with nc.allow_non_contiguous_dma(reason="512 floats, once"):
                    for i, n in enumerate(("L0_mix_kln_weight", "L0_mix_kln_bias")):
                        sp.dma_start(kcol[:, :, i], A[n].rearrange("(a h) o e -> (h o e) a", a=2)).then_inc(landed, 16)
                for i, n in enumerate(("L0_mix_vln_weight", "L0_mix_vln_bias")):
                    sp.dma_start(vrow[:, i, :], row_bcast(A[n].rearrange("h o e -> (h o e)"), 128)).then_inc(landed, 16)
                sp.wait_ge(c.filled, 16)

            @block.vector
            def _(dve):
                v = nc.vector
                v.memset(c.banks[0][:, :], 0.0).then_inc(zeroed, 1)
                v.memset(c.banks[1][:, :], 0.0).then_inc(zeroed, 1)
                v.memset(z[:, :, :, :], 1.0).then_inc(zeroed, 1)
                order = Order(dve, order_s)
                wide = [P, PART * HEADS, HC]

                def centre(g):
                    dve.wait_ge(xn_ready, PART * (g + 1))
                    mean = neg_mean[:, g % 2, :]
                    order.then(v.tensor_reduce(mean, by_head(xn, g), AX.X, ALU.add))
                    order.then(v.tensor_scalar(mean, mean, -1.0 / HC, None, ALU.mult))
                    v.tensor_tensor(by_head(xc, g), by_head(xn, g), mean.unsqueeze(2).to_broadcast(wide), ALU.add).then_inc(xc_ready, 1)

                def variance(g):
                    dve.wait_ge(sq_ready, g + 1)
                    order.then(v.tensor_reduce(rz[:, g % 2, :], by_head(sq, g), AX.X, ALU.add))
                    v.tensor_scalar(rz[:, g % 2, :], rz[:, g % 2, :], 1.0 / (HC - 1), None, ALU.mult).then_inc(ss_ready, 1)

                def divide(g):
                    dve.wait_ge(std_ready, g + 1)
                    order.then(v.tensor_scalar(rz[:, g % 2, :], rz[:, g % 2, :], LN_EPS, None, ALU.add))
                    order.then(v.reciprocal(rz[:, g % 2, :], rz[:, g % 2, :]))
                    wait_from(dve, z_used, PART * (g - 1))
                    v.tensor_tensor(z[:, g % 2, :, 0:128].rearrange("p a (h e) -> p a h e", e=HC), xc[:, g % 2, :, :].rearrange("p t (k h e) -> p (t k) h e", k=2, e=HC),
                                    rz[:, g % 2, :].rearrange("p (a h) -> p a h", h=4).unsqueeze(3).to_broadcast([P, 2 * PART, 4, HC]), ALU.mult).then_inc(z_ready, 1)
                dve.wait_ge(zeroed, 3)
                for g in range(PARTS + 2):
                    if 2 <= g:
                        divide(g - 2)
                    if g < PARTS:
                        centre(g)
                    if 1 <= g <= PARTS:
                        variance(g - 1)
                dve.wait_ge(g_ready, 1)
                dve.wait_ge(landed, 64)
                order.then(v.tensor_copy(srow[:, :], c.banks[1][:, 0:D]))
                for k in range(2):
                    gram, s_col = c.banks[0][:, 129 * k:129 * k + 128], c.banks[0][:, 129 * k + 128:129 * k + 129]
                    m, cols = mixer[:, k, :], slice(128 * k, 128 * k + 128)
                    kw, kb = kcol[:, k, 0:1], kcol[:, k, 1:2]
                    order.then(v.tensor_scalar(m, srow[:, cols], kb, None, ALU.mult))
                    order.then(v.scalar_tensor_tensor(out=m, in0=gram, scalar=kw, in1=m, op0=ALU.mult, op1=ALU.add))
                    order.then(v.tensor_tensor(m, m, vrow[:, 0, cols], ALU.mult))
                    order.then(v.tensor_scalar(u[:, 0:1], s_col, kw, None, ALU.mult))
                    order.then(v.scalar_tensor_tensor(out=u[:, 1:2], in0=kb, scalar=float(N), in1=u[:, 0:1], op0=ALU.mult, op1=ALU.add))
                    order.then(v.scalar_tensor_tensor(out=m, in0=vrow[:, 1, cols], scalar=u[:, 1:2], in1=m, op0=ALU.mult, op1=ALU.add))
                    order.then(v.scalar_tensor_tensor(out=m, in0=m, scalar=1.0 / N, in1=c.blocks[:, :], op0=ALU.mult, op1=ALU.mult))
                    order.then(v.tensor_tensor(m, m, c.ident[:, :], ALU.add))

            @block.scalar
            def _(act):
                def norm(g):
                    wait_from(act, xc_ready, g - 1)
                    for t in range(PART * g, PART * g + PART):
                        nc.scalar.activation(xn[:, g % 2, t % PART, :], c.X[:, t, :], ACT.Identity, scale=c.rstd[:, t:t + 1], bias=c.nmr[:, t:t + 1]).then_inc(xn_ready, 1)

                def square(g):
                    act.wait_ge(xc_ready, g + 1)
                    wait_from(act, ss_ready, g - 1)
                    nc.scalar.activation(sq[:, g % 2, :, :], xc[:, g % 2, :, :], ACT.Square).then_inc(sq_ready, 1)

                def root(g):
                    act.wait_ge(ss_ready, g + 1)
                    nc.scalar.activation(rz[:, g % 2, :], rz[:, g % 2, :], ACT.Sqrt).then_inc(std_ready, 1)
                norm(0)
                for g in range(PARTS):
                    if g + 1 < PARTS:
                        norm(g + 1)
                    square(g)
                    root(g)

            @block.tensor
            def _(pe):
                pe.wait_ge(zeroed, 3)
                for t in range(WIN):
                    g = t // PART
                    if t % PART == 0:
                        pe.wait_ge(z_ready, g + 1)
                    for k in range(2):
                        zk = z[:, g % 2, 2 * (t % PART) + k, :]
                        nc.tensor.matmul(c.banks[0][:, 129 * k:129 * k + 129], zk[:, 0:128], zk, start=False, stop=False, skip_group_check=True)
                        last = nc.tensor.matmul(c.banks[1][:, 128 * k:128 * k + 128], c.ones[0:P, :], zk[:, 0:128], start=False, stop=False, skip_group_check=True)
                    last.then_inc(z_used, 1)
                pe.wait_ge(z_used, WIN)
                pe.sem_inc(g_ready, 1)


class Sort:

    def __init__(self, c, scope, slot_win):
        self.c, self.slot_win = c, slot_win

        def sb(name, shape, dt=F32):
            return c.sb(scope, "so_" + name, shape, dt)

        self.masks = sb("masks", [P, WIN, EC], F16)
        self.raw = sb("raw", [P, 3, EC], I32)
        self.win, self.row, self.rank, self.code_hi, self.code_lo, self.tmp, self.tile_of, self.row_of = (
            sb(n, [P, EC])[:, :] for n in ("win", "row", "rank", "code_hi", "code_lo", "tmp", "tile_of", "row_of"))
        self.zero, self.ones = sb("zero", [P, WIN]), sb("ones", [P, 1])
        self.counts, self.ntile, self.base = sb("counts", [P, WIN]), sb("ntile", [P, WIN]), sb("base", [P, WIN])
        self.cum = sb("cum", [P, WIN + 1])
        self.landed, self.order_s, self.counted, self.summed, self.ranked, self.ntile_ready, self.passed_ready = c.sem(
            "so_landed", "so_order", "so_counted", "so_summed", "so_ranked", "so_ntile_ready", "so_passed_ready")
        self.ends, self.passed = sb("ends", [WIN, 2]), sb("passed", [WIN - 1, TILES])

    def load(self, sp):
        for i, n in enumerate(("dst", "src", "edge_type_2")):
            sp.dma_start(self.raw[:, i, :], self.c.A[n].rearrange("(p j) -> p j", j=EC)).then_inc(self.landed, 16)

    def count(self, dve):
        masks, raw, win, row, rank, code_hi, code_lo, tmp = self.masks, self.raw, self.win, self.row, self.rank, self.code_hi, self.code_lo, self.tmp
        zero, ones, counts = self.zero[:, :], self.ones, self.counts
        v, order = self.c.nc.vector, Order(dve, self.order_s)
        order.then(v.memset(zero, 0.0))
        order.then(v.memset(ones[:, :], 1.0))
        dve.wait_ge(self.landed, 48)
        order.then(v.tensor_copy(rank, raw[:, 0, :]))
        order.then(v.tensor_scalar(tmp, rank, 1.0 / WIN, -(WIN - 1) / 2 / WIN, ALU.mult, ALU.add))
        order.then(v.tensor_scalar(row, tmp, ROUND, ROUND, ALU.add, ALU.subtract))
        order.then(v.scalar_tensor_tensor(out=win, in0=row, scalar=-float(WIN), in1=rank, op0=ALU.mult, op1=ALU.add))
        order.then(v.tensor_copy(code_lo, raw[:, 1, :]))
        order.then(v.tensor_copy(tmp, raw[:, 2, :]))
        order.then(v.tensor_scalar(tmp, tmp, 0.0, float(N), ALU.not_equal, ALU.mult))
        order.then(v.tensor_tensor(code_lo, code_lo, tmp, ALU.add))
        order.then(v.tensor_scalar(tmp, code_lo, 1.0 / 8, -3.5 / 8, ALU.mult, ALU.add))
        order.then(v.tensor_scalar(code_hi, tmp, ROUND, ROUND, ALU.add, ALU.subtract))
        order.then(v.scalar_tensor_tensor(out=code_lo, in0=code_hi, scalar=-8.0, in1=code_lo, op0=ALU.mult, op1=ALU.add))
        order.then(v.tensor_scalar(code_lo, code_lo, 128.0, 1.0, ALU.mult, ALU.add))
        order.then(v.tensor_tensor(code_lo, code_lo, row, ALU.add))
        for w in range(WIN):
            v.tensor_scalar(masks[:, w, :], win, float(w), 0.0, ALU.is_equal, ALU.add,
                            accum_out=counts[:, w:w + 1]).then_inc(self.counted, 1)
        dve.wait_ge(self.counted, WIN)
        ntile, end = self.ends[:, 0:1], self.ends[:, 1:2]
        dve.wait_ge(self.summed, 1)
        order.then(v.tensor_scalar(ntile, self.c.banks[5][0:WIN, 0:1], 1.0 / SLOT, (SLOT / 2 - 0.5) / SLOT, ALU.mult, ALU.add))
        v.tensor_scalar(ntile, ntile, ROUND, ROUND, ALU.add, ALU.subtract).then_inc(self.ntile_ready, 1)
        dve.wait_ge(self.summed, 2)
        order.then(v.tensor_tensor(end, ntile, self.c.banks[4][0:WIN, 0:1], ALU.add))
        v.tensor_scalar(self.passed[:, :], self.c.iota[0:WIN - 1, :], self.ends[0:WIN - 1, 1:2], None, ALU.is_ge).then_inc(self.passed_ready, 1)
        dve.wait_ge(self.summed, 3)
        order.then(v.tensor_copy(self.slot_win[:, :], self.c.banks[3][0:1, 0:TILES]))
        self.steps = order.k

    def sum_counts(self, pe):
        mm, banks = self.c.nc.tensor.matmul, self.c.banks
        pe.wait_ge(self.counted, WIN)
        mm(banks[6][0:P, 0:WIN], self.c.ones[0:P, 0:P], self.counts[:, :], start=True, stop=True)
        mm(banks[7][0:P, 0:WIN], self.c.tri[0:P, 0:P], self.counts[:, :], start=True, stop=True)
        mm(banks[5][0:WIN, 0:1], self.counts[:, :], self.c.ones[0:P, 0:1], start=True, stop=True).then_inc(self.summed, 1)
        pe.wait_ge(self.ntile_ready, 1)
        mm(banks[4][0:WIN, 0:1], self.c.tri[0:WIN, 0:WIN], self.ends[:, 0:1], start=True, stop=True).then_inc(self.summed, 1)
        pe.wait_ge(self.passed_ready, 1)
        mm(banks[3][0:1, 0:TILES], self.c.ones[0:WIN - 1, 0:1], self.passed[:, :], start=True, stop=True).then_inc(self.summed, 1)

    def place(self, dve, scan):
        c, masks, rank, tmp, tile_of, row_of = self.c, self.masks, self.rank, self.tmp, self.tile_of, self.row_of
        zero, ones, ntile, base, cum = self.zero, self.ones, self.ntile, self.base, self.cum
        v, order = c.nc.vector, Order(dve, self.order_s)
        order.k = self.steps
        dve.wait_ge(self.summed, 1)
        totals, before = c.banks[6][0:P, 0:WIN], c.banks[7][0:P, 0:WIN]
        order.then(v.tensor_scalar(ntile[:, :], totals, 1.0 / SLOT, (SLOT / 2 - 0.5) / SLOT, ALU.mult, ALU.add))
        order.then(v.tensor_scalar(ntile[:, :], ntile[:, :], ROUND, ROUND, ALU.add, ALU.subtract))
        order.then(v.memset(cum[:, 0:1], 0.0))
        order.then(v.tensor_tensor_scan(cum[:, 1:WIN + 1], ntile[:, :], zero[:, :], 0.0, ALU.add, ALU.add))
        order.then(v.scalar_tensor_tensor(out=base[:, :], in0=cum[:, 0:WIN], scalar=float(SLOT), in1=before, op0=ALU.mult, op1=ALU.add))
        flat = "p w e -> p (w e)"
        order.then(v.tensor_tensor_scan(scan[:, :, :].rearrange(flat), masks[:, :, :].rearrange(flat), ones[:, 0:1].to_broadcast([P, WIN * EC]),
                                        0.0, ALU.add, ALU.mult))
        order.then(v.tensor_scalar(base[:, :], base[:, :], -1.0, None, ALU.add))
        order.then(v.tensor_tensor(base[:, 1:WIN], base[:, 1:WIN], scan[:, 0:WIN - 1, EC - 1], ALU.subtract))
        for w in range(WIN):
            v.scalar_tensor_tensor(out=scan[:, w, :], in0=scan[:, w, :], scalar=base[:, w:w + 1], in1=masks[:, w, :], op0=ALU.add, op1=ALU.mult).then_inc(self.ranked, 1)
        dve.wait_ge(self.ranked, WIN)
        order.then(v.tensor_reduce(rank, scan[:, :, :].rearrange("p w e -> p e w"), AX.X, ALU.add))
        order.then(v.tensor_scalar(tmp, rank, 1.0 / SLOT, -(SLOT - 1) / 2 / SLOT, ALU.mult, ALU.add))
        order.then(v.tensor_scalar(tile_of, tmp, ROUND, ROUND, ALU.add, ALU.subtract))
        order.then(v.scalar_tensor_tensor(out=row_of, in0=tile_of, scalar=-float(SLOT), in1=rank, op0=ALU.mult, op1=ALU.add))


def ranks_stage(c, sort, HT, table_y):
    with ExitStack() as scope:
        scan = c.sb(scope, "so_scan", [P, WIN, EC])
        sync, tensor, scalar, gpsimd = first_messages(c, scope, HT, table_y)
        with c.nc.Block() as block:
            @block.sync
            def _(sp):
                sync(sp)

            @block.tensor
            def _(pe):
                tensor(pe)

            @block.scalar
            def _(act):
                scalar(act)

            @block.gpsimd
            def _(pool):
                gpsimd(pool)

            @block.vector
            def _(dve):
                sort.place(dve, scan)


def move_stage(c, sort, slot_row, slot_dst):
    nc = c.nc
    with ExitStack() as scope:
        def sb(name, shape, dt=F32):
            return c.sb(scope, "mv_" + name, shape, dt)

        tile_of, row_of, code_hi, code_lo = sort.tile_of, sort.row_of, sort.code_hi, sort.code_lo
        G = 16
        lo16 = sb("lo16", [P, EC], F16)
        hot_row, hot_hi, hot_lo = (sb(n, [P, 2, G, SLOT], F16) for n in ("hot_row", "hot_hi", "hot_lo"))
        hot_tile = sb("hot_tile", [P, 2, G, TILES], F16)
        hi, lo, mid = (sb(n, [128, TILES])[:, :] for n in ("hi", "lo", "mid"))
        cast_s, rows_ready, tiles_ready, hi_ready, lo_ready, hots_used, zeroed, moved, move_order = c.sem(
            *("mv_" + n for n in ("cast", "rows_ready", "tiles_ready", "hi_ready", "lo_ready", "hots_used", "zeroed", "moved", "order")))
        BATCHES = EC // G
        wide = [P, G, SLOT]
        with nc.Block() as block:
            @block.vector
            def _(dve):
                v = nc.vector
                v.memset(c.banks[0][:, :], 0.0).then_inc(zeroed, 1)
                v.memset(c.banks[1][:, :], 0.0).then_inc(zeroed, 1)
                v.tensor_copy(lo16[:, :], code_lo).then_inc(cast_s, 1)

                def hots(q, b):
                    wait_from(dve, hi_ready, G * q - G)
                    wait_from(dve, lo_ready, q - 1)
                    for g in range(G):
                        last = v.tensor_scalar(hot_row[:, b, g, :], c.iota[0:P, 0:SLOT], col(row_of, q * G + g), None, ALU.is_equal)
                    last.then_inc(rows_ready, 1)
                    wait_from(dve, hots_used, q - 1)
                    for g in range(G):
                        last = v.tensor_scalar(hot_tile[:, b, g, :], c.iota[0:P, :], col(tile_of, q * G + g), None, ALU.is_equal)
                    last.then_inc(tiles_ready, 1)
                over_tiles(dve, hots, count=BATCHES)
                dve.wait_ge(moved, 1)
                order = Order(dve, move_order)
                order.then(v.tensor_copy(hi, c.banks[0][:, 0:TILES]))
                order.then(v.tensor_copy(lo, c.banks[1][:, 0:TILES]))
                order.then(v.tensor_scalar(mid, lo, 1.0 / 128, -63.5 / 128, ALU.mult, ALU.add))
                order.then(v.tensor_scalar(mid, mid, ROUND, ROUND, ALU.add, ALU.subtract))
                order.then(v.scalar_tensor_tensor(out=lo, in0=mid, scalar=-128.0, in1=lo, op0=ALU.mult, op1=ALU.add))
                order.then(v.tensor_scalar(slot_dst[:, :], lo, -1.0, None, ALU.add))
                order.then(v.scalar_tensor_tensor(out=hi, in0=hi, scalar=8.0, in1=mid, op0=ALU.mult, op1=ALU.add))
                order.then(v.tensor_copy(slot_row[:, :], hi))

            @block.scalar
            def _(act):
                def codes(q, b):
                    act.wait_ge(rows_ready, q + 1)
                    wait_from(act, hots_used, q - 1)
                    for g in range(G):
                        nc.scalar.activation(hot_hi[:, b, g, :], hot_row[:, b, g, :], ACT.Copy, scale=col(code_hi, q * G + g)).then_inc(hi_ready, 1)
                over_tiles(act, codes, count=BATCHES)

            @block.gpsimd
            def _(pool):
                def codes(q, b):
                    pool.wait_ge(rows_ready, q + 1)
                    wait_from(pool, hots_used, q - 1)
                    nc.gpsimd.tensor_tensor(hot_lo[:, b, :, :], hot_row[:, b, :, :], lo16[:, bass.ds(q * G, G)].unsqueeze(2).to_broadcast(wide), ALU.mult).then_inc(lo_ready, 1)
                pool.wait_ge(cast_s, 1)
                over_tiles(pool, codes, count=BATCHES)

            @block.tensor
            def _(pe):
                pe.wait_ge(zeroed, 2)

                def add(q, b):
                    pe.wait_ge(tiles_ready, q + 1)
                    pe.wait_ge(lo_ready, q + 1)
                    for g in range(G):
                        pe.wait_ge(hi_ready, G * q + g + 1)
                        nc.tensor.matmul(c.banks[0][:, 0:TILES], hot_hi[:, b, g, :], hot_tile[:, b, g, :], start=False, stop=False, skip_group_check=True)
                        last = nc.tensor.matmul(c.banks[1][:, 0:TILES], hot_lo[:, b, g, :], hot_tile[:, b, g, :], start=False, stop=False, skip_group_check=True)
                    last.then_inc(hots_used, 1)
                over_tiles(pe, add, count=BATCHES)
                pe.wait_ge(hots_used, BATCHES)
                pe.sem_inc(moved, 1)


def keep_turned(c, pool, HT, hT, t_ready, kept):
    def keep(t, b):
        pool.wait_ge(t_ready, t + 1)
        c.nc.gpsimd.tensor_copy(HT[:, :, bass.ds(t * SLOT, P)], hT[:, b, :, :]).then_inc(kept, 1)
    over_tiles(pool, keep)


def first_messages(c, scope, HT, table_y):
    nc, A, layer = c.nc, c.A, 0

    def sb(name, shape, dt=F32):
        return c.sb(scope, "m0_" + name, shape, dt)

    w_rel = sb("w_rel", [128, 2, RELS * D])
    h, hT = sb("h", [P, 2, D]), sb("hT", [128, 2, 2, P])
    y = sb("y", [P, 2, RELS * D])
    ty = table_y.rearrange("(r p t) d -> p r t d", r=RELS, t=WIN)
    landed, h_ready, turned, t_ready, products, y_ready, kept = c.sem(
        *("m0_" + n for n in ("landed", "h_ready", "turned", "t_ready", "products", "y_ready", "kept")))
    y_stored = [c.sem(f"m0_y_stored{i}") for i in range(2)]

    def sync(sp):
        for r in range(RELS):
            sp.dma_start(w_rel[:, :, r * D:(r + 1) * D], A["L0_gnn_W"][layer, r].rearrange("(k p) n -> p k n", k=2)).then_inc(landed, 16)

        def store(t, b):
            sp.wait_ge(y_ready, t + 1)
            sp.dma_start(ty[:, :, t, :], y[:, b, :].rearrange("p (r d) -> p r d", r=RELS)).then_inc(y_stored[b], 16)
        over_tiles(sp, store)
        sp.wait_ge(y_stored[0], 16 * (WIN // 2 + 1))
        sp.wait_ge(y_stored[1], 16 * (WIN // 2))

    def tensor(pe):
        def turn(t, b):
            pe.wait_ge(h_ready, t + 1)
            wait_from(pe, t_ready, t - 1)
            for k in range(2):
                last = nc.tensor.transpose(c.banks[b][:, k * 128:k * 128 + P], h[:, b, k * 128:(k + 1) * 128], c.ident[0:P, 0:P])
            last.then_inc(turned, 1)

        def multiply(t, b):
            pe.wait_ge(t_ready, t + 1)
            wait_from(pe, y_ready, t - 1)
            for k in range(2):
                last = nc.tensor.matmul(c.banks[2 + b][0:P, :], hT[:, b, k, :], w_rel[:, k, :], start=(k == 0), stop=(k == 1))
            last.then_inc(products, 1)
        pe.wait_ge(landed, 16 * RELS)
        over_tiles(pe, (turn, 1), multiply)

    def scalar(act):
        def norm(t, b):
            wait_from(act, turned, t - 1)
            nc.scalar.activation(h[:, b, :], c.X[:, t, :], ACT.Identity, scale=col(c.rstd, t), bias=col(c.nmr, t)).then_inc(h_ready, 1)

        def copy_t(t, b):
            act.wait_ge(turned, t + 1)
            wait_from(act, products, t - 1)
            wait_from(act, kept, t - 1)
            nc.scalar.activation(hT[:, b, :, :], c.banks[b][:, 0:256].rearrange("p (k n) -> p k n", k=2)[:, :, 0:P], ACT.Copy).then_inc(t_ready, 1)

        def copy_y(t, b):
            act.wait_ge(products, t + 1)
            if not isinstance(t, int) or t >= 2:
                act.wait_ge(y_stored[b], t * 8 - 8 * b)
            nc.scalar.activation(y[:, b, :], c.banks[2 + b][0:P, :], ACT.Copy).then_inc(y_ready, 1)
        over_tiles(act, (copy_t, 1), (norm, 3), copy_y)

    def gpsimd(pool):
        keep_turned(c, pool, HT, hT, t_ready, kept)
    return sync, tensor, scalar, gpsimd


def message_stage(c, layer, aggr, selfp, HT, table_y):
    nc, A = c.nc, c.A
    n_ = lambda name: f"me{layer}_{name}"
    with ExitStack() as scope:
        def sb(name, shape, dt=F32):
            return c.sb(scope, n_(name), shape, dt)

        w_rel = sb("w_rel", [128, 2, RELS * D])
        gamma = sb("gamma", [P, D])
        h, normed = sb("h", [P, 2, D]), sb("normed", [P, 2, D])
        LOADS = RELS + 1
        hT, y = sb("hT", [128, 2, 2, P]), sb("y", [P, 2, RELS * D])
        ty = table_y.rearrange("(r p t) d -> p r t d", r=RELS, t=WIN)
        landed, order_s, var_ready, std_ready, n_ready, h_ready, turned, t_ready, products, y_ready, kept, normed_s, scaled_s = c.sem(
            *(n_(n) for n in ("landed", "order", "var", "std", "n_ready", "h_ready", "turned", "t_ready", "products", "y_ready", "kept", "normed", "scaled")))
        y_stored = [c.sem(n_(f"y_stored{i}")) for i in range(2)]
        with nc.Block() as block:
            @block.sync
            def _(sp):
                for r in range(RELS):
                    sp.dma_start(w_rel[:, :, r * D:(r + 1) * D], A["L0_gnn_W"][layer, r].rearrange("(k p) n -> p k n", k=2)).then_inc(landed, 16)
                sp.dma_start(gamma[:, :], row_bcast(A["L0_gnn_ln_gamma"][layer - 1], P)).then_inc(landed, 16)

                def step(t, b):
                    sp.wait_ge(y_ready, t + 1)
                    sp.dma_start(ty[:, :, t, :], y[:, b, :].rearrange("p (r d) -> p r d", r=RELS)).then_inc(y_stored[b], 16)
                over_tiles(sp, step)
                sp.wait_ge(y_stored[0], 16 * (WIN // 2 + 1))
                sp.wait_ge(y_stored[1], 16 * (WIN // 2))

            @block.vector
            def _(dve):
                v = nc.vector
                order = Order(dve, order_s)
                tile_stats(c, dve, order, aggr)
                c.finish_stats(order, var_ready, std_ready)

                def norm(t, b):
                    wait_from(dve, n_ready, t - 1)
                    v.tensor_scalar(normed[:, b, :], aggr[:, t, :], col(c.rstd, t), col(c.nmr, t), ALU.mult, ALU.add).then_inc(normed_s, 1)

                def scale(t, b):
                    dve.wait_ge(normed_s, t + 1)
                    v.tensor_tensor(normed[:, b, :], normed[:, b, :], gamma[:, :], ALU.mult).then_inc(scaled_s, 1)

                def add_self(t, b):
                    dve.wait_ge(scaled_s, t + 1)
                    wait_from(dve, turned, t - 1)
                    v.tensor_tensor(h[:, b, :], normed[:, b, :], selfp[:, t, :], ALU.add).then_inc(n_ready, 1)
                dve.wait_ge(landed, 16 * LOADS)
                over_tiles(dve, (add_self, 3), (scale, 4), (norm, 5))

            @block.scalar
            def _(act):
                c.root(act, var_ready, std_ready)

                def relu(t, b):
                    act.wait_ge(n_ready, t + 1)
                    nc.scalar.activation(h[:, b, :], h[:, b, :], ACT.Relu).then_inc(h_ready, 1)

                def copy_t(t, b):
                    act.wait_ge(turned, t + 1)
                    wait_from(act, products, t - 1)
                    wait_from(act, kept, t - 1)
                    nc.scalar.activation(hT[:, b, :, :], c.banks[b][:, 0:256].rearrange("p (k n) -> p k n", k=2)[:, :, 0:P], ACT.Copy).then_inc(t_ready, 1)

                def copy_y(t, b):
                    act.wait_ge(products, t + 1)
                    if not isinstance(t, int) or t >= 2:
                        act.wait_ge(y_stored[b], t * 8 - 8 * b)
                    nc.scalar.activation(y[:, b, :], c.banks[2 + b][0:P, :], ACT.Copy).then_inc(y_ready, 1)
                over_tiles(act, (copy_t, 1), (relu, 2), copy_y)

            @block.gpsimd
            def _(pool):
                keep_turned(c, pool, HT, hT, t_ready, kept)

            @block.tensor
            def _(pe):
                def turn(t, b):
                    pe.wait_ge(h_ready, t + 1)
                    wait_from(pe, t_ready, t - 1)
                    for k in range(2):
                        last = nc.tensor.transpose(c.banks[b][:, k * 128:k * 128 + P], h[:, b, k * 128:(k + 1) * 128], c.ident[0:P, 0:P])
                    last.then_inc(turned, 1)

                def multiply(t, b):
                    pe.wait_ge(t_ready, t + 1)
                    wait_from(pe, y_ready, t - 1)
                    for k in range(2):
                        last = nc.tensor.matmul(c.banks[2 + b][0:P, :], hT[:, b, k, :], w_rel[:, k, :], start=(k == 0), stop=(k == 1))
                    last.then_inc(products, 1)
                pe.wait_ge(landed, 16 * LOADS)
                over_tiles(pe, (turn, 1), multiply)


def gather_stage(c, layer, aggr, selfp, HT, mixer, table_y, slot_row, slot_dst, slot_win):
    nc, A, first = c.nc, c.A, layer == 0
    n_ = lambda name: f"ga{layer}_{name}"
    with ExitStack() as scope:
        def sb(name, shape, dt=F32):
            return c.sb(scope, n_(name), shape, dt)

        index = sb("index", [128, 2, HALF], I32)
        got, hot = sb("got", [128, RING, D]), sb("hot", [128, RING, P])
        w_self, bias = sb("w_self", [128, 2, D]), sb("bias", [P, 2, D])
        hT = sb("hT", [128, 2, P])
        index_ready, released, summed, hot_ready, added, zeroed, landed, bias_s, h_ready, own_ready, kept = c.sem(
            *(n_(n) for n in ("index_ready", "released", "summed", "hot_ready", "added", "zeroed", "landed", "bias", "h_ready", "own_ready", "kept")))
        gathered = [c.sem(n_(f"gathered{g}")) for g in range(RING)]
        ROUNDS = TILES // RING
        selfp_flat, X_flat = (b[:, :, :].rearrange("p t d -> p (t d)") for b in (selfp, c.X))

        def over_rounds(engine, step):
            assert ROUNDS == WIN + 1
            step(0, False)
            with engine.Fori(RING, TILES - 2 * RING + 1, RING) as s:
                step(s, False)
            step(TILES - RING, True)

        with nc.Block() as block:
            @block.sync
            def _(sp):
                sp.dma_start(w_self[:, :, :], A["L0_gnn_loop_w"][layer].rearrange("(k p) n -> p k n", k=2)).then_inc(landed, 16)
                for i, n in enumerate(("L0_gnn_bias", "L0_gnn_ln_beta")):
                    sp.dma_start(bias[:, i, :], row_bcast(A[n][layer], P)).then_inc(landed, 16)

            @block.gpsimd
            def _(pool):
                def half(s, k):
                    pool.wait_ge(index_ready, s + HALF)
                    pool.sem_inc(released, 1)
                    for g in range(HALF):
                        nc.gpsimd.indirect_dma_start(got[:, k * HALF + g, :], None, table_y,
                                                     bass.IndirectOffsetOnAxis(ap=index[:, k, g:g + 1], axis=0)).then_inc(gathered[k * HALF + g], 16)

                def round_(s, last):
                    half(s, 0)
                    half(s + HALF, 1)
                over_rounds(pool, round_)

            @block.scalar
            def _(act):
                def stage(s, k):
                    wait_from(act, summed, s - HALF)
                    nc.scalar.activation(index[:, k, :], slot_row[:, bass.ds(s, HALF)], ACT.Copy).then_inc(index_ready, HALF)

                def round_(s, last):
                    stage(s, 0)
                    stage(s + HALF, 1)
                    if not last:
                        wait_from(act, own_ready, s)
                        nc.scalar.activation(hT[:, :, :], HT[:, :, bass.ds(s * (SLOT // RING), P)], ACT.Copy).then_inc(h_ready, RING)
                over_rounds(act, round_)

            @block.tensor
            def _(pe):
                def total(s, g):
                    if g % QUAD == 0:
                        pe.wait_ge(hot_ready, s + g + QUAD)
                        wait_from(pe, added, s + g - QUAD)
                    pe.wait_ge(gathered[g], s + 16)
                    nc.tensor.matmul(c.banks[g // 2 % 4][0:P, D * (g % 2):D * (g % 2) + D], hot[:, g, :], got[:, g, :], start=(g % 2 == 0), stop=True,
                                     skip_group_check=True).then_inc(summed, 1)

                def own(s):
                    if isinstance(s, int) and s == 0:
                        pe.wait_ge(landed, 48)
                    pe.wait_ge(h_ready, s + RING)
                    wait_from(pe, kept, s)
                    for k in range(2):
                        last = nc.tensor.matmul(c.banks[4][0:P, 0:D], hT[:, k, :], w_self[:, k, :], start=(k == 0), stop=(k == 1), skip_group_check=True)
                    if first:
                        for k in range(2):
                            last = nc.tensor.matmul(c.banks[4][0:P, D + 128 * k:D + 128 * k + 128], hT[:, k, :], mixer[:, k, :],
                                                    start=False, stop=True, skip_group_check=True)
                    last.then_inc(own_ready, RING)

                def round_(s, last):
                    for g in range(RING):
                        total(s, g)
                        if g == HALF and not last:
                            own(s)
                over_rounds(pe, round_)

            @block.vector
            def _(dve):
                v = nc.vector
                QUADS_RING = RING // QUAD

                def make_hots(s, q):
                    wide = [128, QUAD, P]
                    g = QUAD * q % RING
                    v.tensor_tensor(hot[:, g:g + QUAD, :], c.iota_f[:, 0:P].unsqueeze(1).to_broadcast(wide),
                                    slot_dst[:, bass.ds(s + QUAD * q, QUAD)].unsqueeze(2).to_broadcast(wide), ALU.is_equal).then_inc(hot_ready, QUAD)

                def adds(s, q):
                    dve.wait_ge(summed, s + QUAD * q + QUAD)
                    for g in range(QUAD * q, QUAD * q + QUAD):
                        w = dve.value_load(slot_win[0:1, bass.ds(s + g, 1)], min_val=0, max_val=WIN - 1)
                        wait_from(dve, added, s + g)
                        v.tensor_tensor(aggr[:, bass.ds(w, 1), :].rearrange("p o d -> p (o d)"), aggr[:, bass.ds(w, 1), :].rearrange("p o d -> p (o d)"),
                                        c.banks[g // 2 % 4][0:P, D * (g % 2):D * (g % 2) + D], ALU.add).then_inc(added, 1)

                def keep(s):
                    dve.wait_ge(own_ready, s + RING)
                    tile = bass.ds(s * (D // RING), D)
                    last = v.tensor_tensor(selfp_flat[:, tile], bias[:, 0, :], c.banks[4][0:P, 0:D], ALU.add)
                    if first:
                        last = v.tensor_tensor(X_flat[:, tile], X_flat[:, tile], c.banks[4][0:P, D:2 * D], ALU.add)
                    last.then_inc(kept, RING)

                def round_(s, last):
                    for q in range(QUADS_RING):
                        if not last or q + 2 < QUADS_RING:
                            make_hots(s, q + 2)
                        adds(s, q)
                    if not last:
                        keep(s)
                v.memset(aggr[:, :, :], 0.0).then_inc(zeroed, 1)
                make_hots(0, 0)
                make_hots(0, 1)
                dve.wait_ge(landed, 48)
                v.tensor_tensor(bias[:, 0, :], bias[:, 0, :], bias[:, 1, :], ALU.add).then_inc(bias_s, 1)
                dve.wait_ge(zeroed, 1)
                dve.wait_ge(bias_s, 1)
                over_rounds(dve, round_)


def gnn_out_stage(c, aggr, selfp, following):
    nc, A = c.nc, c.A
    with ExitStack() as scope:
        gamma, normed = c.sb(scope, "go_gamma", [P, D]), c.sb(scope, "go_normed", [P, 2, D])
        scaled = c.sb(scope, "go_scaled", [P, 2, D])
        landed, order_s, var_ready, std_ready, rstd_ready, var2_ready, std2_ready, self_added, normed_s, scaled_s, added = c.sem(
            *("go_" + n for n in ("landed", "order", "var", "std", "rstd", "var2", "std2", "self_added", "normed", "scaled", "added")))
        PART = 5
        with nc.Block() as block:
            @block.sync
            def _(sp):
                sp.dma_start(gamma[:, :], row_bcast(A["L0_gnn_ln_gamma"][LAYERS - 1], P)).then_inc(landed, 16)
                following.sync(sp)

            @block.tensor
            def _(pe):
                following.tensor(pe)

            @block.gpsimd
            def _(pool):
                following.gpsimd(pool)
                for t in range(0, WIN, PART):
                    x = c.X[:, t:t + PART, :]
                    nc.gpsimd.tensor_tensor(x, x, selfp[:, t:t + PART, :], ALU.add).then_inc(self_added, PART)

            @block.vector
            def _(dve):
                v = nc.vector
                order = Order(dve, order_s)
                tile_stats(c, dve, order, aggr)
                c.finish_stats(order, var_ready, std_ready)
                dve.sem_inc(rstd_ready, 1)
                dve.wait_ge(landed, 16)

                def scale(t, b):
                    dve.wait_ge(normed_s, t + 1)
                    wait_from(dve, added, t - 1)
                    v.tensor_tensor(scaled[:, b, :], normed[:, b, :], gamma[:, :], ALU.mult).then_inc(scaled_s, 1)

                def add(t, b):
                    dve.wait_ge(scaled_s, t + 1)
                    dve.wait_ge(self_added, t + 1)
                    v.tensor_tensor(c.X[:, t, :], c.X[:, t, :], scaled[:, b, :], ALU.add).then_inc(added, 1)

                def stats(t, b):
                    dve.wait_ge(added, t + 1)
                    v.bn_stats(c.stats[:, t, :], c.X[:, t, :]).then_inc(order_s, 1)
                over_tiles(dve, (scale, 2), (add, 1), stats)
                order.k += WIN
                dve.wait_ge(order_s, order.k)
                following.vector(dve)
                c.finish_stats(order, var2_ready, std2_ready)

            @block.scalar
            def _(act):
                following.scalar(act)
                c.root(act, var_ready, std_ready)

                def norm(t, b):
                    wait_from(act, scaled_s, t - 1)
                    nc.scalar.activation(normed[:, b, :], aggr[:, t, :], ACT.Identity, scale=col(c.rstd, t), bias=col(c.nmr, t)).then_inc(normed_s, 1)
                act.wait_ge(rstd_ready, 1)
                over_tiles(act, norm)
                c.root(act, var2_ready, std2_ready)


class Programs:

    def __init__(self, sync, vector, tensor=None, scalar=None, gpsimd=None):
        self.sync, self.vector, self.tensor, self.scalar, self.gpsimd = sync, vector, tensor, scalar, gpsimd


class SliceBuffers:
    def __init__(self, c, scope):
        def sb(name, shape):
            return c.sb(scope, "sl_" + name, shape)

        self.logit_w, self.logit_rows, self.b_out = sb("logit_w", [128, 2, INNER]), sb("logit_rows", [P, INNER]), sb("b_out", [P, D])
        self.w_x, self.w_xT = sb("w_x", [128, 2, INNER]), sb("w_xT", [128, 4, D])
        self.pair = sb("pair", [128, 128])
        self.b_x, self.b_slice, self.logit_b = sb("b_x", [128, 4]), sb("b_slice", [1, SD]), sb("logit_b", [1, INNER])
        self.inv_temp = sb("inv_temp", [128, HEADS])


def slice_preparation(c, w):
    nc, A, banks = c.nc, c.A, c.banks
    logit_w, logit_rows, b_out, w_x, w_xT, pair = w.logit_w, w.logit_rows, w.b_out, w.w_x, w.w_xT, w.pair
    b_x, b_slice, logit_b, inv_temp = w.b_x, w.b_slice, w.logit_b, w.inv_temp
    landed, cleared, order_s, turned, copied, made = c.sem(*("slp_" + n for n in ("landed", "cleared", "order", "turned", "copied", "made")))

    def sync(sp):
        sp.dma_start(w_x[:, :, :], A["L0_ffn_W_x"].rearrange("(k p) n -> p k n", k=2)).then_inc(landed, 16)
        with nc.allow_non_contiguous_dma(reason="512 floats, once"):
            sp.dma_start(b_x[:, :], A["L0_ffn_b_x"].rearrange("(k p) -> p k", p=128)).then_inc(landed, 16)
        sp.dma_start(b_slice[:, :], A["L0_ffn_b_slice"].unsqueeze(0)).then_inc(landed, 16)
        sp.dma_start(inv_temp[:, :], row_bcast(A["L0_ffn_temperature"].rearrange("a h b e -> (a h b e)"), 128)).then_inc(landed, 16)
        sp.dma_start(b_out[:, :], row_bcast(A["L0_ffn_b_out"], P)).then_inc(landed, 16)
        sp.wait_ge(cleared, 1)
        for i in range(2):
            sp.dma_start(pair[i * SD:(i + 1) * SD, i * SD:(i + 1) * SD], A["L0_ffn_W_slice"]).then_inc(landed, 16)

    def gpsimd(pool):
        nc.gpsimd.memset(pair[:, :], 0.0).then_inc(cleared, 1)

    def tensor(pe):
        pe.wait_ge(landed, 112)
        for k in range(2):
            for a in range(4):
                nc.tensor.transpose(banks[k][:, a * 128:a * 128 + 128], w_x[:, k, a * 128:a * 128 + 128], c.ident[:, :]).then_inc(turned, 1)
        pe.wait_ge(copied, 2)
        for k in range(2):
            for a in range(4):
                nc.tensor.matmul(banks[2 + k][:, a * 128:a * 128 + 128], w_xT[:, a, k * 128:k * 128 + 128], pair[:, :],
                                 start=(a == 0), stop=True, skip_group_check=True)
        for a in range(4):
            last = nc.tensor.matmul(banks[4][0:1, a * 128:a * 128 + 128], b_x[:, a:a + 1], pair[:, :],
                                    start=(a == 0), stop=True, skip_group_check=True)
        last.then_inc(made, 1)
        pe.wait_ge(order_s, 4)
        nc.tensor.matmul(banks[5][0:P, :], c.ones[0:1, 0:P], logit_b[:, :], start=True, stop=True).then_inc(made, 1)

    def scalar(act):
        for k in range(2):
            act.wait_ge(turned, 4 * k + 4)
            nc.scalar.activation(w_xT[:, :, k * 128:k * 128 + 128], banks[k][:, :].rearrange("p (a n) -> p a n", a=4), ACT.Copy).then_inc(copied, 1)

    def vector(dve):
        v, order = nc.vector, Order(dve, order_s)
        dve.wait_ge(landed, 112)
        order.then(v.tensor_scalar(inv_temp[:, :], inv_temp[:, :], 0.1, 5.0, ALU.max, ALU.min))
        order.then(v.reciprocal(inv_temp[:, :], inv_temp[:, :]))
        dve.wait_ge(made, 1)
        by_head = "p (h g) -> p h g"
        for k in range(2):
            v.tensor_tensor(logit_w[:, k, :].rearrange(by_head, h=HEADS), banks[2 + k][:, :].rearrange(by_head, h=HEADS),
                            inv_temp[:, :].unsqueeze(2).to_broadcast([128, HEADS, SD]), ALU.mult)
        order.then(v.tensor_tensor(logit_b[:, :].rearrange(by_head, h=HEADS), banks[4][0:1, :].rearrange(by_head, h=HEADS),
                                   b_slice[:, :].unsqueeze(1).to_broadcast([1, HEADS, SD]), ALU.add))
        order.then(v.tensor_tensor(logit_b[:, :].rearrange(by_head, h=HEADS), logit_b[:, :].rearrange(by_head, h=HEADS),
                                   inv_temp[0:1, :].unsqueeze(2).to_broadcast([1, HEADS, SD]), ALU.mult))
        assert order.k == 4
        dve.wait_ge(made, 2)
        order.then(v.tensor_copy(logit_rows[:, :], banks[5][0:P, :]))

    return Programs(sync=sync, gpsimd=gpsimd, tensor=tensor, scalar=scalar, vector=vector)


def slice_stage(c, prepared, following):
    nc, A, banks = c.nc, c.A, c.banks
    logit_w, logit_rows, b_out = prepared.logit_w, prepared.logit_rows, prepared.b_out
    with ExitStack() as scope:
        def sb(name, shape, dt=F32):
            return c.sb(scope, "sl_" + name, shape, dt)

        W = sb("weights", [P, WIN, INNER])
        M = sb("M", [128, 4, D])
        with ExitStack() as s1:
            def qb(name, shape, dt=F32):
                return c.sb(s1, "sla_" + name, shape, dt)

            HN = qb("HN", [P, WIN, D])
            h, hT = qb("h", [P, 2, D]), qb("hT", [128, 2, 2, P])
            e, w = qb("e", [P, 2, INNER]), qb("w", [P, 2, INNER])
            w_sum = qb("w_sum", [P, INNER])
            peak, total = qb("peak", [P, 2, HEADS]), qb("total", [P, 2, HEADS])
            w_zeroed, w_summed, order_s, total_s, hn_ready, h_ready, turned, t_ready, logits, e_ready, exped, r_ready, w_ready, w_kept, pooled, zeroed = c.sem(
                *("sla_" + n for n in ("w_zeroed", "w_summed", "order", "total", "hn_ready", "h_ready", "turned", "t_ready", "logits", "e_ready", "exped", "r_ready", "w_ready", "w_kept",
                                       "pooled", "zeroed")))
            by_head = "p (h g) -> p h g"
            with nc.Block() as block:
                @block.sync
                def _(sp):
                    following.sync(sp)

                @block.vector
                def _(dve):
                    v = nc.vector
                    for i in (4, 5, 6):
                        v.memset(banks[i][:, :], 0.0).then_inc(zeroed, 1)

                    def make_h(t, b):
                        c.normalised(HN[:, t, :], t).then_inc(hn_ready, 1)

                    def shift(t, b):
                        order = Order(dve, order_s, t, 2)
                        dve.wait_ge(logits, t + 1)
                        wait_from(dve, w_ready, t - 1)
                        eb = e[:, b, :].rearrange(by_head, h=HEADS)
                        order.then(v.tensor_tensor(e[:, b, :], banks[2 + b][0:P, :], logit_rows[:, :], ALU.add))
                        order.then(v.tensor_reduce(peak[:, b, :], eb, AX.X, ALU.max))
                        v.tensor_tensor(eb, eb, peak[:, b, :].unsqueeze(2).to_broadcast([P, HEADS, SD]), ALU.subtract).then_inc(e_ready, 1)

                    def sum_up(t, b):
                        order = Order(dve, total_s, t, 1)
                        dve.wait_ge(exped, t + 1)
                        order.then(v.tensor_reduce(total[:, b, :], e[:, b, :].rearrange(by_head, h=HEADS), AX.X, ALU.add))
                        v.reciprocal(total[:, b, :], total[:, b, :]).then_inc(r_ready, 1)
                    over_tiles(dve, (shift, 2), (sum_up, 1), (make_h, 5))

                @block.gpsimd
                def _(pool):
                    def weights(t, b):
                        pool.wait_ge(r_ready, t + 1)
                        wait_from(pool, pooled, t - 1)
                        wait_from(pool, w_kept, t - 1)
                        wait_from(pool, w_summed, t - 1)
                        nc.gpsimd.tensor_tensor(w[:, b, :].rearrange(by_head, h=HEADS), e[:, b, :].rearrange(by_head, h=HEADS),
                                                total[:, b, :].unsqueeze(2).to_broadcast([P, HEADS, SD]), ALU.mult).then_inc(w_ready, 1)

                    def sum_w(t, b):
                        pool.wait_ge(w_ready, t + 1)
                        wait_from(pool, w_summed, t)
                        nc.gpsimd.tensor_tensor(w_sum[:, :], w_sum[:, :], w[:, b, :], ALU.add).then_inc(w_summed, 1)
                    nc.gpsimd.memset(w_sum[:, :], 0.0).then_inc(w_zeroed, 1)
                    pool.wait_ge(w_zeroed, 1)
                    over_tiles(pool, (weights, 1), sum_w)

                @block.scalar
                def _(act):
                    def copy_h(t, b):
                        act.wait_ge(hn_ready, t + 1)
                        wait_from(act, turned, t - 1)
                        nc.scalar.activation(h[:, b, :], HN[:, t, :], ACT.Copy).then_inc(h_ready, 1)

                    def copy_t(t, b):
                        act.wait_ge(turned, t + 1)
                        wait_from(act, logits, t - 1)
                        nc.scalar.activation(hT[:, b, :, :], banks[b][:, 0:256].rearrange("p (k n) -> p k n", k=2)[:, :, 0:P], ACT.Copy).then_inc(t_ready, 1)

                    def exp(t, b):
                        act.wait_ge(e_ready, t + 1)
                        nc.scalar.activation(e[:, b, :], e[:, b, :], ACT.Exp).then_inc(exped, 1)

                    def keep(t, b):
                        act.wait_ge(w_ready, t + 1)
                        nc.scalar.activation(W[:, t, :], w[:, b, :], ACT.Copy).then_inc(w_kept, 1)
                    over_tiles(act, (copy_t, 3), (copy_h, 4), (exp, 2), keep)

                @block.tensor
                def _(pe):
                    def turn(t, b):
                        pe.wait_ge(h_ready, t + 1)
                        wait_from(pe, t_ready, t - 1)
                        for k in range(2):
                            last = nc.tensor.transpose(banks[b][:, k * 128:k * 128 + P], h[:, b, k * 128:(k + 1) * 128], c.ident[0:P, 0:P])
                        last.then_inc(turned, 1)

                    def logit(t, b):
                        pe.wait_ge(t_ready, t + 1)
                        wait_from(pe, order_s, 2 * t - 3)
                        for k in range(2):
                            last = nc.tensor.matmul(banks[2 + b][0:P, :], hT[:, b, k, :], logit_w[:, k, :], start=(k == 0), stop=(k == 1))
                        last.then_inc(logits, 1)

                    def pool_x(t, b):
                        pe.wait_ge(w_ready, t + 1)
                        for a in range(4):
                            wa = w[:, b, a * 128:(a + 1) * 128]
                            last = nc.tensor.matmul(banks[4 + a // 2][:, (a % 2) * D:(a % 2 + 1) * D], wa, HN[:, t, :], start=False, stop=False, skip_group_check=True)
                        last.then_inc(pooled, 1)
                    pe.wait_ge(zeroed, 3)
                    over_tiles(pe, (logit, 2), (turn, 3), pool_x)
                    pe.wait_ge(w_summed, WIN)
                    for a in range(4):
                        nc.tensor.matmul(banks[6][:, a:a + 1], w_sum[:, a * 128:(a + 1) * 128], c.ones[0:P, 0:1], start=False, stop=False, skip_group_check=True)

        with ExitStack() as s2:
            def rb(name, shape, dt=F32):
                return c.sb(s2, "slb_" + name, shape, dt)

            w_fx, b_fx = rb("w_fx", [128, 2, INNER]), rb("b_fx", [1, INNER])
            w_qkv = rb("w_qkv", [SD, 3, SD])
            w_out = rb("w_out", [SD, HEADS, D])
            inv, share = rb("inv", [128, 4]), rb("share", [128, 4])
            U, UT, shareT = rb("U", [128, 4, D]), rb("UT", [128, 2, INNER]), rb("shareT", [1, INNER])
            tokT, qkvT = rb("tokT", [SD, INNER]), rb("qkvT", [SD, 3, INNER])
            attn, attnT = rb("attn", [SD, HEADS, SD]), rb("attnT", [SD, INNER])
            peak, total, vw = rb("peak", [SD, HEADS]), rb("total", [SD, HEADS]), rb("vw", [SD, HEADS, D])
            landed, order_s, act_done, pe_done = c.sem(*("slb_" + n for n in ("landed", "dve_steps", "act_steps", "pe_steps")))
            with nc.Block() as block:
                @block.sync
                def _(sp):
                    sp.dma_start(w_fx[:, :, :], A["L0_ffn_W_fx"].rearrange("(k p) n -> p k n", k=2)).then_inc(landed, 16)
                    sp.dma_start(b_fx[:, :], A["L0_ffn_b_fx"].unsqueeze(0)).then_inc(landed, 16)
                    for i, n in enumerate("qkv"):
                        sp.dma_start(w_qkv[:, i, :], A[f"L0_ffn_W_{n}"]).then_inc(landed, 16)
                    sp.dma_start(w_out[:, :, :], A["L0_ffn_W_out"].rearrange("(h c) n -> c h n", c=SD)).then_inc(landed, 16)

                @block.vector
                def _(dve):
                    v, order = nc.vector, Order(dve, order_s)
                    order.then(v.tensor_scalar(inv[:, :], banks[6][:, 0:4], 1e-5, None, ALU.add))
                    order.then(v.reciprocal(inv[:, :], inv[:, :]))
                    order.then(v.tensor_tensor(share[:, :], inv[:, :], banks[6][:, 0:4], ALU.mult))
                    for a in range(4):
                        order.then(v.tensor_scalar(U[:, a, :], banks[4 + a // 2][:, (a % 2) * D:(a % 2 + 1) * D], inv[:, a:a + 1], None, ALU.mult))
                    assert order.k == 7
                    following.vector(dve)
                    dve.wait_ge(pe_done, 4)
                    scores = banks[7][0:SD, :].rearrange("p (h g) -> p h g", h=HEADS)
                    order.then(v.tensor_reduce(peak[:, :], scores, AX.X, ALU.max))
                    order.then(v.tensor_tensor(attn[:, :, :], scores, peak[:, :].unsqueeze(2).to_broadcast([SD, HEADS, SD]), ALU.subtract))
                    dve.wait_ge(act_done, 6)
                    order.then(v.tensor_reduce(total[:, :], attn[:, :, :], AX.X, ALU.add))
                    order.then(v.reciprocal(total[:, :], total[:, :]))
                    order.then(v.tensor_tensor(attn[:, :, :], attn[:, :, :], total[:, :].unsqueeze(2).to_broadcast([SD, HEADS, SD]), ALU.mult))
                    assert order.k == 12
                    dve.wait_ge(pe_done, 5)
                    for i in range(4):
                        order.then(v.tensor_copy(vw[:, 2 * i:2 * i + 2, :].rearrange("p a d -> p (a d)"), banks[i][0:SD, :]))

                @block.scalar
                def _(act):
                    act.wait_ge(pe_done, 1)
                    for k in range(2):
                        nc.scalar.activation(UT[:, k, :], banks[k][:, :], ACT.Copy).then_inc(act_done, 1)
                    nc.scalar.activation(shareT[:, :], banks[2][0:1, :], ACT.Copy).then_inc(act_done, 1)
                    act.wait_ge(pe_done, 2)
                    nc.scalar.activation(tokT[:, :], banks[3][0:SD, :], ACT.Copy).then_inc(act_done, 1)
                    act.wait_ge(pe_done, 3)
                    for i in range(3):
                        last = nc.scalar.activation(qkvT[:, i, :], banks[4 + i][0:SD, :], ACT.Copy)
                    last.then_inc(act_done, 1)
                    act.wait_ge(order_s, 9)
                    nc.scalar.activation(attn[:, :, :], attn[:, :, :], ACT.Exp, scale=float(SD) ** -0.5).then_inc(act_done, 1)
                    act.wait_ge(pe_done, 6)
                    nc.scalar.activation(attnT[:, :], banks[4][0:SD, :], ACT.Copy).then_inc(act_done, 1)
                    act.wait_ge(pe_done, 7)
                    for i in range(2):
                        nc.scalar.activation(M[:, 2 * i:2 * i + 2, :].rearrange("p a d -> p (a d)"), banks[5 + i][:, :], ACT.Copy).then_inc(act_done, 1)

                @block.tensor
                def _(pe):
                    mm = nc.tensor.matmul
                    pe.wait_ge(order_s, 7)
                    for k in range(2):
                        for a in range(4):
                            nc.tensor.transpose(banks[k][:, a * 128:a * 128 + 128], U[:, a, k * 128:k * 128 + 128], c.ident[:, :])
                    for a in range(4):
                        last = nc.tensor.transpose(banks[2][0:1, a * 128:a * 128 + 128], share[:, a:a + 1], c.ident[:, :])
                    last.then_inc(pe_done, 1)
                    pe.wait_ge(act_done, 3)
                    pe.wait_ge(landed, 96)
                    for h in range(HEADS):
                        at, o = slice(h * SD, (h + 1) * SD), banks[3][0:SD, h * SD:(h + 1) * SD]
                        for k in range(2):
                            mm(o, w_fx[:, k, at], UT[:, k, at], start=(h == 0 and k == 0), stop=False, skip_group_check=True)
                        last = mm(o, b_fx[0:1, at], shareT[0:1, at], start=False, stop=True, skip_group_check=True)
                    last.then_inc(pe_done, 1)
                    pe.wait_ge(act_done, 4)
                    for i in range(3):
                        last = mm(banks[4 + i][0:SD, :], w_qkv[:, i, :], tokT[:, :], start=True, stop=True)
                    last.then_inc(pe_done, 1)
                    pe.wait_ge(act_done, 5)
                    for h in range(HEADS):
                        at = slice(h * SD, (h + 1) * SD)
                        last = mm(banks[7][0:SD, at], qkvT[:, 0, at], qkvT[:, 1, at], start=(h == 0), stop=True, skip_group_check=True)
                    last.then_inc(pe_done, 1)
                    for h in range(HEADS):
                        last = mm(banks[h // 2][0:SD, (h % 2) * D:(h % 2 + 1) * D], qkvT[:, 2, h * SD:(h + 1) * SD], w_out[:, h, :],
                                  start=(h % 2 == 0), stop=True, skip_group_check=True)
                    last.then_inc(pe_done, 1)
                    pe.wait_ge(order_s, 12)
                    for h in range(HEADS):
                        last = nc.tensor.transpose(banks[4][0:SD, h * SD:(h + 1) * SD], attn[:, h, :], c.ident[0:SD, 0:SD])
                    last.then_inc(pe_done, 1)
                    pe.wait_ge(act_done, 7)
                    pe.wait_ge(order_s, 16)
                    for h in range(HEADS):
                        a = h // 2
                        last = mm(banks[5 + a // 2][(h % 2) * SD:(h % 2 + 1) * SD, (a % 2) * D:(a % 2 + 1) * D],
                                  attnT[:, h * SD:(h + 1) * SD], vw[:, h, :], start=(a % 2 == 0), stop=True, skip_group_check=True)
                    last.then_inc(pe_done, 1)

        with ExitStack() as s3:
            w, wT = c.sb(s3, "slc_w", [P, 2, INNER]), c.sb(s3, "slc_wT", [128, 2, 4, P])
            order_s, biased, w_ready, turned, t_ready, products, added, var_ready, std_ready = c.sem(
                *("slc_" + n for n in ("order", "biased", "w_ready", "turned", "t_ready", "products", "added", "var", "std")))
            with nc.Block() as block:
                @block.gpsimd
                def _(pool):
                    def stage(t, b):
                        wait_from(pool, turned, t - 1)
                        nc.gpsimd.tensor_copy(w[:, b, :], W[:, t, :]).then_inc(w_ready, 1)
                    over_tiles(pool, stage)

                @block.tensor
                def _(pe):
                    def turn(t, b):
                        pe.wait_ge(w_ready, t + 1)
                        wait_from(pe, t_ready, t - 1)
                        for a in range(4):
                            last = nc.tensor.transpose(banks[b][:, a * 128:a * 128 + P], w[:, b, a * 128:(a + 1) * 128], c.ident[0:P, 0:P])
                        last.then_inc(turned, 1)

                    def multiply(t, b):
                        pe.wait_ge(t_ready, t + 1)
                        wait_from(pe, added, t - 1)
                        o = banks[2 + b][0:P, 0:D]
                        for a in range(4):
                            last = nc.tensor.matmul(o, wT[:, b, a, :], M[:, a, :], start=(a == 0), stop=(a == 3))
                        last.then_inc(products, 1)
                    over_tiles(pe, (turn, 1), multiply)

                @block.scalar
                def _(act):
                    def copy_t(t, b):
                        act.wait_ge(turned, t + 1)
                        wait_from(act, products, t - 1)
                        nc.scalar.activation(wT[:, b, :, :], banks[b][:, :].rearrange("p (a n) -> p a n", a=4)[:, :, 0:P], ACT.Copy).then_inc(t_ready, 1)
                    over_tiles(act, copy_t)
                    c.root(act, var_ready, std_ready)

                @block.vector
                def _(dve):
                    def add_bias(t, b):
                        nc.vector.tensor_tensor(c.X[:, t, :], c.X[:, t, :], b_out[:, :], ALU.add).then_inc(biased, 1)

                    def add(t, b):
                        dve.wait_ge(products, t + 1)
                        dve.wait_ge(biased, t + 1)
                        nc.vector.tensor_tensor(c.X[:, t, :], c.X[:, t, :], banks[2 + b][0:P, 0:D], ALU.add).then_inc(added, 1)

                    def stats(t, b):
                        dve.wait_ge(added, t + 1)
                        nc.vector.bn_stats(c.stats[:, t, :], c.X[:, t, :]).then_inc(order_s, 1)
                    over_tiles(dve, (add, 1), (add_bias, 2), stats)
                    dve.wait_ge(order_s, WIN)
                    order = Order(dve, order_s)
                    order.k = WIN
                    c.finish_stats(order, var_ready, std_ready)


XTW = GD * GH + GH


class AttentionBuffers:
    def __init__(self, c, scope):
        def sb(name, shape, dt=F32):
            return c.sb(scope, "at_" + name, shape, dt)

        self.w_qkv, self.w_x = sb("w_qkv", [128, 2, 3 * D]), sb("w_x", [128, 2, XTW + GH])
        self.w_out, self.b_out, self.ends = sb("w_out", [128, 2, D]), sb("b_out", [1, D]), sb("ends", [P, 2, WIN], I32)
        self.w_n1, self.a_row, self.prod = sb("w_n1", [128, 2]), sb("a_row", [128, 2, D]), sb("prod", [128, 2, D])


def attention_preparation(c, w):
    nc, A = c.nc, c.A
    w_qkv, w_x, w_out, b_out, ends, w_n1, a_row, prod = w.w_qkv, w.w_x, w.w_out, w.b_out, w.ends, w.w_n1, w.a_row, w.prod
    landed, order_s = c.sem("atp_landed", "atp_order")

    def sync(sp):
        sp.dma_start(w_qkv[:, :, :], A["L1_mix_w_qkv"].rearrange("(k p) n -> p k n", k=2)).then_inc(landed, 16)
        sp.dma_start(w_x[:, :, 0:D], A["L1_gnn_weight"].rearrange("(k p) n -> p k n", k=2)).then_inc(landed, 16)
        for i, n in enumerate("rl"):
            sp.dma_start(a_row[:, i, :], row_bcast(A[f"L1_gnn_attn_{n}"].rearrange("h d -> (h d)"), 128)).then_inc(landed, 16)
        with nc.allow_non_contiguous_dma(reason="256 floats, once"):
            sp.dma_start(w_n1[:, :], A["L1_mix_w_norm1"].rearrange("(k p) -> p k", p=128)).then_inc(landed, 16)
        sp.dma_start(w_out[:, :, :], A["L1_mix_w_out"].rearrange("(k p) n -> p k n", k=2)).then_inc(landed, 16)
        sp.dma_start(b_out[:, :], A["L1_mix_b_out"].unsqueeze(0)).then_inc(landed, 16)
        for i, n in enumerate(("src", "dst")):
            sp.dma_start(ends[:, i, :], A[n][0:N].rearrange("(p t) -> p t", t=WIN)).then_inc(landed, 16)

    def vector(dve):
        v, order = nc.vector, Order(dve, order_s)
        dve.wait_ge(landed, 144)
        for k in range(2):
            order.then(v.tensor_scalar(w_qkv[:, k, :], w_qkv[:, k, :], w_n1[:, k:k + 1], None, ALU.mult))
            for i in range(2):
                order.then(v.tensor_tensor(prod[:, i, :], w_x[:, k, 0:D], a_row[:, i, :], ALU.mult))
                order.then(v.tensor_reduce(w_x[:, k, D + GH * i:D + GH * i + GH], prod[:, i, :].rearrange("p (h d) -> p h d", h=GH), AX.X, ALU.add))
    return Programs(sync=sync, vector=vector)


def attention_stage(c, prepared):
    nc, A, banks = c.nc, c.A, c.banks
    KV = 128 + 4
    with ExitStack() as scope:
        def sb(name, shape, dt=F32):
            return c.sb(scope, "at_" + name, shape, dt)

        Q = sb("Q", [P, WIN, D])
        rms = sb("rms", [P, WIN])
        kv = sb("kv", [128, 2, KV])
        w_qkv, w_x, w_out, b_out, ends = prepared.w_qkv, prepared.w_x, prepared.w_out, prepared.b_out, prepared.ends
        XT = sb("XT", [P, WIN, XTW])
        AL = sb("AL", [P, WIN, GH])
        table_x = nc.dram_tensor("table_x", [N, XTW], F32, kind="Internal").ap()
        table_l = nc.dram_tensor("table_l", [N, GH], F32, kind="Internal").ap()
        tx, tl = (t.rearrange("(p t) d -> p t d", t=WIN) for t in (table_x, table_l))

        with ExitStack() as s1:
            def qb(name, shape, dt=F32):
                return c.sb(s1, "ata_" + name, shape, dt)

            h, hT, xt = qb("h", [P, 2, D]), qb("hT", [128, 2, 2, P]), qb("xt", [P, 2, XTW + GH])
            e, m = qb("e", [P, 2, 2 * D]), qb("m", [P, 2, 2 * D])
            k_, v_ = qb("k", [P, 2, D]), qb("v", [P, 2, 2, 129])
            (order_s, ms_ready, rms_std, h_ready, turned, t_ready, qk_done, xt_done, products, xt_ready, v_ready, e_ready, exped,
             kq_ready, summed, sums_order) = c.sem(
                *("ata_" + n for n in ("order", "ms", "rms_std", "h_ready", "turned", "t_ready", "qk_done", "xt_done", "products", "xt_ready",
                                       "v_ready", "e_ready", "exped", "kq_ready", "summed", "sums_order")))
            stored = [c.sem(f"ata_stored{i}") for i in range(2)]
            with nc.Block() as block:
                @block.sync
                def _(sp):
                    def step(t, b):
                        sp.wait_ge(xt_ready, t + 1)
                        sp.dma_start(tx[:, t, :], xt[:, b, 0:XTW]).then_inc(stored[b], 16)
                        sp.dma_start(tl[:, t, :], xt[:, b, XTW:XTW + GH]).then_inc(stored[b], 16)
                    over_tiles(sp, step)
                    sp.wait_ge(stored[0], 32 * (WIN // 2 + 1))
                    sp.wait_ge(stored[1], 32 * (WIN // 2))

                @block.vector
                def _(dve):
                    v, order = nc.vector, Order(dve, order_s)
                    order.then(v.tensor_scalar(rms[:, :], c.fin[:, 3, :], -LN_EPS, None, ALU.add))
                    order.then(v.tensor_tensor(rms[:, :], rms[:, :], c.rstd[:, :], ALU.mult))
                    order.then(v.tensor_tensor(rms[:, :], rms[:, :], c.rstd[:, :], ALU.mult))
                    v.tensor_scalar(rms[:, :], rms[:, :], RMS_EPS, None, ALU.add).then_inc(ms_ready, 1)
                    dve.wait_ge(rms_std, 1)
                    order.then(v.reciprocal(rms[:, :], rms[:, :]))
                    order.then(v.memset(v_[:, :, :, :], 1.0))
                    order.then(v.memset(banks[6][:, :], 0.0))
                    dve.sem_inc(sums_order, 1)

                    def make_h(t, b):
                        wait_from(dve, turned, t - 1)
                        c.normalised(h[:, b, :], t).then_inc(h_ready, 1)

                    def elu(t, b):
                        dve.wait_ge(qk_done, t + 1)
                        wait_from(dve, kq_ready, 2 * t - 2)
                        r = col(rms, t)
                        qk = banks[4 + b][0:P, :]
                        v.tensor_scalar(e[:, b, :], qk, r, 0.0, ALU.mult, ALU.min)
                        v.tensor_scalar(m[:, b, :], qk, r, 0.0, ALU.mult, ALU.max).then_inc(e_ready, 1)
                    over_tiles(dve, (elu, 2), (make_h, 4))

                @block.gpsimd
                def _(pool):
                    def join(t, b):
                        pool.wait_ge(exped, t + 1)
                        nc.gpsimd.tensor_tensor(Q[:, t, :], e[:, b, 0:D], m[:, b, 0:D], ALU.add).then_inc(kq_ready, 1)
                        wait_from(pool, summed, t - 1)
                        nc.gpsimd.tensor_tensor(k_[:, b, :], e[:, b, D:2 * D], m[:, b, D:2 * D], ALU.add).then_inc(kq_ready, 1)
                    over_tiles(pool, join)

                @block.scalar
                def _(act):
                    act.wait_ge(ms_ready, 1)
                    nc.scalar.activation(rms[:, :], rms[:, :], ACT.Sqrt).then_inc(rms_std, 1)

                    def copy_t(t, b):
                        act.wait_ge(turned, t + 1)
                        wait_from(act, products, t - 1)
                        nc.scalar.activation(hT[:, b, :, :], banks[b][:, 0:256].rearrange("p (k n) -> p k n", k=2)[:, :, 0:P], ACT.Copy).then_inc(t_ready, 1)

                    def copy_xt(t, b):
                        act.wait_ge(xt_done, t + 1)
                        if not isinstance(t, int) or t >= 2:
                            act.wait_ge(stored[b], t * 16 - 16 * b)
                        nc.scalar.activation(xt[:, b, :], banks[2 + b][0:P, 0:XTW + GH], ACT.Copy).then_inc(xt_ready, 1)

                    def exp(t, b):
                        act.wait_ge(e_ready, t + 1)
                        nc.scalar.activation(e[:, b, :], e[:, b, :], ACT.Exp).then_inc(exped, 1)

                    def copy_v(t, b):
                        act.wait_ge(products, t + 1)
                        wait_from(act, summed, t - 1)
                        nc.scalar.activation(v_[:, b, :, 0:128], banks[7][0:P, 0:D].rearrange("p (a n) -> p a n", a=2), ACT.Identity, scale=col(rms, t)).then_inc(v_ready, 1)
                    over_tiles(act, (copy_t, 3), (copy_xt, 2), (exp, 2), (copy_v, 2))

                @block.tensor
                def _(pe):
                    mm = nc.tensor.matmul

                    def turn(t, b):
                        pe.wait_ge(h_ready, t + 1)
                        wait_from(pe, t_ready, t - 1)
                        for k in range(2):
                            last = nc.tensor.transpose(banks[b][:, k * 128:k * 128 + P], h[:, b, k * 128:(k + 1) * 128], c.ident[0:P, 0:P])
                        last.then_inc(turned, 1)

                    def multiply(t, b):
                        pe.wait_ge(t_ready, t + 1)
                        wait_from(pe, e_ready, t - 1)
                        for k in range(2):
                            last = mm(banks[4 + b][0:P, :], hT[:, b, k, :], w_qkv[:, k, 0:2 * D], start=(k == 0), stop=(k == 1))
                        last.then_inc(qk_done, 1)
                        wait_from(pe, xt_ready, t - 1)
                        for k in range(2):
                            last = mm(banks[2 + b][0:P, 0:XTW + GH], hT[:, b, k, :], w_x[:, k, :], start=(k == 0), stop=(k == 1))
                        last.then_inc(xt_done, 1)
                        wait_from(pe, v_ready, t)
                        for k in range(2):
                            last = mm(banks[7][0:P, 0:D], hT[:, b, k, :], w_qkv[:, k, 2 * D:3 * D], start=(k == 0), stop=(k == 1))
                        last.then_inc(products, 1)

                    def sums(t, b):
                        pe.wait_ge(kq_ready, 2 * t + 2)
                        pe.wait_ge(v_ready, t + 1)
                        for a in range(2):
                            last = mm(banks[6][:, 129 * a:129 * a + 129], k_[:, b, a * 128:a * 128 + 128], v_[:, b, a, :], start=False, stop=False, skip_group_check=True)
                        last.then_inc(summed, 1)
                    pe.wait_ge(sums_order, 1)
                    over_tiles(pe, (turn, 3), (multiply, 2), sums)

        H = sb("H", [P, WIN, D])
        with ExitStack() as s2:
            def rb(name, shape, dt=F32):
                return c.sb(s2, "atb_" + name, shape, dt)

            q, qT, z = rb("q", [P, 2, D]), rb("qT", [128, 2, 2, P]), rb("z", [P, 2, 2, 4])
            att, aT = rb("att", [P, 2, D]), rb("aT", [128, 2, 2, P])
            (kv_ready, q_ready, turned, t_ready, products, att_ready, turned2, t2_ready, products2, order_s, normed, added, got_x, got_l) = c.sem(
                *("atb_" + n for n in ("kv_ready", "q_ready", "turned", "t_ready", "products", "att_ready", "turned2", "t2_ready", "products2",
                                       "order", "normed", "added", "got_x", "got_l")))
            with nc.Block() as block:
                @block.gpsimd
                def _(pool):
                    for t in range(WIN):
                        nc.gpsimd.indirect_dma_start(AL[:, t, :], None, table_l, bass.IndirectOffsetOnAxis(ap=ends[:, 0, t:t + 1], axis=0)).then_inc(got_l, 16)
                        nc.gpsimd.indirect_dma_start(XT[:, t, :], None, table_x, bass.IndirectOffsetOnAxis(ap=ends[:, 1, t:t + 1], axis=0)).then_inc(got_x, 16)
                    pool.wait_ge(got_l, 16 * WIN)
                    pool.wait_ge(got_x, 16 * WIN)

                @block.tensor
                def _(pe):
                    mm = nc.tensor.matmul

                    def turn(t, b):
                        pe.wait_ge(q_ready, t + 1)
                        wait_from(pe, t_ready, t - 1)
                        for k in range(2):
                            last = nc.tensor.transpose(banks[b][:, k * 128:k * 128 + P], q[:, b, k * 128:(k + 1) * 128], c.ident[0:P, 0:P])
                        last.then_inc(turned, 1)

                    def multiply(t, b):
                        pe.wait_ge(t_ready, t + 1)
                        wait_from(pe, att_ready, 2 * t - 2)
                        for a in range(2):
                            last = mm(banks[2 + b][0:P, KV * a:KV * a + KV], qT[:, b, a, :], kv[:, a, :], start=(a == 0), stop=True, skip_group_check=True)
                        last.then_inc(products, 1)

                    def turn_att(t, b):
                        pe.wait_ge(att_ready, 2 * t + 2)
                        wait_from(pe, t2_ready, t - 1)
                        for k in range(2):
                            last = nc.tensor.transpose(banks[4 + b][:, k * 128:k * 128 + P], att[:, b, k * 128:(k + 1) * 128], c.ident[0:P, 0:P])
                        last.then_inc(turned2, 1)

                    def out(t, b):
                        pe.wait_ge(t2_ready, t + 1)
                        wait_from(pe, added, t - 1)
                        o = banks[6 + b][0:P, 0:D]
                        for k in range(2):
                            mm(o, aT[:, b, k, :], w_out[:, k, :], start=(k == 0), stop=False)
                        mm(o, c.ones[0:1, 0:P], b_out[:, :], start=False, stop=True).then_inc(products2, 1)
                    pe.wait_ge(kv_ready, 1)
                    over_tiles(pe, (turn_att, 2), (multiply, 3), (out, 1), (turn, 4))

                @block.scalar
                def _(act):
                    def stage_q(t, b):
                        wait_from(act, turned, t - 1)
                        nc.scalar.activation(q[:, b, :], Q[:, t, :], ACT.Copy).then_inc(q_ready, 1)

                    def norm(t, b):
                        nc.scalar.activation(H[:, t, :], c.X[:, t, :], ACT.Identity, scale=col(c.rstd, t), bias=col(c.nmr, t)).then_inc(normed, 1)

                    def copy_q(t, b):
                        act.wait_ge(turned, t + 1)
                        wait_from(act, products, t - 1)
                        nc.scalar.activation(qT[:, b, :, :], banks[b][:, 0:256].rearrange("p (k n) -> p k n", k=2)[:, :, 0:P], ACT.Copy).then_inc(t_ready, 1)

                    def copy_a(t, b):
                        act.wait_ge(turned2, t + 1)
                        wait_from(act, products2, t - 1)
                        nc.scalar.activation(aT[:, b, :, :], banks[4 + b][:, 0:256].rearrange("p (k n) -> p k n", k=2)[:, :, 0:P], ACT.Copy).then_inc(t2_ready, 1)
                    over_tiles(act, (copy_a, 2), (norm, 3), (copy_q, 4), (stage_q, 5))

                @block.vector
                def _(dve):
                    v, order = nc.vector, Order(dve, order_s)
                    for a in range(2):
                        order.then(v.tensor_tensor(kv[:, a, 0:128], c.blocks[:, :], banks[6][:, 129 * a:129 * a + 128], ALU.mult))
                        order.then(v.tensor_scalar(kv[:, a, 128:KV], c.heads[:, :], banks[6][:, 129 * a + 128:129 * a + 129], None, ALU.mult))
                    dve.sem_inc(kv_ready, 1)
                    start = order.k

                    def divide(t, b):
                        order = Order(dve, order_s, t, 2)
                        order.start = order.start + start
                        dve.wait_ge(products, t + 1)
                        wait_from(dve, turned2, t - 1)
                        p = banks[2 + b][0:P, 0:2 * KV].rearrange("p (a n) -> p a n", a=2)
                        order.then(v.tensor_scalar(z[:, b, :, :], p[:, :, 128:KV], 1e-6, None, ALU.add))
                        order.then(v.reciprocal(z[:, b, :, :], z[:, b, :, :]))
                        for a in range(2):
                            v.tensor_tensor(att[:, b, a * 128:a * 128 + 128].rearrange("p (h e) -> p h e", e=HC), p[:, a, 0:128].rearrange("p (h e) -> p h e", e=HC),
                                            z[:, b, a, :].unsqueeze(2).to_broadcast([P, 4, HC]), ALU.mult).then_inc(att_ready, 1)

                    def add(t, b):
                        dve.wait_ge(normed, t + 1)
                        dve.wait_ge(products2, t + 1)
                        v.tensor_tensor(H[:, t, :], H[:, t, :], banks[6 + b][0:P, 0:D], ALU.add).then_inc(added, 1)

                    def use(t, b):
                        dve.wait_ge(added, t + 1)
                        v.bn_stats(c.stats[:, t, :], H[:, t, :])
                        v.tensor_tensor(c.X[:, t, :], c.X[:, t, :], H[:, t, :], ALU.add)
                    over_tiles(dve, (divide, 3), (add, 1), use)

        with ExitStack() as s3:
            def ub(name, shape, dt=F32):
                return c.sb(s3, "atc_" + name, shape, dt)

            score, peak, msg, part = ub("score", [P, WIN, GH]), ub("peak", [P, WIN]), ub("msg", [P, WIN, GD]), ub("part", [P, WIN, GD])
            rs, w_n2, g = ub("rs", [P, WIN]), ub("w_n2", [P, D]), ub("g", [P, 2, D])
            scaled = ub("scaled", [P, 2, D])
            landed, order_s, s_ready, exped, ms_ready, rooted, scaled_ready, g_ready, msg_added, stats_made, added, var_ready, std_ready, rs_ready = c.sem(
                *("atc_" + n for n in ("landed", "order", "s_ready", "exped", "ms", "rooted", "scaled_ready", "g_ready", "msg_added", "stats_made", "added", "var", "std", "rs_ready")))
            with nc.Block() as block:
                @block.sync
                def _(sp):
                    sp.dma_start(w_n2[:, :], row_bcast(A["L1_mix_w_norm2"], P)).then_inc(landed, 16)

                @block.vector
                def _(dve):
                    v, order = nc.vector, Order(dve, order_s)
                    m0, s0, m1, s1 = (c.stats[:, :, i] for i in (1, 2, 4, 5))
                    a, b_, s = (c.fin[:, i, :] for i in range(3))
                    order.then(v.tensor_tensor(a, m0, m0, ALU.mult))
                    order.then(v.tensor_tensor(b_, m1, m1, ALU.mult))
                    order.then(v.tensor_tensor(a, a, b_, ALU.add))
                    order.then(v.tensor_tensor(s, s0, s1, ALU.add))
                    order.then(v.tensor_scalar(a, a, 0.5, RMS_EPS, ALU.mult, ALU.add))
                    v.scalar_tensor_tensor(out=rs[:, :], in0=s, scalar=1.0 / D, in1=a, op0=ALU.mult, op1=ALU.add).then_inc(ms_ready, 1)
                    dve.wait_ge(rooted, 1)
                    v.reciprocal(rs[:, :], rs[:, :]).then_inc(rs_ready, 1)
                    order.then(v.tensor_tensor(score[:, :, :], AL[:, :, :], XT[:, :, GD * GH:XTW], ALU.add))
                    order.then(v.scalar_tensor_tensor(out=score[:, :, :], in0=score[:, :, :], scalar=0.01, in1=score[:, :, :], op0=ALU.mult, op1=ALU.max))
                    order.then(v.tensor_reduce(peak[:, :], score[:, :, :], AX.X, ALU.max))
                    v.tensor_tensor(score[:, :, :], score[:, :, :], peak[:, :].unsqueeze(2).to_broadcast([P, WIN, GH]), ALU.subtract).then_inc(s_ready, 1)
                    dve.wait_ge(exped, 1)
                    order.then(v.tensor_reduce(peak[:, :], score[:, :, :], AX.X, ALU.add))
                    order.then(v.reciprocal(peak[:, :], peak[:, :]))
                    order.then(v.tensor_tensor(score[:, :, :], score[:, :, :], peak[:, :].unsqueeze(2).to_broadcast([P, WIN, GH]), ALU.mult))
                    for h in range(GH):
                        out = msg if h == 0 else part
                        order.then(v.tensor_tensor(out[:, :, :], XT[:, :, h * GD:(h + 1) * GD], score[:, :, h:h + 1].to_broadcast([P, WIN, GD]), ALU.mult))
                        if h:
                            order.then(v.tensor_tensor(msg[:, :, :], msg[:, :, :], part[:, :, :], ALU.add))

                    def add_msg(t, b):
                        x = c.X[:, t, :].rearrange("p (h d) -> p h d", h=GH)
                        v.tensor_tensor(x, x, msg[:, t, :].unsqueeze(1).to_broadcast([P, GH, GD]), ALU.add).then_inc(msg_added, 1)

                    def add_g(t, b):
                        dve.wait_ge(msg_added, t + 1)
                        dve.wait_ge(g_ready, t + 1)
                        v.tensor_tensor(c.X[:, t, :], c.X[:, t, :], g[:, b, :], ALU.add).then_inc(added, 1)

                    def stats(t, b):
                        dve.wait_ge(added, t + 1)
                        v.bn_stats(c.stats[:, t, :], c.X[:, t, :]).then_inc(stats_made, 1)
                    over_tiles(dve, (add_msg, 2), (add_g, 1), stats)
                    dve.wait_ge(stats_made, WIN)
                    c.finish_stats(order, var_ready, std_ready)

                @block.gpsimd
                def _(pool):
                    def scale(t, b):
                        pool.wait_ge(scaled_ready, t + 1)
                        wait_from(pool, added, t - 1)
                        nc.gpsimd.tensor_tensor(g[:, b, :], scaled[:, b, :], w_n2[:, :], ALU.mult).then_inc(g_ready, 1)
                    pool.wait_ge(landed, 16)
                    over_tiles(pool, scale)

                @block.scalar
                def _(act):
                    act.wait_ge(ms_ready, 1)
                    nc.scalar.activation(rs[:, :], rs[:, :], ACT.Sqrt).then_inc(rooted, 1)
                    act.wait_ge(s_ready, 1)
                    nc.scalar.activation(score[:, :, :], score[:, :, :], ACT.Exp).then_inc(exped, 1)

                    def scale(t, b):
                        wait_from(act, g_ready, t - 1)
                        nc.scalar.activation(scaled[:, b, :], H[:, t, :], ACT.Copy, scale=col(rs, t)).then_inc(scaled_ready, 1)
                    act.wait_ge(rs_ready, 1)
                    over_tiles(act, scale)
                    c.root(act, var_ready, std_ready)


def router_stage(c, pos, expert_of, share, weights_landed, load_weights, table_xs):
    nc, A, banks = c.nc, c.A, c.banks
    picks_n = PICKS * WIN
    with ExitStack() as scope:
        def sb(name, shape, dt=F32):
            return c.sb(scope, "ro_" + name, shape, dt)

        HN, h, xT = sb("HN", [P, WIN, D]), sb("h", [P, 2, D]), sb("xT", [128, 2, 2, P])
        affine = sb("affine", [128, 2, 2])
        w_r, b_r = sb("w_r", [128, 2, EXPERTS]), sb("b_r", [P, EXPERTS])
        logit, top, index = sb("logit", [P, 2, EXPERTS]), sb("top", [P, 2, 8]), sb("index", [P, 2, 8], U32)
        tops, picks = sb("tops", [P, PICKS, WIN]), sb("picks", [P, PICKS, WIN])
        mask, scan, zero = (sb(n, [P, EXPERTS, picks_n]) for n in ("mask", "scan", "zero"))
        counts, ntile, offset, place = sb("counts", [P, EXPERTS]), sb("ntile", [P, EXPERTS]), sb("offset", [P, EXPERTS]), sb("place", [P, picks_n])
        ends = sb("ends", [P, EXPERTS + 1])
        ended = sb("ended", [1, TOKEN_TILES])
        passed_e = sb("passed_e", [1, TOKEN_TILES, EXPERTS - 1])
        (landed, order_s, h_ready, turned, t_ready, kept, logits, late_s, gap_ready, exped, counted, summed, pos_ready, scattered, passed, made) = c.sem(
            *("ro_" + n for n in ("landed", "order", "h_ready", "turned", "t_ready", "kept", "logits", "late", "gap", "exped",
                                  "counted", "summed", "pos_ready", "scattered", "passed", "made")))
        with nc.Block() as block:
            @block.sync
            def _(sp):
                with nc.allow_non_contiguous_dma(reason="512 floats, once"):
                    for i, n in enumerate(("L1_ffn_gamma", "L1_ffn_beta")):
                        sp.dma_start(affine[:, i, :], A[n].rearrange("(k p) -> p k", p=128)).then_inc(landed, 16)
                sp.dma_start(w_r[:, :, :], A["L1_ffn_Wr"].rearrange("(k p) n -> p k n", k=2)).then_inc(landed, 16)
                sp.dma_start(b_r[:, :], row_bcast(A["L1_ffn_br"], P)).then_inc(landed, 16)
                load_weights(sp, weights_landed)

            @block.vector
            def _(dve):
                v = nc.vector

                def make_h(t, b):
                    wait_from(dve, kept, t - 1)
                    wait_from(dve, turned, t - 1)
                    c.normalised(h[:, b, :], t).then_inc(h_ready, 1)

                def best(t, b):
                    order = Order(dve, order_s, t, 5)
                    dve.wait_ge(logits, t + 1)
                    order.then(v.tensor_tensor(logit[:, b, :], banks[2 + b][0:P, 0:EXPERTS], b_r[:, :], ALU.add))
                    dve.sem_inc(passed, 1)
                    order.then(v.max(top[:, b, :], logit[:, b, :]))
                    dve.sem_inc(passed, 1)
                    order.then(v.max_index(index[:, b, :], top[:, b, :], logit[:, b, :]))
                    order.then(v.tensor_scalar(tops[:, :, bass.ds(t, 1)].rearrange("p k o -> p (k o)"), top[:, b, 0:2], 1.0, None, ALU.mult))
                    order.then(v.tensor_scalar(picks[:, :, bass.ds(t, 1)].rearrange("p k o -> p (k o)"), index[:, b, 0:2], 1.0, None, ALU.mult))
                v.memset(zero[:, :, :], 0.0).then_inc(made, 1)
                dve.wait_ge(landed, 64)
                over_tiles(dve, (make_h, 2), best)
                order = Order(dve, late_s)
                wide = [P, EXPERTS, picks_n]
                of_pick = picks[:, :, :].rearrange("p k t -> p (k t)").unsqueeze(1).to_broadcast(wide)
                order.then(v.tensor_tensor(mask[:, :, :], c.iota_f[0:P, 0:EXPERTS].unsqueeze(2).to_broadcast(wide), of_pick, ALU.is_equal))
                v.tensor_reduce(counts[:, :], mask[:, :, :], AX.X, ALU.add).then_inc(counted, 1)
                v.tensor_tensor(share[:, 0, :], tops[:, 1, :], tops[:, 0, :], ALU.subtract).then_inc(gap_ready, 1)
                dve.wait_ge(made, 1)
                flat = "p e k -> p (e k)"
                order.then(v.tensor_tensor_scan(scan[:, :, :].rearrange(flat), mask[:, :, :].rearrange(flat), zero[:, :, :].rearrange(flat), 0.0, ALU.add, ALU.add))
                dve.wait_ge(summed, 1)
                totals, before = banks[4][0:P, 0:EXPERTS], banks[5][0:P, 0:EXPERTS]
                order.then(v.tensor_scalar(ntile[:, :], totals, 1.0 / SLOT, (SLOT / 2 - 0.5) / SLOT, ALU.mult, ALU.add))
                order.then(v.tensor_scalar(ntile[:, :], ntile[:, :], ROUND, ROUND, ALU.add, ALU.subtract))
                order.then(v.memset(ends[:, 0:1], 0.0))
                order.then(v.tensor_tensor_scan(ends[:, 1:EXPERTS + 1], ntile[:, :], zero[:, 0, 0:EXPERTS], 0.0, ALU.add, ALU.add))
                order.then(v.scalar_tensor_tensor(out=offset[:, :], in0=ends[:, 0:EXPERTS], scalar=float(SLOT), in1=before, op0=ALU.mult, op1=ALU.add))
                order.then(v.tensor_scalar(offset[:, :], offset[:, :], -1.0, None, ALU.add))
                order.then(v.tensor_tensor(offset[:, 1:EXPERTS], offset[:, 1:EXPERTS], scan[:, 0:EXPERTS - 1, picks_n - 1], ALU.subtract))
                order.then(v.tensor_tensor(scan[:, :, :], scan[:, :, :], offset[:, :].unsqueeze(2).to_broadcast(wide), ALU.add))
                order.then(v.tensor_tensor(scan[:, :, :], scan[:, :, :], mask[:, :, :], ALU.mult))
                order.then(v.tensor_reduce(place[:, :], scan[:, :, :].rearrange("p e k -> p k e"), AX.X, ALU.add))
                v.tensor_copy(pos[:, :], place[:, :]).then_inc(pos_ready, 1)
                shape = [1, TOKEN_TILES, EXPERTS - 1]
                order.then(v.tensor_tensor(passed_e[:, :, :], c.iota_f[0:1, 0:TOKEN_TILES].unsqueeze(2).to_broadcast(shape),
                                           ends[0:1, 1:EXPERTS].unsqueeze(1).to_broadcast(shape), ALU.is_ge))
                order.then(v.tensor_reduce(ended[:, :], passed_e[:, :, :], AX.X, ALU.add))
                order.then(v.tensor_copy(expert_of[:, :], ended[:, :]))
                dve.wait_ge(exped, 1)
                order.then(v.tensor_scalar(share[:, 0, :], share[:, 1, :], 1.0, None, ALU.add))
                order.then(v.reciprocal(share[:, 0, :], share[:, 0, :]))
                order.then(v.tensor_tensor(share[:, 1, :], share[:, 1, :], share[:, 0, :], ALU.mult))

            @block.gpsimd
            def _(pool):
                def keep(t, b):
                    pool.wait_ge(h_ready, t + 1)
                    nc.gpsimd.tensor_copy(HN[:, t, :], h[:, b, :]).then_inc(kept, 1)
                over_tiles(pool, keep)
                pool.wait_ge(pos_ready, 1)
                pool.wait_ge(kept, WIN)
                for i in range(picks_n):
                    nc.gpsimd.indirect_dma_start(table_xs, bass.IndirectOffsetOnAxis(ap=pos[:, i:i + 1], axis=0), HN[:, i % WIN, :], None).then_inc(scattered, 16)
                pool.wait_ge(scattered, 16 * picks_n)

            @block.scalar
            def _(act):
                def copy_t(t, b):
                    act.wait_ge(turned, t + 1)
                    wait_from(act, logits, t - 1)
                    for k in range(2):
                        nc.scalar.activation(xT[:, b, k, :], banks[b][:, k * 128:k * 128 + P], ACT.Identity,
                                             bias=affine[:, 1, k:k + 1], scale=affine[:, 0, k:k + 1]).then_inc(t_ready, 1)
                act.wait_ge(landed, 64)
                over_tiles(act, copy_t)
                act.wait_ge(gap_ready, 1)
                nc.scalar.activation(share[:, 1, :], share[:, 0, :], ACT.Exp).then_inc(exped, 1)

            @block.tensor
            def _(pe):
                def turn(t, b):
                    pe.wait_ge(h_ready, t + 1)
                    wait_from(pe, t_ready, 2 * t - 2)
                    for k in range(2):
                        last = nc.tensor.transpose(banks[b][:, k * 128:k * 128 + P], h[:, b, k * 128:(k + 1) * 128], c.ident[0:P, 0:P])
                    last.then_inc(turned, 1)

                def route(t, b):
                    pe.wait_ge(t_ready, 2 * t + 2)
                    wait_from(pe, order_s, 5 * t - 9)
                    for k in range(2):
                        last = nc.tensor.matmul(banks[2 + b][0:P, 0:EXPERTS], xT[:, b, k, :], w_r[:, k, :], start=(k == 0), stop=(k == 1))
                    last.then_inc(logits, 1)
                pe.wait_ge(landed, 64)
                over_tiles(pe, (turn, 1), route)
                pe.wait_ge(counted, 1)
                nc.tensor.matmul(banks[4][0:P, 0:EXPERTS], c.ones[0:P, 0:P], counts[:, :], start=True, stop=True)
                nc.tensor.matmul(banks[5][0:P, 0:EXPERTS], c.tri[0:P, 0:P], counts[:, :], start=True, stop=True).then_inc(summed, 1)


def expert_stage(c, table_xs):
    nc, A, banks = c.nc, c.A, c.banks
    KH = HID // 128
    table_ys = nc.dram_tensor("table_ys", [TOKEN_TILES * SLOT, D], F32, kind="Internal").ap()
    xs_tiles, ys_tiles = (t.rearrange("(j p) d -> p j d", p=SLOT) for t in (table_xs, table_ys))
    with ExitStack() as scope:
        def sb(name, shape, dt=F32):
            return c.sb(scope, "ex_" + name, shape, dt)

        w1, w2 = sb("w1", [128, EXPERTS, 2, HID]), sb("w2", [128, EXPERTS, KH, D])
        b1, b2 = sb("b1", [SLOT, EXPERTS * HID]), sb("b2", [SLOT, EXPERTS * D])
        affine = sb("affine", [128, 2, 2])
        pos, expert_of = sb("pos", [P, PICKS * WIN], I32), sb("expert_of", [1, TOKEN_TILES], I32)
        share = sb("share", [P, PICKS, WIN])
        weights_landed = c.sem("ex_weights")
        WEIGHTS = 2 * EXPERTS + 4

        def load_weights(sp, s):
            for e in range(EXPERTS):
                sp.dma_start(w1[:, e, :, :], A["L1_ffn_W1"][e].rearrange("(k p) n -> p k n", k=2)).then_inc(s, 16)
                sp.dma_start(w2[:, e, :, :], A["L1_ffn_W2"][e].rearrange("(k p) n -> p k n", k=KH)).then_inc(s, 16)
            for b, n in ((b1, "L1_ffn_b1"), (b2, "L1_ffn_b2")):
                sp.dma_start(b[:, :], row_bcast(A[n].rearrange("e h -> (e h)"), SLOT)).then_inc(s, 16)
            with nc.allow_non_contiguous_dma(reason="512 floats, once"):
                for i, n in enumerate(("L1_ffn_gamma", "L1_ffn_beta")):
                    sp.dma_start(affine[:, i, :], A[n].rearrange("(k p) -> p k", p=128)).then_inc(s, 16)
        router_stage(c, pos, expert_of, share, weights_landed, load_weights, table_xs)

        with ExitStack() as s1:
            def tb(name, shape, dt=F32):
                return c.sb(s1, "ex_" + name, shape, dt)

            xs, xT = tb("xs", [SLOT, 2, D]), tb("xT", [128, 2, 2, SLOT])
            hid, hT, y = tb("hid", [SLOT, 2, HID]), tb("hT", [128, 2, KH, SLOT]), tb("y", [SLOT, 2, D])
            turned, t_ready, up_done, biased, gelu_done, h_turned, ht_ready, down_done, y_ready = c.sem(
                *("ex_" + n for n in ("turned", "t_ready", "up_done", "biased", "gelu_done", "h_turned", "ht_ready", "down_done", "y_ready")))
            loaded, stored = ([c.sem(f"ex_{n}{i}") for i in range(2)] for n in ("loaded", "stored"))

            def expert(engine, j):
                return engine.value_load(expert_of[0:1, bass.ds(j, 1)], min_val=0, max_val=EXPERTS - 1)

            with nc.Block() as block:
                @block.sync
                def _(sp):
                    def load(j, b):
                        wait_from(sp, turned, j - 1)
                        sp.dma_start(xs[:, b, :], xs_tiles[:, j, :]).then_inc(loaded[b], 16)

                    def store(j, b):
                        sp.wait_ge(y_ready, j + 1)
                        sp.dma_start(ys_tiles[:, j, :], y[:, b, :]).then_inc(stored[b], 16)
                    over_tiles(sp, (load, 5), store, count=TOKEN_TILES)
                    for s in stored:
                        sp.wait_ge(s, 16 * (TOKEN_TILES // 2))

                @block.tensor
                def _(pe):
                    mm = nc.tensor.matmul

                    def turn_x(j, b):
                        pe.wait_ge(loaded[b], 8 * j - 8 * b + 16)
                        wait_from(pe, t_ready, 2 * j - 2)
                        for k in range(2):
                            last = nc.tensor.transpose(banks[b][:, k * 128:k * 128 + SLOT], xs[:, b, k * 128:(k + 1) * 128], c.ident[:, :])
                        last.then_inc(turned, 1)

                    def up(j, b):
                        e = expert(pe, j)
                        pe.wait_ge(t_ready, 2 * j + 2)
                        wait_from(pe, biased, j - 1)
                        for k in range(2):
                            last = mm(banks[2 + b][:, :], xT[:, b, k, :], w1[:, bass.ds(e, 1), k, :].rearrange("p o n -> p (o n)"), start=(k == 0), stop=(k == 1))
                        last.then_inc(up_done, 1)

                    def turn_h(j, b):
                        pe.wait_ge(gelu_done, j + 1)
                        wait_from(pe, ht_ready, j - 1)
                        for k in range(KH):
                            last = nc.tensor.transpose(banks[4 + b][:, k * SLOT:(k + 1) * SLOT], hid[:, b, k * 128:(k + 1) * 128], c.ident[:, :])
                        last.then_inc(h_turned, 1)

                    def down(j, b):
                        e = expert(pe, j)
                        pe.wait_ge(ht_ready, j + 1)
                        wait_from(pe, y_ready, j - 1)
                        for k in range(KH):
                            last = mm(banks[6 + b][:, 0:D], hT[:, b, k, :], w2[:, bass.ds(e, 1), k, :].rearrange("p o n -> p (o n)"), start=(k == 0), stop=(k == KH - 1))
                        last.then_inc(down_done, 1)
                    pe.wait_ge(weights_landed, 16 * WEIGHTS)
                    over_tiles(pe, (up, 2), (turn_h, 1), (turn_x, 3), down, count=TOKEN_TILES)

                @block.scalar
                def _(act):
                    def copy_x(j, b):
                        act.wait_ge(turned, j + 1)
                        wait_from(act, up_done, j - 1)
                        for k in range(2):
                            nc.scalar.activation(xT[:, b, k, :], banks[b][:, k * 128:k * 128 + SLOT], ACT.Identity,
                                                 bias=affine[:, 1, k:k + 1], scale=affine[:, 0, k:k + 1]).then_inc(t_ready, 1)

                    def gelu(j, b):
                        act.wait_ge(biased, j + 1)
                        nc.scalar.activation(hid[:, b, :], hid[:, b, :], ACT.Gelu).then_inc(gelu_done, 1)

                    def copy_h(j, b):
                        act.wait_ge(h_turned, j + 1)
                        wait_from(act, down_done, j - 1)
                        nc.scalar.activation(hT[:, b, :, :].rearrange("p k n -> p (k n)"), banks[4 + b][:, :], ACT.Copy).then_inc(ht_ready, 1)
                    act.wait_ge(weights_landed, 16 * WEIGHTS)
                    over_tiles(act, (copy_h, 1), (copy_x, 3), (gelu, 2), count=TOKEN_TILES)

                @block.vector
                def _(dve):
                    v = nc.vector

                    def add_b1(j, b):
                        e = expert(dve, j)
                        dve.wait_ge(up_done, j + 1)
                        wait_from(dve, h_turned, j - 1)
                        v.tensor_tensor(hid[:, b, :], b1[:, bass.ds(e * HID, HID)], banks[2 + b][:, :], ALU.add).then_inc(biased, 1)

                    def add_b2(j, b):
                        e = expert(dve, j)
                        dve.wait_ge(down_done, j + 1)
                        if not isinstance(j, int) or j >= 2:
                            dve.wait_ge(stored[b], j * 8 - 8 * b)
                        v.tensor_tensor(y[:, b, :], b2[:, bass.ds(e * D, D)], banks[6 + b][:, 0:D], ALU.add).then_inc(y_ready, 1)
                    dve.wait_ge(weights_landed, 16 * WEIGHTS)
                    over_tiles(dve, (add_b1, 2), add_b2, count=TOKEN_TILES)

        with ExitStack() as s2:
            GOT, PART = 10, 5
            got = c.sb(s2, "ex_got", [P, GOT, D])
            gathered = [c.sem(f"ex_gathered{i}") for i in range(GOT)]
            added, out_stored = c.sem("ex_added", "ex_out_stored")
            tokens = [(t, k) for g in range(0, WIN, PART) for k in range(PICKS) for t in range(g, g + PART)]
            with nc.Block() as block:
                @block.gpsimd
                def _(pool):
                    for i, (t, k) in enumerate(tokens):
                        wait_from(pool, added, i - GOT + 1)
                        nc.gpsimd.indirect_dma_start(got[:, i % GOT, :], None, table_ys,
                                                     bass.IndirectOffsetOnAxis(ap=pos[:, k * WIN + t:k * WIN + t + 1], axis=0)).then_inc(gathered[i % GOT], 16)

                @block.vector
                def _(dve):
                    for i, (t, k) in enumerate(tokens):
                        dve.wait_ge(gathered[i % GOT], 16 * (i // GOT + 1))
                        if k:
                            dve.wait_ge(added, i - PART + 1)
                        x = c.X[:, t, :]
                        nc.vector.scalar_tensor_tensor(out=x, in0=got[:, i % GOT, :], scalar=share[:, k, t:t + 1], in1=x, op0=ALU.mult, op1=ALU.add).then_inc(added, 1)

                @block.sync
                def _(sp):
                    out = c.out.rearrange("(p t) d -> p t d", t=WIN)
                    for g in range(0, WIN, PART):
                        sp.wait_ge(added, PICKS * (g + PART))
                        sp.dma_start(out[:, g:g + PART, :], c.X[:, g:g + PART, :]).then_inc(out_stored, 16)
                    sp.wait_ge(out_stored, 16 * (WIN // PART))


def build(nc, A, out):
    with ExitStack() as keep:
        c = Chip(nc, A, out, keep)
        table_y = nc.dram_tensor("table_y", [RELS * N, D], F32, kind="Internal").ap()
        table_xs = nc.dram_tensor("table_xs", [TOKEN_TILES * SLOT, D], F32, kind="Internal").ap()
        tail = keep.enter_context(ExitStack())
        slice_w, attention_w = SliceBuffers(c, tail), AttentionBuffers(c, tail)
        with ExitStack() as graph:
            slot_row = c.sb(graph, "slot_row", [128, TILES], I32)
            slot_dst = c.sb(graph, "slot_dst", [128, TILES])
            slot_win = c.sb(graph, "slot_win", [1, TILES], I32)
            HT = c.sb(graph, "HT", [128, 2, WIN * SLOT])
            mixer = c.sb(graph, "mixer", [128, 2, D // 2])
            with ExitStack() as start:
                sort = Sort(c, start, slot_win)
                load_stage(c, sort, table_xs)
                mix0_stage(c, mixer)
                ranks_stage(c, sort, HT, table_y)
                move_stage(c, sort, slot_row, slot_dst)
            c.recycle()
            aggr, selfp = c.sb(graph, "aggr", [P, WIN, D]), c.sb(graph, "selfp", [P, WIN, D])
            for layer in range(LAYERS):
                if layer:
                    message_stage(c, layer, aggr, selfp, HT, table_y)
                gather_stage(c, layer, aggr, selfp, HT, mixer, table_y, slot_row, slot_dst, slot_win)
            gnn_out_stage(c, aggr, selfp, slice_preparation(c, slice_w))
        c.recycle()
        slice_stage(c, slice_w, attention_preparation(c, attention_w))
        c.recycle()
        attention_stage(c, attention_w)
        tail.close()
        c.recycle()
        expert_stage(c, table_xs)


def constants():
    import numpy as np
    head = np.arange(128) // HC
    return {
        "c_ident": np.eye(128, dtype=np.float32),
        "c_tri": np.triu(np.ones((128, 128), np.float32), 1),
        "c_iota": np.tile(np.arange(TILES, dtype=np.float16), (128, 1)),
        "c_iota_f": np.tile(np.arange(128, dtype=np.float32), (128, 1)),
        "c_blocks": (head[:, None] == head[None, :]).astype(np.float32),
        "c_heads": (head[:, None] == np.arange(4)[None, :]).astype(np.float32),
    }


def kernel(**inputs):
    import numpy as np
    import concourse.bacc as bacc
    from concourse.bass_utils import run_bass_kernel_spmd

    nc = bacc.Bacc("TRN2", target_bir_lowering=False, num_devices=1)
    arrays, handles = {}, {}
    for name, a in {**inputs, **constants()}.items():
        a = np.ascontiguousarray(a)
        arrays[f"in_{name}"] = a
        handles[name] = nc.dram_tensor(f"in_{name}", a.shape, mybir.dt.from_np(a.dtype), kind="ExternalInput").ap()
    out = nc.dram_tensor("out_0", (N, D), F32, kind="ExternalOutput").ap()
    build(nc, handles, out)
    return run_bass_kernel_spmd(nc, [arrays], core_ids=[0]).results[0]["out_0"]
```
